# Optimizing a Trainium2 kernel written in Bass

```python
import numpy as np
import jax
import jax.numpy as jnp

def _softmax(x, axis=-1):
    return jax.nn.softmax(x, axis=axis)

def _gelu(x):
    return jax.nn.gelu(x, approximate=True)

def _silu(x):
    return jax.nn.silu(x)

def _sigmoid(x):
    return jax.nn.sigmoid(x)

def _layernorm(x, axis=-1, eps=1e-05):
    m = jnp.mean(x, axis=axis, keepdims=True)
    v = jnp.var(x, axis=axis, keepdims=True)
    return (x - m) / jnp.sqrt(v + eps)

def _scatter_add(tgt, idx, src, axis=0):
    return tgt.at[idx].add(src)

def _segment_sum(src, seg, n):
    return jax.ops.segment_sum(src, seg, n)
kernel_name = 'mk_gnn_ffn_d1_gnn_r8_378051'

def setup_inputs(seed: int=0):
    np.random.seed(seed)
    _w = jnp.asarray

    def _rec_inputs():
        import jax
        import jax.numpy as jnp
        _gk = jax.random.key(seed)
        x = -8.776e-05 + 1 * jax.random.normal(jax.random.fold_in(_gk, 1), (6250, 256), jnp.float32)
        _s = jax.random.randint(jax.random.fold_in(_gk, 2), (50000,), 0, 6250, jnp.int32)
        _d = jax.random.randint(jax.random.fold_in(_gk, 3), (50000,), 0, 6250, jnp.int32)
        _loop = jnp.arange(6250, dtype=jnp.int32)
        src = jnp.concatenate([_s, _d, _loop])
        dst = jnp.concatenate([_d, _s, _loop])
        _o = jnp.argsort(dst, stable=True)
        src = src[_o]
        dst = dst[_o]
        edge_type_3 = jax.random.randint(jax.random.fold_in(_gk, 12), (106250,), 0, 3, jnp.int32)
        node_type_4 = jax.random.randint(jax.random.fold_in(_gk, 13), (6250,), 0, 4, jnp.int32)
        return (x, src, dst, edge_type_3, node_type_4)
    x, src, dst, edge_type_3, node_type_4 = _rec_inputs()

    def _L0_gnn_setup():
        import jax, jax.numpy as jnp
        import numpy as np
        import math
        L, H, HD, D = (3, 8, 32, 256)
        TN, TE = (4, 3)

        def _layer_norm(x, g, b, eps=1e-05):
            m = jnp.mean(x, axis=-1, keepdims=True)
            v = jnp.var(x, axis=-1, keepdims=True)
            return (x - m) / jnp.sqrt(v + eps) * g + b

        def _typed_transform(xh, W, types):
            out = jnp.zeros_like(xh)
            for t in range(W.shape[0]):
                y = jnp.einsum('mhd,hde->mhe', xh, W[t])
                out = jnp.where((types == t)[:, None, None], y, out)
            return out
        N, E = (2500, 40000)
        key = jax.random.key(seed)
        ks = jax.random.split(key, 16)
        inp = {}
        inp['x'] = jax.random.normal(ks[0], (N, D), dtype=jnp.float32)
        inp['edge_index'] = jax.random.randint(ks[1], (2, E), 0, N)
        inp['edge_type'] = jax.random.randint(ks[2], (E,), 0, TE)
        inp['node_type'] = jax.random.randint(ks[3], (N,), 0, TN)
        inp['W_Q'] = jax.random.normal(ks[4], (L, TN, H, HD, HD), dtype=jnp.float32) * 0.02
        inp['W_K'] = jax.random.normal(ks[5], (L, TN, H, HD, HD), dtype=jnp.float32) * 0.02
        inp['W_V'] = jax.random.normal(ks[6], (L, TN, H, HD, HD), dtype=jnp.float32) * 0.02
        inp['W_E'] = jax.random.normal(ks[7], (L, TE, H, HD, HD), dtype=jnp.float32) * 0.02
        inp['mu'] = jnp.ones((L, H, TE), dtype=jnp.float32)
        inp['Wo'] = jax.random.normal(ks[8], (L, D, D), dtype=jnp.float32) * 0.02
        inp['bo'] = jnp.zeros((L, D), dtype=jnp.float32)
        inp['ln1_g'] = jnp.ones((L, D), dtype=jnp.float32)
        inp['ln1_b'] = jnp.zeros((L, D), dtype=jnp.float32)
        inp['ln2_g'] = jnp.ones((L, D), dtype=jnp.float32)
        inp['ln2_b'] = jnp.zeros((L, D), dtype=jnp.float32)
        inp['w1'] = jax.random.normal(ks[9], (L, D, 4 * D), dtype=jnp.float32) * 0.02
        inp['b1'] = jnp.zeros((L, 4 * D), dtype=jnp.float32)
        inp['w2'] = jax.random.normal(ks[10], (L, 4 * D, D), dtype=jnp.float32) * 0.02
        inp['b2'] = jnp.zeros((L, D), dtype=jnp.float32)
        inp['out_g'] = jnp.ones((D,), dtype=jnp.float32)
        inp['out_b'] = jnp.zeros((D,), dtype=jnp.float32)
        return inp
    _L0_gnn_all = _L0_gnn_setup()
    _L0_gnn_in = {k: v for k, v in _L0_gnn_all.items() if k in ('W_Q', 'W_K', 'W_V', 'W_E', 'mu', 'Wo', 'bo', 'ln1_g', 'ln1_b', 'ln2_g', 'ln2_b', 'w1', 'b1', 'w2', 'b2', 'out_g', 'out_b')}
    del _L0_gnn_all

    def _L0_ffn_setup():
        import jax, jax.numpy as jnp
        import numpy as np
        B, N, D = (16, 512, 256)
        NUM_EXPERTS, TOP_K, HEADS = (4, 2, 4)
        N_EDGES = 131072
        LN_EPS = 1e-05

        def _layernorm(x, g, b):
            mu = x.mean(-1, keepdims=True)
            var = ((x - mu) ** 2).mean(-1, keepdims=True)
            return (x - mu) * jax.lax.rsqrt(var + LN_EPS) * g + b

        def _forward(x, edge_index, W_gat, att_src, att_dst, b_gat, ln_gamma, ln_beta, W1, b1, W2, b2):
            Bc, Nc, Dc = x.shape
            M = Bc * Nc
            x_flat = x.reshape(M, Dc)
            h = (x_flat @ W_gat).reshape(M, HEADS, NUM_EXPERTS)
            loops = jnp.arange(M, dtype=edge_index.dtype)
            src = jnp.concatenate([edge_index[0], loops])
            dst = jnp.concatenate([edge_index[1], loops])
            a_src = (h * att_src).sum(-1)
            a_dst = (h * att_dst).sum(-1)
            e = jax.nn.leaky_relu(a_src[src] + a_dst[dst], negative_slope=0.2)
            e_max = jax.ops.segment_max(e, dst, num_segments=M)
            ee = jnp.exp(e - e_max[dst])
            denom = jax.ops.segment_sum(ee, dst, num_segments=M)
            alpha = ee / (denom[dst] + 1e-16)
            msg = h[src] * alpha[:, :, None]
            agg = jax.ops.segment_sum(msg, dst, num_segments=M).reshape(M, HEADS * NUM_EXPERTS) + b_gat
            scores = _layernorm(agg, ln_gamma, ln_beta).reshape(M, HEADS, NUM_EXPERTS).mean(1)
            scores = scores.reshape(Bc, Nc, NUM_EXPERTS)
            topk_s, topk_i = jax.lax.top_k(scores, TOP_K)
            w = jax.nn.softmax(topk_s, axis=-1)
            out = jnp.zeros_like(x)
            for ei in range(NUM_EXPERTS):
                g = jnp.where(topk_i == ei, w, 0.0).sum(-1)
                hh = jax.nn.gelu(x @ W1[ei] + b1[ei], approximate=False)
                out = out + g[..., None] * (hh @ W2[ei] + b2[ei])
            return out
        key = jax.random.key(seed)
        ks = jax.random.split(key, 8)
        s = 0.05
        return {'x': jax.random.normal(ks[0], (B, N, D), jnp.float32), 'W_gat': jax.random.normal(ks[1], (D, HEADS * NUM_EXPERTS), jnp.float32) * s, 'att_src': jax.random.normal(ks[2], (HEADS, NUM_EXPERTS), jnp.float32) * s, 'att_dst': jax.random.normal(ks[3], (HEADS, NUM_EXPERTS), jnp.float32) * s, 'b_gat': jnp.zeros((HEADS * NUM_EXPERTS,), jnp.float32), 'ln_gamma': jnp.ones((HEADS * NUM_EXPERTS,), jnp.float32), 'ln_beta': jnp.zeros((HEADS * NUM_EXPERTS,), jnp.float32), 'W1': jax.random.normal(ks[4], (NUM_EXPERTS, D, 2 * D), jnp.float32) * s, 'b1': jnp.zeros((NUM_EXPERTS, 2 * D), jnp.float32), 'W2': jax.random.normal(ks[5], (NUM_EXPERTS, 2 * D, D), jnp.float32) * s, 'b2': jnp.zeros((NUM_EXPERTS, D), jnp.float32), 'edge_index': jax.random.randint(ks[6], (2, N_EDGES), 0, B * N, jnp.int32)}
    _L0_ffn_all = _L0_ffn_setup()
    _L0_ffn_in = {k: v for k, v in _L0_ffn_all.items() if k in ('W_gat', 'att_src', 'att_dst', 'b_gat', 'ln_gamma', 'ln_beta', 'W1', 'b1', 'W2', 'b2', 'edge_index')}
    del _L0_ffn_all
    return {'x': x, 'src': src, 'dst': dst, 'edge_type_3': edge_type_3, 'node_type_4': node_type_4, 'L0_gnn_W_Q': _L0_gnn_in['W_Q'], 'L0_gnn_W_K': _L0_gnn_in['W_K'], 'L0_gnn_W_V': _L0_gnn_in['W_V'], 'L0_gnn_W_E': _L0_gnn_in['W_E'], 'L0_gnn_mu': _L0_gnn_in['mu'], 'L0_gnn_Wo': _L0_gnn_in['Wo'], 'L0_gnn_bo': _L0_gnn_in['bo'], 'L0_gnn_ln1_g': _L0_gnn_in['ln1_g'], 'L0_gnn_ln1_b': _L0_gnn_in['ln1_b'], 'L0_gnn_ln2_g': _L0_gnn_in['ln2_g'], 'L0_gnn_ln2_b': _L0_gnn_in['ln2_b'], 'L0_gnn_w1': _L0_gnn_in['w1'], 'L0_gnn_b1': _L0_gnn_in['b1'], 'L0_gnn_w2': _L0_gnn_in['w2'], 'L0_gnn_b2': _L0_gnn_in['b2'], 'L0_gnn_out_g': _L0_gnn_in['out_g'], 'L0_gnn_out_b': _L0_gnn_in['out_b'], 'L0_ffn_W_gat': _L0_ffn_in['W_gat'], 'L0_ffn_att_src': _L0_ffn_in['att_src'], 'L0_ffn_att_dst': _L0_ffn_in['att_dst'], 'L0_ffn_b_gat': _L0_ffn_in['b_gat'], 'L0_ffn_ln_gamma': _L0_ffn_in['ln_gamma'], 'L0_ffn_ln_beta': _L0_ffn_in['ln_beta'], 'L0_ffn_W1': _L0_ffn_in['W1'], 'L0_ffn_b1': _L0_ffn_in['b1'], 'L0_ffn_W2': _L0_ffn_in['W2'], 'L0_ffn_b2': _L0_ffn_in['b2'], 'L0_ffn_edge_index': _L0_ffn_in['edge_index']}

def reference(x, src, dst, edge_type_3, node_type_4, L0_gnn_W_Q, L0_gnn_W_K, L0_gnn_W_V, L0_gnn_W_E, L0_gnn_mu, L0_gnn_Wo, L0_gnn_bo, L0_gnn_ln1_g, L0_gnn_ln1_b, L0_gnn_ln2_g, L0_gnn_ln2_b, L0_gnn_w1, L0_gnn_b1, L0_gnn_w2, L0_gnn_b2, L0_gnn_out_g, L0_gnn_out_b, L0_ffn_W_gat, L0_ffn_att_src, L0_ffn_att_dst, L0_ffn_b_gat, L0_ffn_ln_gamma, L0_ffn_ln_beta, L0_ffn_W1, L0_ffn_b1, L0_ffn_W2, L0_ffn_b2, L0_ffn_edge_index):
    import jax
    import jax.numpy as jnp

    def _L0_gnn_ref(x, edge_index, edge_type, node_type, W_Q, W_K, W_V, W_E, mu, Wo, bo, ln1_g, ln1_b, ln2_g, ln2_b, w1, b1, w2, b2, out_g, out_b):
        import jax, jax.numpy as jnp
        import numpy as np
        import math
        L, H, HD, D = (3, 8, 32, 256)
        TN, TE = (4, 3)

        def _layer_norm(x, g, b, eps=1e-05):
            m = jnp.mean(x, axis=-1, keepdims=True)
            v = jnp.var(x, axis=-1, keepdims=True)
            return (x - m) / jnp.sqrt(v + eps) * g + b

        def _typed_transform(xh, W, types):
            out = jnp.zeros_like(xh)
            for t in range(W.shape[0]):
                y = jnp.einsum('mhd,hde->mhe', xh, W[t])
                out = jnp.where((types == t)[:, None, None], y, out)
            return out
        N = x.shape[0]
        src, dst = (edge_index[0], edge_index[1])
        scale = math.sqrt(HD)
        for l in range(L):
            xh = x.reshape(N, H, HD)
            Q = _typed_transform(xh, W_Q[l], node_type)
            K = _typed_transform(xh, W_K[l], node_type)
            V = _typed_transform(xh, W_V[l], node_type)
            q_dst = Q[dst]
            kt = _typed_transform(K[src], W_E[l], edge_type)
            scores = jnp.sum(q_dst * kt, axis=-1) / scale
            scores = scores * mu[l].T[edge_type]
            m = jax.ops.segment_max(scores, dst, num_segments=N)
            m = jnp.maximum(m, -1000000000.0)
            e = jnp.exp(scores - m[dst])
            s = jax.ops.segment_sum(e, dst, num_segments=N)
            w = e / (s[dst] + 1e-10)
            agg = jax.ops.segment_sum(V[src] * w[..., None], dst, num_segments=N)
            attn = agg.reshape(N, D) @ Wo[l] + bo[l]
            x = _layer_norm(x + attn, ln1_g[l], ln1_b[l])
            h = jax.nn.gelu(x @ w1[l] + b1[l], approximate=False) @ w2[l] + b2[l]
            x = _layer_norm(x + h, ln2_g[l], ln2_b[l])
        return _layer_norm(x, out_g, out_b)

    def _L0_ffn_ref(x, W_gat, att_src, att_dst, b_gat, ln_gamma, ln_beta, W1, b1, W2, b2, edge_index):
        import jax, jax.numpy as jnp
        import numpy as np
        B, N, D = (16, 512, 256)
        NUM_EXPERTS, TOP_K, HEADS = (4, 2, 4)
        N_EDGES = 131072
        LN_EPS = 1e-05

        def _layernorm(x, g, b):
            mu = x.mean(-1, keepdims=True)
            var = ((x - mu) ** 2).mean(-1, keepdims=True)
            return (x - mu) * jax.lax.rsqrt(var + LN_EPS) * g + b

        def _forward(x, edge_index, W_gat, att_src, att_dst, b_gat, ln_gamma, ln_beta, W1, b1, W2, b2):
            Bc, Nc, Dc = x.shape
            M = Bc * Nc
            x_flat = x.reshape(M, Dc)
            h = (x_flat @ W_gat).reshape(M, HEADS, NUM_EXPERTS)
            loops = jnp.arange(M, dtype=edge_index.dtype)
            src = jnp.concatenate([edge_index[0], loops])
            dst = jnp.concatenate([edge_index[1], loops])
            a_src = (h * att_src).sum(-1)
            a_dst = (h * att_dst).sum(-1)
            e = jax.nn.leaky_relu(a_src[src] + a_dst[dst], negative_slope=0.2)
            e_max = jax.ops.segment_max(e, dst, num_segments=M)
            ee = jnp.exp(e - e_max[dst])
            denom = jax.ops.segment_sum(ee, dst, num_segments=M)
            alpha = ee / (denom[dst] + 1e-16)
            msg = h[src] * alpha[:, :, None]
            agg = jax.ops.segment_sum(msg, dst, num_segments=M).reshape(M, HEADS * NUM_EXPERTS) + b_gat
            scores = _layernorm(agg, ln_gamma, ln_beta).reshape(M, HEADS, NUM_EXPERTS).mean(1)
            scores = scores.reshape(Bc, Nc, NUM_EXPERTS)
            topk_s, topk_i = jax.lax.top_k(scores, TOP_K)
            w = jax.nn.softmax(topk_s, axis=-1)
            out = jnp.zeros_like(x)
            for ei in range(NUM_EXPERTS):
                g = jnp.where(topk_i == ei, w, 0.0).sum(-1)
                hh = jax.nn.gelu(x @ W1[ei] + b1[ei], approximate=False)
                out = out + g[..., None] * (hh @ W2[ei] + b2[ei])
            return out
        return _forward(x, edge_index, W_gat, att_src, att_dst, b_gat, ln_gamma, ln_beta, W1, b1, W2, b2)
    edge_index = jnp.stack([src, dst])
    x = x + _L0_gnn_ref(_layernorm(x, axis=-1), edge_index, edge_type_3, node_type_4, L0_gnn_W_Q, L0_gnn_W_K, L0_gnn_W_V, L0_gnn_W_E, L0_gnn_mu, L0_gnn_Wo, L0_gnn_bo, L0_gnn_ln1_g, L0_gnn_ln1_b, L0_gnn_ln2_g, L0_gnn_ln2_b, L0_gnn_w1, L0_gnn_b1, L0_gnn_w2, L0_gnn_b2, L0_gnn_out_g, L0_gnn_out_b)
    x = x + _L0_ffn_ref(_layernorm(x, axis=-1)[None], L0_ffn_W_gat, L0_ffn_att_src, L0_ffn_att_dst, L0_ffn_b_gat, L0_ffn_ln_gamma, L0_ffn_ln_beta, L0_ffn_W1, L0_ffn_b1, L0_ffn_W2, L0_ffn_b2, L0_ffn_edge_index)[0]
    return x

_drawn_inputs = setup_inputs


def setup_inputs(seed=0):
    import zlib

    import numpy as np

    out = dict(_drawn_inputs(seed))
    spreads = {'L0_gnn_mu': (1.0, 0.6),
     'L0_gnn_bo': (0.0, 0.1),
     'L0_gnn_ln1_g': (1.0, 0.2),
     'L0_gnn_ln1_b': (0.0, 0.1),
     'L0_gnn_ln2_g': (1.0, 0.2),
     'L0_gnn_ln2_b': (0.0, 0.1),
     'L0_gnn_b1': (0.0, 0.1),
     'L0_gnn_b2': (0.0, 0.1),
     'L0_gnn_out_g': (1.0, 0.2),
     'L0_gnn_out_b': (0.0, 0.1),
     'L0_ffn_b_gat': (0.0, 0.1),
     'L0_ffn_ln_gamma': (1.0, 0.2),
     'L0_ffn_ln_beta': (0.0, 0.1),
     'L0_ffn_b1': (0.0, 0.302),
     'L0_ffn_b2': (0.0, 0.1)}
    factors = {'L0_gnn_W_Q': 8.0,
     'L0_gnn_W_K': 8.0,
     'L0_gnn_W_V': 3.154,
     'L0_gnn_W_E': 8.0,
     'L0_gnn_Wo': 3.721}
    for name, (base, spread) in spreads.items():
        noise = np.random.default_rng([zlib.crc32(name.encode()), seed]).standard_normal(out[name].shape)
        drawn = base * np.exp(spread * noise) if base else spread * noise
        out[name] = jnp.asarray(drawn.astype(out[name].dtype))
    for name, factor in factors.items():
        out[name] = (out[name] * factor).astype(out[name].dtype)
    return out
```

```python
from contextlib import ExitStack

import concourse.bass as bass
from concourse import mybir

F32 = mybir.dt.float32
I32 = mybir.dt.int32
U32 = mybir.dt.uint32
BF16 = mybir.dt.bfloat16
ALU = mybir.AluOpType
ACT = mybir.ActivationFunctionType
AX = mybir.AxisListType
ds = bass.ds

P = 128
D = 256
HEADS, HD = 8, 32
LAYERS, NODE_TYPES, EDGE_TYPES = 3, 4, 3
N = 6250
NODE_TILES = 50
NPAD = NODE_TILES * P
BUCKETS = 49
LAST = N - (BUCKETS - 1) * P
G = 8
GH, EXPERTS, GW = 4, 4, 16
MF = 512
DFF = 1024
NEG = -1.0e30
CREDIT = 2


class Space:
    pass


def edge_shape(edges, per_partition):
    tiles = (edges + (P - 1) * BUCKETS) // P
    tiles = -(-tiles // (2 * G)) * 2 * G
    e = Space()
    e.edges, e.per, e.tiles = edges, per_partition, tiles
    e.steps, e.chunks = tiles // (2 * G), -(-tiles // P)
    return e


GNN = edge_shape(106250, 832)
GAT = edge_shape(131072, 1024)


class Phase:

    def __init__(self, nc, name):
        self.nc, self.name, self.ctx, self.sems, self.credited, self.per_step = nc, name, ExitStack(), [], [], {}

    def __enter__(self):
        self.ctx.__enter__()
        return self

    def __exit__(self, *a):
        return self.ctx.__exit__(*a)

    def sb(self, name, shape, dt=F32):
        return self.ctx.enter_context(self.nc.sbuf_tensor(f"{self.name}_{name}", shape, dt))

    def pair(self, name, shape, dt=F32):
        return [self.sb(f"{name}{g}", shape, dt) for g in range(2)]

    def ps(self, name, shape, dt=F32):
        return self.ctx.enter_context(self.nc.psum_tensor(f"{self.name}_{name}", shape, dt))

    def dma_sem(self, name):
        s = self.ctx.enter_context(self.nc.semaphore(f"{self.name}_{name}"))
        self.sems.append(s)
        return s

    def dma_pair(self, name):
        return [self.dma_sem(f"{name}{g}") for g in range(2)]

    def sem(self, name, per_step=1):
        s = self.dma_sem(name)
        self.credited.append((s, 2 * per_step))
        self.per_step[s.name] = per_step
        return s

    def store_pair(self, name):
        pair = self.dma_pair(name)
        self.credited += [(s, 16) for s in pair]
        return pair

    def at(self, sem, step, event=None, back=0):
        per = self.per_step[sem.name]
        return step * per + ((2 - back) * per + (per if event is None else event + 1))

    def start(self):
        with self.nc.Block() as block:
            @block.gpsimd
            def _(pool):
                pool.dma_reset()
                for s in self.sems:
                    pool.sem_clear(s)
                for s, start in self.credited:
                    pool.sem_inc(s, start)


def constants(nc, k):
    k.ident = k.sb("ident", [P, P])
    k.iota_row = k.sb("iota_row", [P, P])
    k.iota_p = k.sb("iota_p", [P, 1])
    k.ones = k.sb("ones", [P, P])
    k.tri = k.sb("tri", [P, P])
    k.power = k.sb("power", [P, 1])
    with Phase(nc, "const") as f:
        made = f.dma_sem("made")
        copied = f.dma_sem("copied")
        zero = f.sb("zero", [(NPAD - N) // 2, 2 * D])
        f.start()
        with nc.Block() as block:
            @block.gpsimd
            def _(pool):
                nc.gpsimd.memset(k.ident[:], 0.0)
                nc.gpsimd.memset(k.ones[:], 1.0)
                nc.gpsimd.memset(k.power[:], -0.5)
                nc.gpsimd.memset(k.tri[:], 1.0)
                nc.gpsimd.memset(zero[:], 0.0)
                nc.gpsimd.iota(k.iota_row[:], pattern=[[1, P]], base=0, channel_multiplier=0,
                               allow_small_or_imprecise_dtypes=True)
                nc.gpsimd.iota(k.iota_p[:], pattern=[[1, 1]], base=0, channel_multiplier=1,
                               allow_small_or_imprecise_dtypes=True)
                pool.drain()
                nc.gpsimd.affine_select(out=k.ident[:], in_=k.ident[:], compare_op=ALU.not_equal, fill=1.0,
                                        base=0, pattern=[[-1, P]], channel_multiplier=1)
                nc.gpsimd.affine_select(out=k.tri[:], in_=k.tri[:], compare_op=ALU.is_gt, fill=0.0,
                                        base=0, pattern=[[1, P]], channel_multiplier=-1)
                pool.drain()
                nc.gpsimd.memset(zero[:, 0:1], 0.0).then_inc(made, 1)

            @block.sync
            def _(sp):
                sp.wait_ge(made, 1)
                sp.dma_start(k.XP[0:N, :], k.x).then_inc(copied, 16)
                sp.dma_start(k.XP[N:NPAD, :].rearrange("(p r) c -> p (r c)", r=2), zero[:]).then_inc(copied, 16)
                sp.wait_ge(copied, 32)


def sort_edges(nc, k, name, e, src_in, dst_in, type_in, T):
    nc_, L, steps = nc, e.per, e.per // (2 * G)
    with Phase(nc, name) as f:
        pos = f.sb("pos", [P, L])
        pos_i = f.sb("pos_i", [P, L], I32)
        load = f.sb("load", [P, L, 4])
        hi = f.sb("hi", [P, L])
        ranked = f.dma_sem("ranked")
        counted = f.dma_sem("counted")
        filled = f.dma_sem("filled")
        numbered = f.dma_sem("numbered")
        mapped = f.dma_sem("mapped")
        loaded = f.dma_sem("loaded")
        with ExitStack() as tmp:
            def sb(n_, s, d=F32):
                return tmp.enter_context(nc.sbuf_tensor(f"{name}_{n_}", s, d))
            src_i, dst_i = sb("src_i", [P, L], I32), sb("dst_i", [P, L], I32)
            type_i = sb("type_i", [P, L], I32)
            work_i = sb("work_i", [P, L], I32)
            mask, cum = sb("mask", [P, L]), sb("cum", [P, L])
            fill = sb("fill", [P, e.tiles, 4])
            cnt, off, tiles, tend = (sb(x, [P, BUCKETS]) for x in ("cnt", "off", "tiles", "tend"))
            tiles_i = sb("tiles_i", [P, BUCKETS], I32)
            tile_no, owner = sb("tile_no", [P, e.chunks]), sb("owner", [P, e.chunks])
            owner_i = sb("owner_i", [P, e.chunks], I32)
            scrap = sb("scrap", [P, BUCKETS])
            sums = tmp.enter_context(nc.psum_tensor(f"{name}_sums", [P, 512], F32))
            f.start()
            full = e.edges // L
            rest = e.edges - full * L
            with nc.Block() as block:
                @block.gpsimd
                def _(pool):
                    nc.gpsimd.iota(tile_no[:], pattern=[[P, e.chunks]], base=0, channel_multiplier=1,
                                   allow_small_or_imprecise_dtypes=True).then_inc(numbered, 1)

                @block.sync
                def _(sp):
                    sp.wait_ge(filled, 1)
                    todo = [(dst_i, dst_in), (src_i, src_in)] + ([(type_i, type_in)] if type_in is not None else [])
                    for to, of in todo:
                        sp.dma_start(to[0:full, :], of[0:full * L].rearrange("(p l) -> p l", l=L)).then_inc(loaded, 16)
                        if rest:
                            sp.dma_start(to[full:full + 1, 0:rest],
                                         of[full * L:e.edges].rearrange("(p l) -> p l", p=1)).then_inc(loaded, 16)
                    sp.wait_ge(filled, 2)
                    sp.dma_start(T.edges.rearrange("(p r) c -> p (r c)", p=P), fill[:].rearrange("p r c -> p (r c)")).then_inc(mapped, 16)
                    sp.wait_ge(ranked, 1)
                    with nc.allow_non_contiguous_dma(reason="a few words"):
                        sp.dma_start(T.owner.rearrange("a (c p) -> (a p) c", p=P), owner_i[:]).then_inc(mapped, 16)
                    sp.wait_ge(mapped, 32)

                @block.tensor
                def _(pe):
                    pe.wait_ge(counted, 1)
                    nc.tensor.matmul(sums[:, 0:BUCKETS], k.tri[:], cnt[:], start=True, stop=True)
                    nc.tensor.matmul(sums[:, 64:64 + BUCKETS], k.ones[:], cnt[:], start=True, stop=True).then_inc(counted, 1)

                @block.vector
                def _(dve):
                    V = nc.vector
                    V.memset(dst_i[:], 1 << 20)
                    V.memset(src_i[:], 0)
                    V.memset(type_i[:], 0)
                    V.memset(pos[:], float(1 << 22))
                    V.memset(fill[:, :, 0], float(EDGE_TYPES * N))
                    V.memset(fill[:, :, 1], float(N))
                    V.memset(fill[:, :, 2:4], 999.0)
                    V.memset(load[:, :, 3], 0.0)
                    dve.drain()
                    V.memset(owner[:], 0.0).then_inc(filled, 1)
                    dve.drain()
                    V.memset(tiles[:], 0.0).then_inc(filled, 1)
                    n_in = (2 if type_in is None else 3) * (2 if rest else 1)
                    dve.wait_ge(loaded, 16 * n_in)
                    V.tensor_single_scalar(work_i[:], dst_i[:], 7, op=ALU.logical_shift_right)
                    dve.drain()
                    V.tensor_copy(hi[:], work_i[:])
                    dve.drain()
                    V.tensor_single_scalar(work_i[:], dst_i[:], P - 1, op=ALU.bitwise_and)
                    dve.drain()
                    V.tensor_copy(load[:, :, 2], work_i[:])
                    V.tensor_copy(mask[:], src_i[:])
                    dve.drain()
                    V.tensor_single_scalar(load[:, :, 1], mask[:], float(N - 1), op=ALU.min)
                    V.tensor_copy(cum[:], type_i[:])
                    dve.drain()
                    V.scalar_tensor_tensor(out=load[:, :, 0], in0=load[:, :, 1], scalar=float(EDGE_TYPES),
                                           in1=cum[:], op0=ALU.mult, op1=ALU.add)
                    dve.drain()
                    with dve.Fori(0, BUCKETS, 1) as b:
                        V.tensor_scalar(mask[:], hi[:], k.iota_row[:, ds(b, 1)], None, ALU.is_equal)
                        dve.drain()
                        V.tensor_tensor_scan(cum[:], k.ones[:, 0:1].to_broadcast([P, L]), mask[:], 0.0,
                                             ALU.mult, ALU.add)
                        dve.drain()
                        V.copy_predicated(pos[:], mask[:].bitcast(U32), cum[:])
                        V.tensor_copy(cnt[:, ds(b, 1)], cum[:, L - 1:L])
                        dve.drain()
                    V.memset(scrap[:, 0:1], 0.0).then_inc(counted, 1)
                    dve.wait_ge(counted, 2)
                    V.tensor_copy(tiles_i[:], sums[:, 64:64 + BUCKETS])
                    dve.drain()
                    V.tensor_single_scalar(tiles[:], sums[:, 64:64 + BUCKETS], float(P - 1), op=ALU.add)
                    dve.drain()
                    V.tensor_copy(tiles_i[:], tiles[:])
                    dve.drain()
                    V.tensor_single_scalar(tiles_i[:], tiles_i[:], 7, op=ALU.logical_shift_right)
                    dve.drain()
                    V.tensor_copy(tiles[:], tiles_i[:])
                    dve.drain()
                    V.tensor_tensor_scan(tend[:], k.ones[:, 0:1].to_broadcast([P, BUCKETS]), tiles[:], 0.0,
                                         ALU.mult, ALU.add)
                    dve.drain()
                    V.tensor_tensor(off[:], tend[:], tiles[:], ALU.subtract)
                    dve.drain()
                    V.scalar_tensor_tensor(out=off[:], in0=off[:], scalar=float(P), in1=sums[:, 0:BUCKETS],
                                           op0=ALU.mult, op1=ALU.add)
                    dve.drain()
                    V.tensor_single_scalar(off[:], off[:], -1.0, op=ALU.add)
                    dve.wait_ge(numbered, 1)
                    for c in range(e.chunks):
                        V.tensor_scalar(scrap[:], tend[:], tile_no[:, c:c + 1], None, ALU.is_le, ALU.add,
                                        accum_out=owner[:, c:c + 1])
                        dve.drain()
                    V.tensor_single_scalar(owner[:], owner[:], float(BUCKETS - 1), op=ALU.min)
                    dve.drain()
                    V.tensor_copy(owner_i[:], owner[:]).then_inc(ranked, 1)
                    dve.drain()
                    with dve.Fori(0, BUCKETS, 1) as b:
                        V.tensor_scalar(mask[:], hi[:], k.iota_row[:, ds(b, 1)], off[:, ds(b, 1)],
                                        ALU.is_equal, ALU.mult)
                        dve.drain()
                        V.tensor_tensor(pos[:], pos[:], mask[:], ALU.add)
                        dve.drain()
                    V.tensor_copy(pos_i[:], pos[:]).then_inc(ranked, 1)

        stage_pos, stage_rec = f.pair("stage_pos", [P, G], I32), f.pair("stage_rec", [P, G, 4])
        staged = [f.sem(f"staged{g}") for g in range(2)]
        issued = f.sem("issued")
        written = [f.dma_sem(f"written{g}") for g in range(2)]
        f.start()
        with nc.Block() as block:
            @block.vector
            def _(dve):
                V = nc.vector
                for g in range(2):
                    V.tensor_copy(stage_pos[g][:], pos_i[:, g * G:(g + 1) * G])
                    V.tensor_copy(stage_rec[g][:], load[:, g * G:(g + 1) * G, :]).then_inc(staged[g], 1)
                with dve.Fori(1, steps, 1) as i:
                    for g in range(2):
                        dve.wait_ge(written[g], i * (16 * G))
                        V.tensor_copy(stage_pos[g][:], pos_i[:, ds(i * 2 * G + g * G, G)])
                        dve.drain()
                        V.tensor_copy(stage_rec[g][:], load[:, ds(i * 2 * G + g * G, G), :]).then_inc(staged[g], 1)

            @block.gpsimd
            def _(pool):
                with pool.Fori(0, steps, 1) as i:
                    for g in range(2):
                        pool.wait_ge(staged[g], i + 1 + CREDIT)
                        pool.sem_inc(issued, 1)
                        for t in range(G):
                            pool.indirect_dma_start(
                                out=T.edges, out_offset=bass.IndirectOffsetOnAxis(ap=stage_pos[g][:, t:t + 1], axis=0),
                                in_=stage_rec[g][:, t, :], in_offset=None,
                                bounds_check=e.tiles * P - 1, oob_is_err=False).then_inc(written[g], 16)
                for g in range(2):
                    pool.wait_ge(written[g], 16 * G * steps)


def spread_edges(nc, k, name, e, T, gnn):
    with Phase(nc, name) as f:
        rec = f.pair("rec", [P, P, 4])
        rows = f.pair("rows", [P, P], BF16)
        last, reset = f.pair("last", [P, P]), f.pair("reset", [P, P])
        turned = [f.ps(f"turned{g}", [P, 4, P]) for g in range(2)]
        loaded, stored = f.dma_pair("loaded"), f.dma_pair("stored")
        flagged, transposed, taken = f.sem("flagged"), f.sem("transposed"), f.sem("taken")
        f.start()
        chunks = [(c, min(P, e.tiles - c * P)) for c in range(e.chunks)]
        with nc.Block() as block:
            @block.sync
            def _(sp):
                for c, n in chunks:
                    g = c % 2
                    if c >= 2:
                        sp.wait_ge(transposed, CREDIT + c - 1)
                        sp.wait_ge(flagged, CREDIT + c - 1)
                    sp.dma_start(rec[g][0:n, :, :].rearrange("p e c -> p (e c)"),
                                 T.edges[c * P * P:(c * P + n) * P, :].rearrange("(p e) c -> p (e c)", e=P)
                                 ).then_inc(loaded[g], 16)

            @block.vector
            def _(dve):
                V = nc.vector
                V.memset(T.idx_v[:, e.tiles:], 0)
                if gnn:
                    V.memset(T.idx_k[:, e.tiles:], 0)
                for c, n in chunks:
                    g = c % 2
                    dve.wait_ge(loaded[g], 16 * (c // 2 + 1))
                    if c >= 2:
                        dve.wait_ge(stored[g], (16 * (HEADS + 1) if gnn else 16) * (c // 2))
                        dve.wait_ge(transposed, CREDIT + c - 1)
                    rel = rec[g][0:n, :, 2]
                    if gnn:
                        V.memset(last[g][:, P - 1:P], 1.0)
                        V.memset(reset[g][:, 0:1], NEG)
                        V.tensor_tensor(last[g][0:n, 0:P - 1], rel[:, 0:P - 1], rel[:, 1:P], ALU.not_equal)
                        V.tensor_tensor(reset[g][0:n, 1:P], rel[:, 0:P - 1], rel[:, 1:P], ALU.not_equal)
                        dve.drain()
                        V.tensor_single_scalar(reset[g][0:n, 1:P], reset[g][0:n, 1:P], NEG, op=ALU.mult)
                        dve.drain()
                    V.tensor_copy(rows[g][0:n, :], rel).then_inc(flagged, 1)
                    dve.wait_ge(transposed, CREDIT + c + 1)
                    cols = slice(c * P, c * P + n)
                    V.tensor_copy(T.rel[:, cols], turned[g][:, 2, 0:n])
                    if gnn:
                        V.tensor_copy(T.idx_k[:, cols], turned[g][:, 0, 0:n])
                        V.tensor_copy(T.last[:, cols], turned[g][:, 3, 0:n])
                    V.tensor_copy(T.idx_v[:, cols], turned[g][:, 1, 0:n]).then_inc(taken, 1)

            @block.tensor
            def _(pe):
                for c, n in chunks:
                    g = c % 2
                    pe.wait_ge(flagged, CREDIT + c + 1)
                    if c >= 2:
                        pe.wait_ge(taken, CREDIT + c - 1)
                    for w in range(3):
                        last_op = nc.tensor.transpose(turned[g][:, w, 0:n], rec[g][0:n, :, w], k.ident[0:n, 0:n])
                    if gnn:
                        last_op = nc.tensor.transpose(turned[g][:, 3, 0:n], last[g][0:n, :], k.ident[0:n, 0:n])
                    last_op.then_inc(transposed, 1)

            @block.scalar
            def _(act):
                for c, n in chunks:
                    g = c % 2
                    act.wait_ge(flagged, CREDIT + c + 1)
                    act.dma_start(T.rows[c * P:c * P + n, :], rows[g][0:n, :]).then_inc(stored[g], 16)
                    if gnn:
                        for h in range(HEADS):
                            act.dma_start(T.resets[c * P:c * P + n, h, :], reset[g][0:n, :]).then_inc(stored[g], 16)
                for g in range(2):
                    act.wait_ge(stored[g], (16 * (HEADS + 1) if gnn else 16) * ((e.chunks + 1 - g) // 2))
class Norm:

    def __init__(self, nc, k, f, name):
        self.nc, self.k = nc, k
        self.stats, self.mv, self.rstd = f.pair(name + "_stats", [P, 6]), f.pair(name + "_mv", [P, 2]), f.pair(name + "_rstd", [P, 1])
        self.measured, self.rooted = f.sem(name + "_measured"), f.sem(name + "_rooted")

    def moments(self, dve, g, x, eps=1e-5):
        nc = self.nc
        nc.vector.bn_stats(self.stats[g][:], x)
        dve.drain()
        nc.vector.bn_aggr(self.mv[g][:], self.stats[g][:])
        dve.drain()
        nc.vector.tensor_single_scalar(self.mv[g][:, 1:2], self.mv[g][:, 1:2], eps, op=ALU.add).then_inc(self.measured, 1)

    def root(self, pool, g, s):
        pool.wait_ge(self.measured, s + 1 + CREDIT)
        self.nc.gpsimd.tensor_tensor(self.rstd[g][:], self.mv[g][:, 1:2], self.k.power[:], ALU.pow).then_inc(self.rooted, 1)

    def apply(self, dve, g, s, out, x):
        dve.wait_ge(self.rooted, s + 1 + CREDIT)
        self.nc.vector.tensor_scalar(out, x, self.mv[g][:, 0:1], self.rstd[g][:], ALU.subtract, ALU.mult)


def rows_of(table, s, n=P):
    return table[ds(s * P, n), :]


def first_norm(nc, k):
    with Phase(nc, "first") as f:
        x, y = f.pair("x", [P, D]), f.pair("y", [P, D])
        norm = Norm(nc, k, f, "norm")
        loaded, stored, done = f.dma_pair("loaded"), f.store_pair("stored"), f.sem("done")
        f.start()
        with nc.Block() as block:
            @block.sync
            def _(sp):
                with sp.Fori(0, NODE_TILES // 2, 1) as i:
                    for g in range(2):
                        sp.wait_ge(done, i * 2 + g + 1)
                        sp.dma_start(x[g][:], rows_of(k.XP, i * 2 + g)).then_inc(loaded[g], 16)

            @block.gpsimd
            def _(pool):
                with pool.Fori(0, NODE_TILES // 2, 1) as i:
                    for g in range(2):
                        norm.root(pool, g, i * 2 + g)

            @block.vector
            def _(dve):
                with dve.Fori(0, NODE_TILES // 2, 1) as i:
                    for g in range(2):
                        dve.wait_ge(loaded[g], i * 16 + 16)
                        norm.moments(dve, g, x[g][:])
                    for g in range(2):
                        dve.wait_ge(stored[g], i * 16 + 16)
                        norm.apply(dve, g, i * 2 + g, y[g][:], x[g][:])
                        dve.drain().then_inc(done, 1)

            @block.scalar
            def _(act):
                with act.Fori(0, NODE_TILES // 2, 1) as i:
                    for g in range(2):
                        act.wait_ge(done, i * 2 + g + 1 + CREDIT)
                        act.dma_start(rows_of(k.X, i * 2 + g), y[g][:]).then_inc(stored[g], 16)
                for g in range(2):
                    act.wait_ge(stored[g], 16 * (NODE_TILES // 2) + 16)


def project(nc, k, l):
    KT3 = EDGE_TYPES * D
    with Phase(nc, "project") as f:
        wb = f.sb("wb", [P, 2, NODE_TYPES, 3 * P])
        we = f.sb("we", [P, 2, EDGE_TYPES, P])
        mu = f.sb("mu", [P, HEADS, EDGE_TYPES])
        xt = f.pair("xt", [P, D])
        xm = f.pair("xm", [P, NODE_TYPES, D])
        xmT = f.pair("xmT", [P, NODE_TYPES * 2, P])
        kk, vv, kT, kp = f.pair("kk", [P, D]), f.pair("vv", [P, D]), f.pair("kT", [P, 2, P]), f.pair("kp", [P, EDGE_TYPES, D])
        xT_ps = f.ps("xT_ps", [P, NODE_TYPES * 2, P])
        qkv_ps = f.ps("qkv_ps", [P, 2, 512])
        kT_ps = f.ps("kT_ps", [P, 512])
        kp_ps = f.ps("kp_ps", [P, 2, 512])
        zeroed, weights, scaled = f.dma_sem("zeroed"), f.dma_sem("weights"), f.dma_sem("scaled")
        loaded, v_stored, k_stored = f.dma_pair("loaded"), f.store_pair("v_stored"), f.store_pair("k_stored")
        masked, turned, copied, product = f.sem("masked"), f.sem("turned"), f.sem("copied"), f.sem("product")
        taken, k_turned, k_copied, k_product, k_scaled = (f.sem(x) for x in ("taken", "k_turned", "k_copied", "k_product", "k_scaled"))
        f.start()
        with nc.Block() as block:
            @block.sync
            def _(sp):
                sp.wait_ge(zeroed, 1)
                for half in range(2):
                    for h in range(4):
                        hh, part = half * 4 + h, slice(h * HD, (h + 1) * HD)
                        for q, w in enumerate((k.W_Q, k.W_K, k.W_V)):
                            sp.dma_start(wb[part, half, :, q * P + h * HD:q * P + (h + 1) * HD],
                                         w[ds(l, 1), :, hh, :, :].rearrange("a t d e -> d (a t) e")).then_inc(weights, 16)
                        sp.dma_start(we[part, half, :, h * HD:(h + 1) * HD],
                                     k.W_E[ds(l, 1), :, hh, :, :].rearrange("a t d e -> d (a t) e")).then_inc(weights, 16)
                sp.dma_start(mu[:].rearrange("p h t -> p (h t)"),
                             k.mu[ds(l, 1), :, :].rearrange("a h t -> a (h t)").to_broadcast([P, HEADS * EDGE_TYPES])).then_inc(weights, 16)
                with sp.Fori(0, NODE_TILES // 2, 1) as i:
                    for g in range(2):
                        sp.wait_ge(masked, i * 2 + g + 1)
                        sp.dma_start(xt[g][:], rows_of(k.X, i * 2 + g)).then_inc(loaded[g], 16)
                    for g in range(2):
                        sp.wait_ge(taken, i * 2 + g + 1 + CREDIT)
                        sp.dma_start(rows_of(k.VT, i * 2 + g), vv[g][:]).then_inc(v_stored[g], 16)
                        sp.wait_ge(k_scaled, i * 2 + g + 1 + CREDIT)
                        sp.dma_start(k.KT[ds((i * 2 + g) * P * EDGE_TYPES, P * EDGE_TYPES), :].rearrange("(p t) c -> p (t c)", t=EDGE_TYPES),
                                     kp[g][:].rearrange("p t c -> p (t c)")).then_inc(k_stored[g], 16)
                for g in range(2):
                    sp.wait_ge(v_stored[g], 16 * (NODE_TILES // 2) + 16)
                    sp.wait_ge(k_stored[g], 16 * (NODE_TILES // 2) + 16)

            @block.vector
            def _(dve):
                V = nc.vector
                V.memset(wb[:], 0.0)
                V.memset(we[:], 0.0)
                dve.drain().then_inc(zeroed, 1)
                dve.wait_ge(weights, 16 * 33)
                V.tensor_single_scalar(mu[:], mu[:], float(HD) ** -0.5, op=ALU.mult)
                dve.drain()
                with dve.Fori(0, NODE_TILES // 2, 1) as i:
                    for g in range(2):
                        s = i * 2 + g
                        dve.wait_ge(loaded[g], i * 16 + 16)
                        dve.wait_ge(turned, s + 1)
                        for t in range(NODE_TYPES):
                            op = V.tensor_scalar(xm[g][:, t, :], xt[g][:], k.type_mask[:, ds(s * NODE_TYPES + t, 1)], None, ALU.mult)
                        dve.drain().then_inc(masked, 1)
                    for g in range(2):
                        s = i * 2 + g
                        dve.wait_ge(k_turned, s + 1 + CREDIT)
                        dve.wait_ge(k_product, s + 1)
                        V.tensor_copy(kT[g][:].rearrange("p a c -> p (a c)"), kT_ps[:, 0:2 * P]).then_inc(k_copied, 1)
                        dve.wait_ge(k_product, s + 1 + CREDIT)
                        dve.wait_ge(k_stored[g], i * 16 + 16)
                        for half in range(2):
                            V.tensor_tensor(kp[g][:, :, half * P:(half + 1) * P].rearrange("p t (h e) -> p t h e", e=HD),
                                            kp_ps[:, half, 0:EDGE_TYPES * P].rearrange("p (t h e) -> p t h e", t=EDGE_TYPES, e=HD),
                                            mu[:, half * 4:(half + 1) * 4, :].rearrange("p h t -> p t h").unsqueeze(3)
                                            .to_broadcast([P, EDGE_TYPES, 4, HD]), ALU.mult)
                        dve.drain().then_inc(k_scaled, 1)

            @block.tensor
            def _(pe):
                T = nc.tensor
                with pe.Fori(0, NODE_TILES // 2, 1) as i:
                    for g in range(2):
                        s = i * 2 + g
                        pe.wait_ge(masked, s + 1 + CREDIT)
                        pe.wait_ge(copied, s + CREDIT)
                        for t in range(NODE_TYPES):
                            for half in range(2):
                                op = T.transpose(xT_ps[:, t * 2 + half, :], xm[g][:, t, half * P:(half + 1) * P], k.ident[:])
                        op.then_inc(turned, 1)
                        pe.wait_ge(copied, s + 1 + CREDIT)
                        pe.wait_ge(taken, s + CREDIT)
                        for half in range(2):
                            for t in range(NODE_TYPES):
                                op = T.matmul(qkv_ps[:, half, 0:3 * P], xmT[g][:, t * 2 + half, :], wb[:, half, t, :],
                                              start=(t == 0), stop=(t == NODE_TYPES - 1))
                        op.then_inc(product, 1)
                        pe.wait_ge(taken, s + 1 + CREDIT)
                        pe.wait_ge(k_copied, s + CREDIT)
                        for half in range(2):
                            op = T.transpose(kT_ps[:, half * P:(half + 1) * P], kk[g][:, half * P:(half + 1) * P], k.ident[:])
                        op.then_inc(k_turned, 1)
                        pe.wait_ge(k_copied, s + 1 + CREDIT)
                        pe.wait_ge(k_scaled, s + CREDIT)
                        for half in range(2):
                            op = T.matmul(kp_ps[:, half, 0:EDGE_TYPES * P], kT[g][:, half, :],
                                          we[:, half, :, :].rearrange("p t c -> p (t c)"), start=True, stop=True)
                        op.then_inc(k_product, 1)

            @block.scalar
            def _(act):
                A = nc.scalar
                with act.Fori(0, NODE_TILES // 2, 1) as i:
                    for g in range(2):
                        s = i * 2 + g
                        act.wait_ge(turned, s + 1 + CREDIT)
                        act.wait_ge(product, s + 1)
                        A.copy(xmT[g][:, 0:4, :], xT_ps[:, 0:4, :])
                        A.copy(xmT[g][:, 4:8, :], xT_ps[:, 4:8, :])
                        act.drain().then_inc(copied, 1)
                        act.wait_ge(product, s + 1 + CREDIT)
                        act.wait_ge(k_turned, s + 1)
                        act.wait_ge(v_stored[g], i * 16 + 16)
                        A.copy(k.q_all[:, ds(s * D, D)].rearrange("p (a c) -> p a c", a=2), qkv_ps[:, :, 0:P])
                        A.copy(kk[g][:].rearrange("p (a c) -> p a c", a=2), qkv_ps[:, :, P:2 * P])
                        A.copy(vv[g][:].rearrange("p (a c) -> p a c", a=2), qkv_ps[:, :, 2 * P:3 * P])
                        act.drain().then_inc(taken, 1)


def load_owners(eng, owner, s, regs):
    eng.load(regs, owner[0:1, ds(s * G, G)])
    return [eng.snap(r, min_val=0, max_val=BUCKETS - 1) for r in regs]


def one_hots(nc, k, dve, T, s, g, dst_rows, to_node, to_edge):
    nc.vector.tensor_scalar(to_edge[g][:], dst_rows[g][:], k.iota_p[:], None, ALU.is_equal)
    nc.vector.tensor_tensor(to_node[g][:], T.rel[:, ds(s * G, G)].unsqueeze(2).to_broadcast([P, G, P]),
                            k.iota_row[:].unsqueeze(1).to_broadcast([P, G, P]), ALU.is_equal)


def edge_scores(nc, k, T):
    e = GNN
    with Phase(nc, "scores") as f:
        stage = f.pair("stage", [P, G], I32)
        dst_rows = f.pair("dst_rows", [P, G * P], BF16)
        resets = f.pair("resets", [G * HEADS, P])
        to_node, to_edge = f.pair("to_node", [P, G, P]), f.pair("to_edge", [P, G * P])
        kb = f.pair("kb", [P, G, D])
        sg, run = f.pair("sg", [P, G, HEADS]), f.pair("run", [G * HEADS, P])
        tops = f.pair("tops", [P, G, HEADS + 1])
        mv, absent = f.pair("mv", [P, G, HEADS]), f.pair("absent", [P, G])
        q_ps = f.ps("q_ps", [P, 4, 2, D])
        sT_ps = f.ps("sT_ps", [P, 512])
        run_ps = f.ps("run_ps", [P, 512])
        top_ps = f.ps("top_ps", [P, 512])
        staged, issued, turns = f.sem("staged"), f.sem("issued"), f.sem("turns")
        gathered, rows_in, resets_in = f.dma_pair("gathered"), f.dma_pair("rows_in"), f.dma_pair("resets_in")
        hot, scored = f.sem("hot"), f.sem("scored")
        queried, multiplied = f.sem("queried", 4), f.sem("multiplied", 4)
        s_turned, ran, r_turned, topped, at_nodes, kept, merged = (
            f.sem(x) for x in ("s_turned", "ran", "r_turned", "topped", "at_nodes", "kept", "merged"))
        f.start()
        with nc.Block() as block:
            @block.sync
            def _(sp):
                with sp.Fori(0, e.steps, 1) as i:
                    for g in range(2):
                        s = i * 2 + g
                        sp.wait_ge(hot, s + 1)
                        sp.dma_start(dst_rows[g][:], T.rows[ds(s * G, G), :].rearrange("(a t) e -> a (t e)", a=1)
                                     .to_broadcast([P, G * P])).then_inc(rows_in[g], 16)
                        sp.wait_ge(ran, s + 1)
                        sp.dma_start(resets[g][:], T.resets[ds(s * G, G), :, :].rearrange("t h e -> (t h) e")).then_inc(resets_in[g], 16)

            @block.gpsimd
            def _(pool):
                with pool.Fori(0, e.steps, 1) as i:
                    for g in range(2):
                        s = i * 2 + g
                        pool.wait_ge(staged, s + 1 + CREDIT)
                        pool.sem_inc(issued, 1)
                        pool.wait_ge(scored, s + 1)
                        pool.sem_inc(issued, 1)
                        for t in range(G):
                            pool.indirect_dma_start(out=kb[g][:, t, :], out_offset=None, in_=k.KT,
                                                    in_offset=bass.IndirectOffsetOnAxis(ap=stage[g][:, t:t + 1], axis=0)
                                                    ).then_inc(gathered[g], 16)

            @block.vector
            def _(dve):
                V = nc.vector
                V.memset(k.m_all[:], -1e9)
                V.tensor_copy(stage[0][:], T.idx_k[:, 0:G]).then_inc(staged, 1)
                V.tensor_copy(stage[1][:], T.idx_k[:, G:2 * G]).then_inc(staged, 1)
                dve.drain()
                regs = [dve.alloc_register(f"score_owner{t}") for t in range(G)]
                with dve.Fori(0, e.steps, 1) as i:
                    for g in range(2):
                        s = i * 2 + g
                        owners = load_owners(dve, T.owner, s, regs)
                        dve.wait_ge(rows_in[g], i * 16 + 16)
                        dve.wait_ge(at_nodes, s + 1)
                        one_hots(nc, k, dve, T, s, g, dst_rows, to_node, to_edge)
                        dve.drain().then_inc(hot, 1)
                        dve.wait_ge(gathered[g], (i + 1) * (16 * G))
                        V.tensor_copy(stage[g][:], T.idx_k[:, ds(s * G + 2 * G, G)]).then_inc(staged, 1)
                        for j in range(4):
                            dve.wait_ge(queried, f.at(queried, s, j))
                            V.tensor_tensor(kb[g][:, 2 * j:2 * j + 2, :], q_ps[:, j, :, :], kb[g][:, 2 * j:2 * j + 2, :],
                                            ALU.mult).then_inc(multiplied, 1)
                        dve.drain()
                        dve.wait_ge(kept, s + 1)
                        V.tensor_reduce(sg[g][:].rearrange("p t h -> p (t h)"), kb[g][:].rearrange("p t (h e) -> p (t h) e", e=HD),
                                        AX.X, ALU.add).then_inc(scored, 1)
                        dve.wait_ge(s_turned, s + 1 + CREDIT)
                        dve.wait_ge(resets_in[g], i * 16 + 16)
                        V.tensor_tensor_scan(run[g][:], resets[g][:], sT_ps[0:G * HEADS, 0:P], NEG, ALU.add, ALU.max).then_inc(ran, 1)
                        dve.wait_ge(r_turned, s + 1 + CREDIT)
                        V.tensor_tensor(tops[g][:, :, 0:HEADS], run_ps[:, 0:G * HEADS].rearrange("p (t h) -> p t h", h=HEADS),
                                        T.last[:, ds(s * G, G)].unsqueeze(2).to_broadcast([P, G, HEADS]), ALU.mult)
                        V.tensor_copy(tops[g][:, :, HEADS], T.last[:, ds(s * G, G)])
                        dve.drain().then_inc(topped, 1)
                        dve.wait_ge(at_nodes, s + 1 + CREDIT)
                        at = top_ps[:, 0:G * (HEADS + 1)].rearrange("p (t h) -> p t h", h=HEADS + 1)
                        V.tensor_scalar(absent[g][:], at[:, :, HEADS], -1.0, -NEG, ALU.add, ALU.mult)
                        dve.drain()
                        V.tensor_tensor(mv[g][:], at[:, :, 0:HEADS], absent[g][:].unsqueeze(2).to_broadcast([P, G, HEADS]), ALU.add)
                        dve.drain()
                        for t in range(G):
                            m = k.m_all[:, ds(owners[t] * HEADS, HEADS)]
                            V.tensor_tensor(m, m, mv[g][:, t, :], ALU.max)
                            dve.drain().then_inc(merged, 1)

            @block.scalar
            def _(act):
                with act.Fori(0, e.steps, 1) as i:
                    for g in range(2):
                        s = i * 2 + g
                        act.wait_ge(scored, s + 1 + CREDIT)
                        nc.scalar.copy(k.s_all[:, ds(s * G * HEADS, G * HEADS)], sg[g][:].rearrange("p t h -> p (t h)")).then_inc(kept, 1)

            @block.tensor
            def _(pe):
                T_ = nc.tensor
                regs = [pe.alloc_register(f"score_owner{t}") for t in range(G)]
                with pe.Fori(0, e.steps, 1) as i:
                    for g in range(2):
                        s = i * 2 + g
                        owners = load_owners(pe, T.owner, s, regs)
                        pe.wait_ge(hot, s + 1 + CREDIT)
                        for j in range(4):
                            pe.wait_ge(multiplied, f.at(multiplied, s, j, back=1))
                            for t in (2 * j, 2 * j + 1):
                                op = T_.matmul(q_ps[:, j, t % 2, :], to_edge[g][:, t * P:(t + 1) * P],
                                               k.q_all[:, ds(owners[t] * D, D)], start=True, stop=True)
                            op.then_inc(queried, 1)
                        pe.wait_ge(scored, s + 1 + CREDIT)
                        pe.wait_ge(ran, s + CREDIT)
                        pe.sem_inc(turns, 1)
                        T_.transpose(sT_ps[0:G * HEADS, 0:P], sg[g][:].rearrange("p t h -> p (t h)"), k.ident[:]).then_inc(s_turned, 1)
                        pe.wait_ge(ran, s + 1 + CREDIT)
                        pe.wait_ge(topped, s + CREDIT)
                        pe.sem_inc(turns, 1)
                        T_.transpose(run_ps[:, 0:G * HEADS], run[g][:], k.ident[0:G * HEADS, 0:G * HEADS]).then_inc(r_turned, 1)
                        pe.wait_ge(topped, s + 1 + CREDIT)
                        pe.wait_ge(merged, s + CREDIT)
                        for t in range(G):
                            op = T_.matmul(top_ps[:, t * (HEADS + 1):(t + 1) * (HEADS + 1)], to_node[g][:, t, :], tops[g][:, t, :],
                                           start=True, stop=True)
                        op.then_inc(at_nodes, 1)


def edge_sums(nc, k, T):
    e, W = GNN, D + HEADS
    with Phase(nc, "sums") as f:
        stage = f.pair("stage", [P, G], I32)
        dst_rows = f.pair("dst_rows", [P, G * P], BF16)
        to_node, to_edge = f.pair("to_node", [P, G, P]), f.pair("to_edge", [P, G * P])
        vb = f.pair("vb", [P, G, W])
        shifted = f.pair("shifted", [P, G, HEADS])
        m_ps = f.ps("m_ps", [P, 512])
        sum_ps = f.ps("sum_ps", [P, 4, 512])
        staged, issued = f.sem("staged"), f.sem("issued")
        gathered, rows_in = f.dma_pair("gathered"), f.dma_pair("rows_in")
        hot, maxima, shift_done, weighed, scaled = (
            f.sem(x) for x in ("hot", "maxima", "shift_done", "weighed", "scaled"))
        summed, added = f.sem("summed", G), f.sem("added", G)
        f.start()
        with nc.Block() as block:
            @block.sync
            def _(sp):
                with sp.Fori(0, e.steps, 1) as i:
                    for g in range(2):
                        s = i * 2 + g
                        sp.wait_ge(hot, s + 1)
                        sp.dma_start(dst_rows[g][:], T.rows[ds(s * G, G), :].rearrange("(a t) e -> a (t e)", a=1)
                                     .to_broadcast([P, G * P])).then_inc(rows_in[g], 16)

            @block.gpsimd
            def _(pool):
                with pool.Fori(0, e.steps, 1) as i:
                    for g in range(2):
                        s = i * 2 + g
                        pool.wait_ge(staged, s + 1 + CREDIT)
                        pool.sem_inc(issued, 1)
                        pool.wait_ge(summed, f.at(summed, s, back=2))
                        pool.sem_inc(issued, 1)
                        for t in range(G):
                            pool.indirect_dma_start(out=vb[g][:, t, 0:D], out_offset=None, in_=k.VT,
                                                    in_offset=bass.IndirectOffsetOnAxis(ap=stage[g][:, t:t + 1], axis=0)
                                                    ).then_inc(gathered[g], 16)

            @block.vector
            def _(dve):
                V = nc.vector
                V.memset(k.a_all[:], 0.0)
                V.tensor_copy(stage[0][:], T.idx_v[:, 0:G]).then_inc(staged, 1)
                V.tensor_copy(stage[1][:], T.idx_v[:, G:2 * G]).then_inc(staged, 1)
                dve.drain()
                regs = [dve.alloc_register(f"sum_owner{t}") for t in range(G)]
                with dve.Fori(0, e.steps, 1) as i:
                    for g in range(2):
                        s = i * 2 + g
                        owners = load_owners(dve, T.owner, s, regs)
                        dve.wait_ge(rows_in[g], i * 16 + 16)
                        dve.wait_ge(summed, f.at(summed, s, back=2))
                        one_hots(nc, k, dve, T, s, g, dst_rows, to_node, to_edge)
                        dve.drain().then_inc(hot, 1)
                        dve.wait_ge(maxima, s + 1 + CREDIT)
                        V.tensor_tensor(shifted[g][:].rearrange("p t h -> p (t h)"), k.s_all[:, ds(s * G * HEADS, G * HEADS)],
                                        m_ps[:, 0:G * HEADS], ALU.subtract).then_inc(shift_done, 1)
                        dve.wait_ge(gathered[g], (i + 1) * (16 * G))
                        V.tensor_copy(stage[g][:], T.idx_v[:, ds(s * G + 2 * G, G)]).then_inc(staged, 1)
                        dve.wait_ge(weighed, s + 1 + CREDIT)
                        v = vb[g][:, :, 0:D].rearrange("p t (h e) -> p t h e", e=HD)
                        V.tensor_tensor(v, v, vb[g][:, :, D:W].unsqueeze(3).to_broadcast([P, G, HEADS, HD]), ALU.mult).then_inc(scaled, 1)
                        for t in range(G):
                            dve.wait_ge(summed, f.at(summed, s, t))
                            a = k.a_all[:, ds(owners[t] * W, W)]
                            V.tensor_tensor(a, a, sum_ps[:, t % 4, 0:W], ALU.add).then_inc(added, 1)
                            dve.drain()

            @block.scalar
            def _(act):
                with act.Fori(0, e.steps, 1) as i:
                    for g in range(2):
                        s = i * 2 + g
                        act.wait_ge(shift_done, s + 1 + CREDIT)
                        act.wait_ge(summed, f.at(summed, s, back=2))
                        nc.scalar.activation(vb[g][:, :, D:W], shifted[g][:], ACT.Exp).then_inc(weighed, 1)

            @block.tensor
            def _(pe):
                T_ = nc.tensor
                regs = [pe.alloc_register(f"sum_owner{t}") for t in range(G)]
                with pe.Fori(0, e.steps, 1) as i:
                    for g in range(2):
                        s = i * 2 + g
                        owners = load_owners(pe, T.owner, s, regs)
                        pe.wait_ge(hot, s + 1 + CREDIT)
                        pe.wait_ge(shift_done, s + CREDIT)
                        for t in range(G):
                            op = T_.matmul(m_ps[:, t * HEADS:(t + 1) * HEADS], to_edge[g][:, t * P:(t + 1) * P],
                                           k.m_all[:, ds(owners[t] * HEADS, HEADS)], start=True, stop=True)
                        op.then_inc(maxima, 1)
                        pe.wait_ge(scaled, s + 1 + CREDIT)
                        for t in range(G):
                            pe.wait_ge(added, f.at(added, s, t - 4) if t >= 4 else f.at(added, s, t + 4, back=1))
                            T_.matmul(sum_ps[:, t % 4, 0:W], to_node[g][:, t, :], vb[g][:, t, :], start=True, stop=True).then_inc(summed, 1)
def row_of(w, l):
    return w[ds(l, 1), :].to_broadcast([P, w.shape[1]])


def finish_layer(nc, k, l):
    FC, W = DFF // P, D + HEADS
    PAIRS = NODE_TILES // 2
    with Phase(nc, "finish") as f:
        wo, w1, w2 = f.sb("wo", [P, 2, D]), f.sb("w1", [P, 2, DFF]), f.sb("w2", [P, FC, D])
        b1 = f.sb("b1", [P, FC])
        rows = {n: f.sb(n, [P, D]) for n in ("bo", "g1", "s1", "b2", "g2", "s2")}
        den, at = f.pair("den", [P, HEADS]), f.pair("at", [P, D])
        aT = f.pair("aT", [P, 2, P])
        xt, y, x1, z = f.pair("xt", [P, D]), f.pair("y", [P, D]), f.pair("x1", [P, D]), f.pair("z", [P, D])
        x1T, hT = f.sb("x1T", [P, 2, 2, P]), f.sb("hT", [P, FC, 2 * P])
        norm1, norm2 = Norm(nc, k, f, "norm1"), Norm(nc, k, f, "norm2")
        turn_ps = f.ps("turn_ps", [P, 2, 2, D])
        aT_ps = turn_ps[:, :, 0, :].rearrange("p g (c n) -> p g c n", n=P)
        o_ps = turn_ps[:, :, 1, :]
        h_ps = f.ps("h_ps", [P, FC, 2 * P])
        y_ps = f.ps("y_ps", [P, 2, 512])
        weights, loaded, stored = f.dma_sem("weights"), f.dma_pair("loaded"), f.store_pair("stored")
        divided, a_turned, a_copied, projected, attended = (
            f.sem(x) for x in ("divided", "a_turned", "a_copied", "projected", "attended"))
        x_ready, x_turned, x_copied, contracted, finished = (
            f.sem(x) for x in ("x_ready", "x_turned", "x_copied", "contracted", "finished"))
        hidden, activated = f.sem("hidden", FC // 2), f.sem("activated", FC // 2)
        f.start()
        with nc.Block() as block:
            @block.sync
            def _(sp):
                one = ds(l, 1)
                for to, of in ((wo[:], k.Wo[one, :, :].rearrange("a (c p) n -> p (a c) n", p=P)),
                               (w1[:], k.w1[one, :, :].rearrange("a (c p) n -> p (a c) n", p=P)),
                               (w2[:], k.w2[one, :, :].rearrange("a (c p) n -> p (a c) n", p=P))):
                    sp.dma_start(to, of).then_inc(weights, 16)
                with nc.allow_non_contiguous_dma(reason="1024 words"):
                    sp.dma_start(b1[:], k.b1[one, :].rearrange("a (c p) -> p (a c)", p=P)).then_inc(weights, 16)
                for n, w in (("bo", k.bo), ("g1", k.ln1_g), ("s1", k.ln1_b), ("b2", k.b2), ("g2", k.ln2_g), ("s2", k.ln2_b)):
                    sp.dma_start(rows[n][:], row_of(w, l)).then_inc(weights, 16)
                with sp.Fori(0, PAIRS, 1) as i:
                    for g in range(2):
                        s = i * 2 + g
                        sp.wait_ge(attended, s + 1)
                        sp.dma_start(xt[g][:], rows_of(k.X, s)).then_inc(loaded[g], 16)

            @block.gpsimd
            def _(pool):
                with pool.Fori(0, PAIRS, 1) as i:
                    for norm in (norm1, norm2):
                        for g in range(2):
                            norm.root(pool, g, i * 2 + g)

            @block.vector
            def _(dve):
                V = nc.vector
                dve.wait_ge(weights, 16 * 10)
                with dve.Fori(0, PAIRS, 1) as i:
                    for g in range(2):
                        s = i * 2 + g
                        V.tensor_single_scalar(den[g][:], k.a_all[:, ds(s * W + D, HEADS)], 1e-10, op=ALU.add)
                    dve.drain()
                    for g in range(2):
                        V.reciprocal(den[g][:], den[g][:])
                    dve.drain()
                    for g in range(2):
                        s = i * 2 + g
                        dve.wait_ge(a_turned, s + 1)
                        V.tensor_tensor(at[g][:].rearrange("p (h e) -> p h e", e=HD),
                                        k.a_all[:, ds(s * W, D)].rearrange("p (h e) -> p h e", e=HD),
                                        den[g][:].unsqueeze(2).to_broadcast([P, HEADS, HD]), ALU.mult).then_inc(divided, 1)
                    for g in range(2):
                        s = i * 2 + g
                        dve.wait_ge(projected, s + 1 + CREDIT)
                        dve.wait_ge(loaded[g], i * 16 + 16)
                        V.tensor_tensor(y[g][:], o_ps[:, g, :], xt[g][:], ALU.add).then_inc(attended, 1)
                    dve.drain()
                    for g in range(2):
                        V.tensor_tensor(y[g][:], y[g][:], rows["bo"][:], ALU.add)
                    dve.drain()
                    for g in range(2):
                        norm1.moments(dve, g, y[g][:])
                    for g in range(2):
                        norm1.apply(dve, g, i * 2 + g, x1[g][:], y[g][:])
                    dve.drain()
                    for g in range(2):
                        V.tensor_tensor(x1[g][:], x1[g][:], rows["g1"][:], ALU.mult)
                    dve.drain()
                    for g in range(2):
                        V.tensor_tensor(x1[g][:], x1[g][:], rows["s1"][:], ALU.add).then_inc(x_ready, 1)
                    dve.drain()
                    for g in range(2):
                        s = i * 2 + g
                        dve.wait_ge(contracted, s + 1 + CREDIT)
                        V.tensor_tensor(y[g][:], y_ps[:, g, 0:D], x1[g][:], ALU.add)
                    dve.drain()
                    for g in range(2):
                        V.tensor_tensor(y[g][:], y[g][:], rows["b2"][:], ALU.add)
                    dve.drain()
                    for g in range(2):
                        norm2.moments(dve, g, y[g][:])
                    for g in range(2):
                        dve.wait_ge(stored[g], i * 16 + 16)
                        norm2.apply(dve, g, i * 2 + g, z[g][:], y[g][:])
                    dve.drain()
                    for g in range(2):
                        V.tensor_tensor(z[g][:], z[g][:], rows["g2"][:], ALU.mult)
                    dve.drain()
                    for g in range(2):
                        V.tensor_tensor(z[g][:], z[g][:], rows["s2"][:], ALU.add).then_inc(finished, 1)
                    dve.drain()

            @block.tensor
            def _(pe):
                T = nc.tensor
                pe.wait_ge(weights, 16 * 10)
                with pe.Fori(0, PAIRS, 1) as i:
                    for g in range(2):
                        s = i * 2 + g
                        pe.wait_ge(divided, s + 1 + CREDIT)
                        pe.wait_ge(x_copied, s + 1)
                        for half in range(2):
                            op = T.transpose(aT_ps[:, g, half, :], at[g][:, half * P:(half + 1) * P], k.ident[:])
                        op.then_inc(a_turned, 1)
                    for g in range(2):
                        s = i * 2 + g
                        pe.wait_ge(a_copied, s + 1 + CREDIT)
                        pe.wait_ge(attended, s + 1)
                        for half in range(2):
                            op = T.matmul(o_ps[:, g, :], aT[g][:, half, :], wo[:, half, :], start=(half == 0), stop=(half == 1))
                        op.then_inc(projected, 1)
                    for g in range(2):
                        s = i * 2 + g
                        pe.wait_ge(x_ready, s + 1 + CREDIT)
                        for half in range(2):
                            op = T.transpose(aT_ps[:, g, half, :], x1[g][:, half * P:(half + 1) * P], k.ident[:])
                        op.then_inc(x_turned, 1)
                    pe.wait_ge(x_copied, i * 2 + 2 + CREDIT)
                    for c in range(FC):
                        if c % 2 == 0:
                            pe.wait_ge(activated, f.at(activated, i, c // 2, back=1))
                        for half in range(2):
                            op = T.matmul(h_ps[:, c, :], w1[:, half, c * P:(c + 1) * P], x1T[:, half, :, :].rearrange("p g n -> p (g n)"),
                                          start=(half == 0), stop=(half == 1))
                        if c % 2:
                            op.then_inc(hidden, 1)
                    for g in range(2):
                        s = i * 2 + g
                        pe.wait_ge(finished, s + 1)
                        for c in range(FC):
                            if g == 0 and c % 2 == 0:
                                pe.wait_ge(activated, f.at(activated, i, c // 2))
                            op = T.matmul(y_ps[:, g, 0:D], hT[:, c, g * P:(g + 1) * P], w2[:, c, :], start=(c == 0), stop=(c == FC - 1))
                        op.then_inc(contracted, 1)

            @block.scalar
            def _(act):
                A = nc.scalar
                act.wait_ge(weights, 16 * 10)
                with act.Fori(0, PAIRS, 1) as i:
                    for g in range(2):
                        s = i * 2 + g
                        act.wait_ge(a_turned, s + 1 + CREDIT)
                        act.wait_ge(projected, s + 1)
                        A.copy(aT[g][:], aT_ps[:, g, :, :]).then_inc(a_copied, 1)
                    for g in range(2):
                        s = i * 2 + g
                        act.wait_ge(x_turned, s + 1 + CREDIT)
                        act.wait_ge(hidden, f.at(hidden, i, back=1))
                        A.copy(x1T[:, :, g, :], aT_ps[:, g, :, :]).then_inc(x_copied, 1)
                    act.wait_ge(contracted, i * 2 + CREDIT)
                    for c in range(FC):
                        if c % 2 == 0:
                            act.wait_ge(hidden, f.at(hidden, i, c // 2))
                        op = A.activation(hT[:, c, :], h_ps[:, c, :], ACT.Gelu, bias=b1[:, c:c + 1])
                        if c % 2:
                            act.drain().then_inc(activated, 1)
                    for g in range(2):
                        s = i * 2 + g
                        act.wait_ge(finished, s + 1 + CREDIT)
                        act.dma_start(rows_of(k.X, s), z[g][:]).then_inc(stored[g], 16)
                for g in range(2):
                    act.wait_ge(stored[g], 16 * PAIRS + 16)


def route_inputs(nc, k):
    PAIRS = NODE_TILES // 2
    ROW = GW + GH
    with Phase(nc, "inputs") as f:
        wg = f.sb("wg", [P, 2, GW])
        att = f.sb("att", [P, 2, GW])
        og, ob = f.sb("og", [P, D]), f.sb("ob", [P, D])
        xt, x0, y, x2, xn = (f.pair(n, [P, D]) for n in ("xt", "x0", "y", "x2", "xn"))
        xT, tab, prod = f.pair("xT", [P, 2, P]), f.pair("tab", [P, ROW]), f.pair("prod", [P, 2, GW])
        norm1, norm2 = Norm(nc, k, f, "norm1"), Norm(nc, k, f, "norm2")
        xT_ps, h_ps = f.ps("xT_ps", [P, 2, 4, P]), f.ps("h_ps", [P, 2, 512])
        weights, loaded = f.dma_sem("weights"), f.dma_pair("loaded")
        stored = f.store_pair("stored")
        ready, normed, turned, copied, product, tabled = (f.sem(x) for x in ("ready", "normed", "turned", "copied", "product", "tabled"))
        f.start()
        with nc.Block() as block:
            @block.sync
            def _(sp):
                sp.dma_start(wg[:], k.W_gat.rearrange("(c p) n -> p c n", p=P)).then_inc(weights, 16)
                for n, w in enumerate((k.att_src, k.att_dst)):
                    sp.dma_start(att[:, n, :], w.rearrange("(a h) e -> a (h e)", a=1).to_broadcast([P, GW])).then_inc(weights, 16)
                sp.dma_start(og[:], k.out_g.rearrange("(a n) -> a n", a=1).to_broadcast([P, D])).then_inc(weights, 16)
                sp.dma_start(ob[:], k.out_b.rearrange("(a n) -> a n", a=1).to_broadcast([P, D])).then_inc(weights, 16)
                with sp.Fori(0, PAIRS, 1) as i:
                    for g in range(2):
                        s = i * 2 + g
                        sp.wait_ge(ready, s + 1)
                        sp.dma_start(xt[g][:], rows_of(k.X, s)).then_inc(loaded[g], 16)
                        sp.dma_start(x0[g][:], rows_of(k.XP, s)).then_inc(loaded[g], 16)

            @block.gpsimd
            def _(pool):
                with pool.Fori(0, PAIRS, 1) as i:
                    for norm in (norm1, norm2):
                        for g in range(2):
                            norm.root(pool, g, i * 2 + g)

            @block.vector
            def _(dve):
                V = nc.vector
                dve.wait_ge(weights, 16 * 5)
                with dve.Fori(0, PAIRS, 1) as i:
                    for g in range(2):
                        dve.wait_ge(loaded[g], i * 32 + 32)
                        norm1.moments(dve, g, xt[g][:])
                    for g in range(2):
                        norm1.apply(dve, g, i * 2 + g, y[g][:], xt[g][:])
                    dve.drain()
                    for g in range(2):
                        V.tensor_tensor(y[g][:], y[g][:], og[:], ALU.mult)
                    dve.drain()
                    for g in range(2):
                        V.tensor_tensor(y[g][:], y[g][:], ob[:], ALU.add)
                    dve.drain()
                    for g in range(2):
                        dve.wait_ge(stored[g], i * 48 + 16)
                        V.tensor_tensor(x2[g][:], y[g][:], x0[g][:], ALU.add).then_inc(ready, 1)
                    dve.drain()
                    for g in range(2):
                        norm2.moments(dve, g, x2[g][:])
                    for g in range(2):
                        norm2.apply(dve, g, i * 2 + g, xn[g][:], x2[g][:])
                        dve.drain().then_inc(normed, 1)
                    for g in range(2):
                        s = i * 2 + g
                        dve.wait_ge(product, s + 1 + CREDIT)
                        V.tensor_copy(tab[g][:, 0:GW], h_ps[:, g, 0:GW])
                    dve.drain()
                    for g in range(2):
                        V.tensor_tensor(prod[g][:], tab[g][:, 0:GW].unsqueeze(1).to_broadcast([P, 2, GW]), att[:], ALU.mult)
                    dve.drain()
                    for g in range(2):
                        s = i * 2 + g
                        pr = prod[g][:].rearrange("p a (h e) -> p a h e", e=EXPERTS)
                        V.tensor_reduce(tab[g][:, GW:ROW], pr[:, 0, :, :], AX.X, ALU.add)
                        V.tensor_reduce(k.dst_term[:, ds(s * GH, GH)], pr[:, 1, :, :], AX.X, ALU.add)
                    dve.drain()
                    for g in range(2):
                        s = i * 2 + g
                        V.tensor_copy(k.h_all[:, ds(s * ROW, ROW)], tab[g][:])
                    dve.drain().then_inc(tabled, 1)

            @block.tensor
            def _(pe):
                T = nc.tensor
                pe.wait_ge(weights, 16 * 5)
                with pe.Fori(0, PAIRS, 1) as i:
                    for g in range(2):
                        s = i * 2 + g
                        pe.wait_ge(normed, s + 1 + CREDIT)
                        pe.wait_ge(copied, s + 1)
                        for half in range(2):
                            op = T.transpose(xT_ps[:, g, half, :], xn[g][:, half * P:(half + 1) * P], k.ident[:])
                        op.then_inc(turned, 1)
                    for g in range(2):
                        s = i * 2 + g
                        pe.wait_ge(copied, s + 1 + CREDIT)
                        pe.wait_ge(tabled, i + CREDIT)
                        for half in range(2):
                            op = T.matmul(h_ps[:, g, 0:GW], xT[g][:, half, :], wg[:, half, :], start=(half == 0), stop=(half == 1))
                        op.then_inc(product, 1)

            @block.scalar
            def _(act):
                with act.Fori(0, PAIRS, 1) as i:
                    for g in range(2):
                        s = i * 2 + g
                        act.wait_ge(turned, s + 1 + CREDIT)
                        act.wait_ge(product, s + 1)
                        nc.scalar.copy(xT[g][:], xT_ps[:, g, 0:2, :]).then_inc(copied, 1)
                    act.wait_ge(tabled, i + 1 + CREDIT)
                    for g in range(2):
                        s = i * 2 + g
                        act.dma_start(rows_of(k.X2, s), x2[g][:]).then_inc(stored[g], 16)
                        act.dma_start(rows_of(k.XN, s), xn[g][:]).then_inc(stored[g], 16)
                        act.dma_start(rows_of(k.HT, s), tab[g][:]).then_inc(stored[g], 16)
                for g in range(2):
                    act.wait_ge(stored[g], 48 * PAIRS + 16)


def route_maxima(nc, k, T):
    e, ROW = GAT, GW + GH
    with Phase(nc, "maxima") as f:
        stage = f.pair("stage", [P, G], I32)
        gb = f.pair("gb", [P, G, ROW])
        dst_rows, other = f.pair("dst_rows", [P, G * P], BF16), f.pair("other", [P, G, P])
        term = f.pair("term", [P, GH, P])
        mt = f.pair("mt", [P, G, GH])
        spread_ps = f.ps("spread_ps", [P, 4, GH * P])
        staged, issued = f.sem("staged"), f.sem("issued")
        gathered, rows_in = f.dma_pair("gathered"), f.dma_pair("rows_in")
        compared, kept = f.sem("compared"), f.sem("kept")
        spread, masked = f.sem("spread", G), f.sem("masked", G)
        f.start()
        with nc.Block() as block:
            @block.sync
            def _(sp):
                with sp.Fori(0, e.steps, 1) as i:
                    for g in range(2):
                        s = i * 2 + g
                        sp.wait_ge(compared, s + 1)
                        sp.dma_start(dst_rows[g][:], T.rows[ds(s * G, G), :].rearrange("(a t) e -> a (t e)", a=1)
                                     .to_broadcast([P, G * P])).then_inc(rows_in[g], 16)

            @block.gpsimd
            def _(pool):
                with pool.Fori(0, e.steps, 1) as i:
                    for g in range(2):
                        s = i * 2 + g
                        pool.wait_ge(staged, s + 1 + CREDIT)
                        pool.sem_inc(issued, 1)
                        pool.wait_ge(spread, f.at(spread, s, back=2))
                        pool.sem_inc(issued, 1)
                        pool.wait_ge(kept, s + 1)
                        pool.sem_inc(issued, 1)
                        for t in range(G):
                            pool.indirect_dma_start(out=gb[g][:, t, :], out_offset=None, in_=k.HT,
                                                    in_offset=bass.IndirectOffsetOnAxis(ap=stage[g][:, t:t + 1], axis=0)
                                                    ).then_inc(gathered[g], 16)

            @block.vector
            def _(dve):
                V = nc.vector
                V.tensor_copy(k.gm_all[:].rearrange("p (n h) -> p n h", h=GH),
                              k.h_all[:].rearrange("p (n r) -> p n r", r=ROW)[:, :, GW:ROW])
                V.tensor_copy(stage[0][:], T.idx_v[:, 0:G]).then_inc(staged, 1)
                V.tensor_copy(stage[1][:], T.idx_v[:, G:2 * G]).then_inc(staged, 1)
                dve.drain()
                regs = [dve.alloc_register(f"max_owner{t}") for t in range(G)]
                with dve.Fori(0, e.steps, 1) as i:
                    for g in range(2):
                        s = i * 2 + g
                        owners = load_owners(dve, T.owner, s, regs)
                        dve.wait_ge(rows_in[g], i * 16 + 16)
                        V.tensor_scalar(other[g][:].rearrange("p t e -> p (t e)"), dst_rows[g][:], k.iota_p[:], NEG,
                                        ALU.not_equal, ALU.mult).then_inc(compared, 1)
                        dve.wait_ge(gathered[g], (i + 1) * (16 * G))
                        V.tensor_copy(stage[g][:], T.idx_v[:, ds(s * G + 2 * G, G)]).then_inc(staged, 1)
                        dve.drain()
                        for t in range(G):
                            dve.wait_ge(spread, f.at(spread, s, t))
                            V.tensor_tensor(term[t % 2][:], spread_ps[:, t % 4, :].rearrange("p (h e) -> p h e", e=P),
                                            other[g][:, t, :].unsqueeze(1).to_broadcast([P, GH, P]), ALU.add).then_inc(masked, 1)
                            dve.drain()
                            V.tensor_reduce(mt[g][:, t, :], term[t % 2][:], AX.X, ALU.max)
                        dve.drain()
                        for t in range(G):
                            m = k.gm_all[:, ds(owners[t] * GH, GH)]
                            V.tensor_tensor(m, m, mt[g][:, t, :], ALU.max)
                            dve.drain()

            @block.scalar
            def _(act):
                with act.Fori(0, e.steps, 1) as i:
                    for g in range(2):
                        s = i * 2 + g
                        act.wait_ge(gathered[g], (i + 1) * (16 * G))
                        nc.scalar.copy(k.g_all[:, ds(s * G * ROW, G * ROW)], gb[g][:].rearrange("p t r -> p (t r)")).then_inc(kept, 1)

            @block.tensor
            def _(pe):
                with pe.Fori(0, e.steps, 1) as i:
                    for g in range(2):
                        s = i * 2 + g
                        pe.wait_ge(gathered[g], (i + 1) * (16 * G))
                        for t in range(G):
                            pe.wait_ge(masked, f.at(masked, s, t - 4) if t >= 4 else f.at(masked, s, t + 4, back=1))
                            for h in range(GH):
                                op = nc.tensor.matmul(spread_ps[:, t % 4, h * P:(h + 1) * P],
                                                      gb[g][:, t, GW + h:GW + h + 1].to_broadcast([P, P]), k.ident[:], start=True, stop=True)
                            op.then_inc(spread, 1)


def route_sums(nc, k, T):
    e, ROW, ALL = GAT, GW + GH, NODE_TILES
    with Phase(nc, "route") as f:
        dst_rows = f.pair("dst_rows", [P, G * P], BF16)
        to_node, to_edge = f.pair("to_node", [P, G, P]), f.pair("to_edge", [P, G * P])
        own = f.sb("own", [P, ALL, GH])
        tmp = f.sb("tmp", [P, ALL, GH])
        terms = f.pair("terms", [P, G, GH])
        wv = f.pair("wv", [P, G, ROW])
        back_ps, sum_ps = f.ps("back_ps", [P, 512]), f.ps("sum_ps", [P, 512])
        rows_in = f.dma_pair("rows_in")
        own_ready, own_exp, hot, fetched, formed, weighed, scaled, summed, added, fetched_read = (
            f.sem(x) for x in ("own_ready", "own_exp", "hot", "fetched", "formed", "weighed", "scaled", "summed", "added", "fetched_read"))
        both = k.t2_all[:].rearrange("p (n x) -> p n x", x=2 * GH)
        h_rows = k.h_all[:].rearrange("p (n r) -> p n r", r=ROW)
        f.start()
        with nc.Block() as block:
            @block.sync
            def _(sp):
                with sp.Fori(0, e.steps, 1) as i:
                    for g in range(2):
                        s = i * 2 + g
                        sp.wait_ge(hot, s + 1)
                        sp.dma_start(dst_rows[g][:], T.rows[ds(s * G, G), :].rearrange("(a t) e -> a (t e)", a=1)
                                     .to_broadcast([P, G * P])).then_inc(rows_in[g], 16)

            @block.vector
            def _(dve):
                V = nc.vector

                def leaky(out, tmp_, x):
                    V.tensor_single_scalar(tmp_, x, 0.2, op=ALU.mult)
                    dve.drain()
                    V.tensor_tensor(out, x, tmp_, ALU.max)
                    dve.drain()

                dst = k.dst_term[:].rearrange("p (n h) -> p n h", h=GH)
                top = k.gm_all[:].rearrange("p (n h) -> p n h", h=GH)
                V.tensor_copy(both[:, :, 0:GH], dst)
                V.tensor_tensor(top, top, dst, ALU.add)
                dve.drain()
                leaky(both[:, :, GH:2 * GH], tmp[:], top)
                V.tensor_tensor(own[:], h_rows[:, :, GW:ROW], dst, ALU.add)
                dve.drain()
                leaky(own[:], tmp[:], own[:])
                V.tensor_tensor(own[:], own[:], both[:, :, GH:2 * GH], ALU.subtract)
                dve.drain().then_inc(own_ready, 1)
                dve.wait_ge(own_exp, 1 + CREDIT)
                sums = k.gs_all[:].rearrange("p (n r) -> p n r", r=ROW)
                V.tensor_copy(sums[:, :, GW:ROW], own[:])
                V.tensor_tensor(sums[:, :, 0:GW].rearrange("p n (h x) -> p n h x", x=EXPERTS),
                                h_rows[:, :, 0:GW].rearrange("p n (h x) -> p n h x", x=EXPERTS),
                                own[:].unsqueeze(3).to_broadcast([P, ALL, GH, EXPERTS]), ALU.mult)
                dve.drain()
                regs = [dve.alloc_register(f"route_owner{t}") for t in range(G)]
                with dve.Fori(0, e.steps, 1) as i:
                    for g in range(2):
                        s = i * 2 + g
                        owners = load_owners(dve, T.owner, s, regs)
                        dve.wait_ge(rows_in[g], i * 16 + 16)
                        dve.wait_ge(summed, s + 1)
                        one_hots(nc, k, dve, T, s, g, dst_rows, to_node, to_edge)
                        dve.drain().then_inc(hot, 1)
                        dve.wait_ge(fetched, s + 1 + CREDIT)
                        rows = k.g_all[:, ds(s * G * ROW, G * ROW)].rearrange("p (t r) -> p t r", r=ROW)
                        back = back_ps[:, 0:G * 2 * GH].rearrange("p (t x) -> p t x", x=2 * GH)
                        t_ = terms[g]
                        V.tensor_tensor(t_[:], rows[:, :, GW:ROW], back[:, :, 0:GH], ALU.add)
                        dve.drain()
                        V.scalar_tensor_tensor(out=t_[:], in0=t_[:], scalar=0.2, in1=t_[:], op0=ALU.mult, op1=ALU.max)
                        dve.drain()
                        V.tensor_tensor(t_[:], t_[:], back[:, :, GH:2 * GH], ALU.subtract).then_inc(formed, 1)
                        dve.wait_ge(weighed, s + 1 + CREDIT)
                        V.tensor_tensor(wv[g][:, :, 0:GW].rearrange("p t (h x) -> p t h x", x=EXPERTS),
                                        rows[:, :, 0:GW].rearrange("p t (h x) -> p t h x", x=EXPERTS),
                                        wv[g][:, :, GW:ROW].unsqueeze(3).to_broadcast([P, G, GH, EXPERTS]), ALU.mult).then_inc(scaled, 1)
                        dve.wait_ge(summed, s + 1 + CREDIT)
                        for t in range(G):
                            a = k.gs_all[:, ds(owners[t] * ROW, ROW)]
                            V.tensor_tensor(a, a, sum_ps[:, t * ROW:(t + 1) * ROW], ALU.add)
                            if t == G - 1:
                                dve.drain().then_inc(added, 1)
                            else:
                                dve.drain()

            @block.scalar
            def _(act):
                act.wait_ge(own_ready, 1 + CREDIT)
                nc.scalar.activation(own[:], own[:], ACT.Exp).then_inc(own_exp, 1)
                with act.Fori(0, e.steps, 1) as i:
                    for g in range(2):
                        s = i * 2 + g
                        act.wait_ge(formed, s + 1 + CREDIT)
                        act.wait_ge(summed, s + 1)
                        nc.scalar.activation(wv[g][:, :, GW:ROW], terms[g][:], ACT.Exp).then_inc(weighed, 1)

            @block.tensor
            def _(pe):
                regs = [pe.alloc_register(f"route_owner{t}") for t in range(G)]
                with pe.Fori(0, e.steps, 1) as i:
                    for g in range(2):
                        s = i * 2 + g
                        owners = load_owners(pe, T.owner, s, regs)
                        pe.wait_ge(hot, s + 1 + CREDIT)
                        pe.wait_ge(formed, s + CREDIT)
                        for t in range(G):
                            op = nc.tensor.matmul(back_ps[:, t * 2 * GH:(t + 1) * 2 * GH], to_edge[g][:, t * P:(t + 1) * P],
                                                  k.t2_all[:, ds(owners[t] * 2 * GH, 2 * GH)], start=True, stop=True)
                        op.then_inc(fetched, 1)
                        pe.wait_ge(scaled, s + 1 + CREDIT)
                        pe.wait_ge(added, s + CREDIT)
                        for t in range(G):
                            op = nc.tensor.matmul(sum_ps[:, t * ROW:(t + 1) * ROW], to_node[g][:, t, :], wv[g][:, t, :], start=True, stop=True)
                        op.then_inc(summed, 1)


def route_gates(nc, k):
    ROW, ALL = GW + GH, NODE_TILES
    with Phase(nc, "gates") as f:
        bg, gam, bet = (f.sb(n, [P, GW]) for n in ("bg", "gam", "bet"))
        agg, dev, sq = (f.sb(n, [P, ALL, GW]) for n in ("agg", "dev", "sq"))
        den = f.sb("den", [P, ALL, GH])
        mean, var, rstd, top, tot = (f.sb(n, [P, ALL]) for n in ("mean", "var", "rstd", "top", "tot"))
        sc, rank, cmp = (f.sb(n, [P, ALL, EXPERTS]) for n in ("sc", "rank", "cmp"))
        eq = f.sb("eq", [P, ALL])
        weights, var_ready, rooted, shifted, exps = f.dma_sem("weights"), f.sem("var_ready"), f.sem("rooted"), f.sem("shifted"), f.sem("exps")
        gates = k.gates[:].rearrange("p (n x) -> p n x", x=EXPERTS)
        f.start()
        with nc.Block() as block:
            @block.sync
            def _(sp):
                for to, of in ((bg, k.b_gat), (gam, k.ln_gamma), (bet, k.ln_beta)):
                    sp.dma_start(to[:], of.rearrange("(a n) -> a n", a=1).to_broadcast([P, GW])).then_inc(weights, 16)

            @block.gpsimd
            def _(pool):
                pool.wait_ge(var_ready, 1 + CREDIT)
                nc.gpsimd.tensor_tensor(rstd[:], var[:], k.power[:].to_broadcast([P, ALL]), ALU.pow).then_inc(rooted, 1)

            @block.scalar
            def _(act):
                act.wait_ge(shifted, 1 + CREDIT)
                nc.scalar.activation(cmp[:], cmp[:], ACT.Exp).then_inc(exps, 1)

            @block.vector
            def _(dve):
                V = nc.vector
                sums = k.gs_all[:].rearrange("p (n r) -> p n r", r=ROW)

                def step(op):
                    dve.drain()

                def wide(row):
                    return row[:].unsqueeze(1).to_broadcast([P, ALL, GW])

                def along(x, n):
                    return x[:].unsqueeze(2).to_broadcast([P, ALL, n])

                dve.wait_ge(weights, 48)
                step(V.tensor_single_scalar(den[:], sums[:, :, GW:ROW], 1e-16, op=ALU.add))
                step(V.reciprocal(den[:], den[:]))
                step(V.tensor_tensor(agg[:].rearrange("p n (h x) -> p n h x", x=EXPERTS),
                                     sums[:, :, 0:GW].rearrange("p n (h x) -> p n h x", x=EXPERTS),
                                     den[:].unsqueeze(3).to_broadcast([P, ALL, GH, EXPERTS]), ALU.mult))
                step(V.tensor_tensor(agg[:], agg[:], wide(bg), ALU.add))
                step(V.tensor_reduce(mean[:], agg[:], AX.X, ALU.add))
                step(V.tensor_single_scalar(mean[:], mean[:], 1.0 / GW, op=ALU.mult))
                step(V.tensor_tensor(dev[:], agg[:], along(mean, GW), ALU.subtract))
                step(V.tensor_tensor(sq[:], dev[:], dev[:], ALU.mult))
                step(V.tensor_reduce(var[:], sq[:], AX.X, ALU.add))
                V.tensor_scalar(var[:], var[:], 1.0 / GW, 1e-5, ALU.mult, ALU.add).then_inc(var_ready, 1)
                dve.wait_ge(rooted, 1 + CREDIT)
                step(V.tensor_tensor(dev[:], dev[:], along(rstd, GW), ALU.mult))
                step(V.tensor_tensor(dev[:], dev[:], wide(gam), ALU.mult))
                step(V.tensor_tensor(dev[:], dev[:], wide(bet), ALU.add))
                step(V.tensor_reduce(sc[:], dev[:].rearrange("p n (h x) -> p n x h", x=EXPERTS), AX.X, ALU.add))
                step(V.tensor_single_scalar(sc[:], sc[:], 1.0 / GH, op=ALU.mult))
                V.memset(rank[:], 0.0)
                for j in range(EXPERTS):
                    step(V.tensor_tensor(cmp[:], sc[:, :, j:j + 1].to_broadcast([P, ALL, EXPERTS]), sc[:], ALU.is_gt))
                    step(V.tensor_tensor(rank[:], rank[:], cmp[:], ALU.add))
                for i_ in range(1, EXPERTS):
                    for j in range(i_):
                        step(V.tensor_tensor(eq[:], sc[:, :, j], sc[:, :, i_], ALU.is_equal))
                        step(V.tensor_tensor(rank[:, :, i_], rank[:, :, i_], eq[:], ALU.add))
                step(V.tensor_single_scalar(rank[:], rank[:], 1.5, op=ALU.is_lt))
                step(V.tensor_reduce(top[:], sc[:], AX.X, ALU.max))
                V.tensor_tensor(cmp[:], sc[:], along(top, EXPERTS), ALU.subtract).then_inc(shifted, 1)
                dve.wait_ge(exps, 1 + CREDIT)
                step(V.tensor_tensor(cmp[:], cmp[:], rank[:], ALU.mult))
                step(V.tensor_reduce(tot[:], cmp[:], AX.X, ALU.add))
                step(V.reciprocal(tot[:], tot[:]))
                step(V.tensor_tensor(gates, cmp[:], along(tot, EXPERTS), ALU.mult))


def experts(nc, k):
    PAIRS, MC = NODE_TILES // 2, MF // P
    with Phase(nc, "experts") as f:
        w1, w2 = f.sb("w1", [P, EXPERTS, 2, MF]), f.sb("w2", [P, EXPERTS, MC, D])
        b1, b2 = f.sb("b1", [P, EXPERTS * MC]), f.sb("b2", [P, EXPERTS, D])
        xn, o, y = f.pair("xn", [P, D]), f.pair("o", [P, D]), f.pair("y", [P, D])
        xT = f.sb("xT", [P, 2, 2, P])
        hT = f.pair("hT", [P, MC, 2 * P])
        xT_ps = f.ps("xT_ps", [P, 2, 2, P])
        h_ps = [f.ps(f"h_ps{b}", [P, MC, 2 * P]) for b in range(2)]
        y_ps = [f.ps(f"y_ps{b}", [P, 2, D]) for b in range(2)]
        weights, loaded, o_loaded, stored = f.dma_sem("weights"), f.dma_pair("loaded"), f.dma_pair("o_loaded"), f.store_pair("stored")
        turned, copied = f.sem("turned"), f.sem("copied")
        BANKS = MC // 2
        hidden, activated = f.sem("hidden", EXPERTS * BANKS), f.sem("activated", EXPERTS * BANKS)
        contracted, added = f.sem("contracted", EXPERTS), f.sem("added", EXPERTS)
        f.start()
        with nc.Block() as block:
            @block.sync
            def _(sp):
                for x in range(EXPERTS):
                    sp.dma_start(w1[:, x, :, :], k.W1[x, :, :].rearrange("(c p) n -> p c n", p=P)).then_inc(weights, 16)
                    sp.dma_start(w2[:, x, :, :], k.W2[x, :, :].rearrange("(c p) n -> p c n", p=P)).then_inc(weights, 16)
                with nc.allow_non_contiguous_dma(reason="2048 words"):
                    sp.dma_start(b1[:], k.mb1.rearrange("x (c p) -> p (x c)", p=P)).then_inc(weights, 16)
                sp.dma_start(b2[:].rearrange("p x n -> p (x n)"), k.mb2.rearrange("(a x) n -> a (x n)", a=1).to_broadcast([P, EXPERTS * D])).then_inc(weights, 16)
                with sp.Fori(0, PAIRS, 1) as i:
                    for g in range(2):
                        s = i * 2 + g
                        sp.wait_ge(turned, i + CREDIT)
                        sp.dma_start(xn[g][:], rows_of(k.XN, s)).then_inc(loaded[g], 16)
                        sp.wait_ge(stored[g], i * 16 + 16)
                        sp.dma_start(o[g][:], rows_of(k.X2, s)).then_inc(o_loaded[g], 16)

            @block.vector
            def _(dve):
                V = nc.vector
                dve.wait_ge(weights, 16 * 10)
                with dve.Fori(0, PAIRS, 1) as i:
                    for g in range(2):
                        dve.wait_ge(o_loaded[g], i * 16 + 16)
                    for x in range(EXPERTS):
                        dve.wait_ge(contracted, f.at(contracted, i, x))
                        for g in range(2):
                            V.tensor_tensor(y[g][:], y_ps[x % 2][:, g, :], b2[:, x, :], ALU.add)
                        dve.drain()
                        for g in range(2):
                            V.scalar_tensor_tensor(out=o[g][:], in0=y[g][:], scalar=k.gates[:, ds((i * 2 + g) * EXPERTS + x, 1)],
                                                   in1=o[g][:], op0=ALU.mult, op1=ALU.add)
                        dve.drain().then_inc(added, 1)

            @block.tensor
            def _(pe):
                T = nc.tensor
                pe.wait_ge(weights, 16 * 10)
                with pe.Fori(0, PAIRS, 1) as i:
                    for g in range(2):
                        pe.wait_ge(loaded[g], i * 16 + 16)
                    pe.wait_ge(copied, i + CREDIT)
                    for g in range(2):
                        for half in range(2):
                            op = T.transpose(xT_ps[:, half, g, :], xn[g][:, half * P:(half + 1) * P], k.ident[:])
                    op.then_inc(turned, 1)
                    pe.wait_ge(copied, i + 1 + CREDIT)

                    def up(x):
                        for c in range(MC):
                            n = x * BANKS + c // 2
                            if c % 2 == 0:
                                pe.wait_ge(activated, f.at(activated, i, n - 2 * BANKS) if x >= 2 else f.at(activated, i, n + 2 * BANKS, back=1))
                            for half in range(2):
                                op = T.matmul(h_ps[x % 2][:, c, :], w1[:, x, half, c * P:(c + 1) * P],
                                              xT[:, half, :, :].rearrange("p g n -> p (g n)"), start=(half == 0), stop=(half == 1))
                            if c % 2:
                                op.then_inc(hidden, 1)

                    def down(x):
                        pe.wait_ge(added, f.at(added, i, x - 2) if x >= 2 else f.at(added, i, x + 2, back=1))
                        for g in range(2):
                            for c in range(MC):
                                if g == 0 and c % 2 == 0:
                                    pe.wait_ge(activated, f.at(activated, i, x * BANKS + c // 2))
                                op = T.matmul(y_ps[x % 2][:, g, :], hT[x % 2][:, c, g * P:(g + 1) * P], w2[:, x, c, :],
                                              start=(c == 0), stop=(c == MC - 1))
                        op.then_inc(contracted, 1)

                    up(0)
                    for x in range(1, EXPERTS):
                        up(x)
                        down(x - 1)
                    down(EXPERTS - 1)

            @block.scalar
            def _(act):
                A = nc.scalar
                act.wait_ge(weights, 16 * 10)
                with act.Fori(0, PAIRS, 1) as i:
                    act.wait_ge(turned, i + 1 + CREDIT)
                    act.wait_ge(hidden, f.at(hidden, i, back=1))
                    A.copy(xT[:].rearrange("p a g n -> p (a g n)"), xT_ps[:].rearrange("p a g n -> p (a g n)")).then_inc(copied, 1)
                    for x in range(EXPERTS):
                        act.wait_ge(contracted, f.at(contracted, i, x - 2) if x >= 2 else f.at(contracted, i, x + 2, back=1))
                        for c in range(MC):
                            n = x * MC + c
                            if c % 2 == 0:
                                act.wait_ge(hidden, f.at(hidden, i, n // 2))
                            A.activation(hT[x % 2][:, c, :], h_ps[x % 2][:, c, :], ACT.Gelu, bias=b1[:, n:n + 1])
                            if c % 2:
                                act.drain().then_inc(activated, 1)
                    act.wait_ge(added, f.at(added, i))
                    for g in range(2):
                        act.dma_start(rows_of(k.XO, i * 2 + g), o[g][:]).then_inc(stored[g], 16)
                for g in range(2):
                    act.wait_ge(stored[g], 16 * PAIRS + 16)


def program(nc, A):
    k = Space()
    k.x, k.src, k.dst, k.edge_type, k.node_type = (A["x"], A["src"], A["dst"], A["edge_type"], A["node_type"])
    k.W_Q, k.W_K, k.W_V, k.W_E, k.mu = (A["W_Q"], A["W_K"], A["W_V"], A["W_E"], A["mu"])
    k.Wo, k.bo, k.ln1_g, k.ln1_b, k.ln2_g = (A["Wo"], A["bo"], A["ln1_g"], A["ln1_b"], A["ln2_g"])
    k.ln2_b, k.w1, k.b1, k.w2, k.b2 = (A["ln2_b"], A["w1"], A["b1"], A["w2"], A["b2"])
    k.out_g, k.out_b, k.W_gat, k.att_src, k.att_dst = (A["out_g"], A["out_b"], A["W_gat"], A["att_src"], A["att_dst"])
    k.b_gat, k.ln_gamma, k.ln_beta, k.W1, k.mb1 = (A["b_gat"], A["ln_gamma"], A["ln_beta"], A["W1"], A["mb1"])
    k.W2, k.mb2, k.edge_src, k.edge_dst, k.out = (A["W2"], A["mb2"], A["edge_src"], A["edge_dst"], A["out"])
    with ExitStack() as ctx:
        k.sb = lambda name, shape, dt=F32: ctx.enter_context(nc.sbuf_tensor(name, shape, dt))

        def dram(name, shape, dt=F32):
            return nc.dram_tensor(name, shape, dt).ap()

        k.XP, k.X, k.X2, k.XN, k.XO = (dram(n, [NPAD, D]) for n in ("x_padded", "x_layer", "x_residual", "x_routed", "x_out"))
        k.VT, k.KT, k.HT = dram("v_table", [NPAD, D]), dram("k_table", [NPAD * EDGE_TYPES, D]), dram("h_table", [NPAD, GW + GH])
        constants(nc, k)

        def tables(name, e, gnn, scope):
            def sb(n, shape, dt=F32):
                return scope.enter_context(nc.sbuf_tensor(f"{name}_{n}", shape, dt))
            T = Space()
            T.edges, T.owner = dram(name + "_edges", [e.tiles * P, 4]), dram(name + "_owner", [1, e.chunks * P], I32)
            T.rows = dram(name + "_rows", [e.tiles, P], BF16)
            T.idx_v, T.rel = sb("idx_v", [P, e.tiles + 2 * G], I32), sb("rel", [P, e.tiles])
            if gnn:
                T.resets = dram(name + "_resets", [e.tiles, HEADS, P])
                T.idx_k, T.last = sb("idx_k", [P, e.tiles + 2 * G], I32), sb("last", [P, e.tiles])
            return T

        with ExitStack() as scope:
            T = tables("gnn", GNN, True, scope)
            sort_edges(nc, k, "gnn_sort", GNN, k.src, k.dst, k.edge_type, T)
            spread_edges(nc, k, "gnn_spread", GNN, T, True)

            def sb(n, shape, dt=F32):
                return scope.enter_context(nc.sbuf_tensor(n, shape, dt))
            k.type_mask = sb("type_mask", [P, NODE_TILES * NODE_TYPES])
            k.a_all = sb("q_or_sums", [P, NODE_TILES * (D + HEADS)])
            k.q_all = k.a_all[:, 0:NODE_TILES * D]
            k.s_all, k.m_all = sb("s_all", [P, GNN.tiles * HEADS]), sb("m_all", [P, NODE_TILES * HEADS])
            node_types(nc, k)
            first_norm(nc, k)
            with nc.Fori(0, LAYERS, 1) as l:
                project(nc, k, l)
                edge_scores(nc, k, T)
                edge_sums(nc, k, T)
                finish_layer(nc, k, l)
        with ExitStack() as scope:
            def sb(n, shape, dt=F32):
                return scope.enter_context(nc.sbuf_tensor(n, shape, dt))
            k.gates = sb("gates", [P, NODE_TILES * EXPERTS])
            with ExitStack() as inner:
                T = tables("gat", GAT, False, inner)
                sort_edges(nc, k, "gat_sort", GAT, k.edge_src, k.edge_dst, None, T)
                spread_edges(nc, k, "gat_spread", GAT, T, False)

                def sbi(n, shape, dt=F32):
                    return inner.enter_context(nc.sbuf_tensor(n, shape, dt))
                k.h_all, k.gs_all = (sbi(n, [P, NODE_TILES * (GW + GH)]) for n in ("h_all", "gs_all"))
                k.dst_term, k.gm_all = (sbi(n, [P, NODE_TILES * GH]) for n in ("dst_term", "gm_all"))
                k.t2_all = sbi("t2_all", [P, NODE_TILES * 2 * GH])
                k.g_all = sbi("g_all", [P, GAT.tiles * (GW + GH)])
                route_inputs(nc, k)
                route_maxima(nc, k, T)
                route_sums(nc, k, T)
                route_gates(nc, k)
            experts(nc, k)
            cut_output(nc, k)


def node_types(nc, k):
    with Phase(nc, "types") as f:
        types_i, types = f.sb("types_i", [P, NODE_TILES], I32), f.sb("types", [P, NODE_TILES])
        zeroed, loaded = f.dma_sem("zeroed"), f.dma_sem("loaded")
        f.start()
        with nc.Block() as block:
            @block.sync
            def _(sp):
                sp.wait_ge(zeroed, 1)
                with nc.allow_non_contiguous_dma(reason="6250 words"):
                    sp.dma_start(types_i[:, 0:BUCKETS - 1], k.node_type[0:(BUCKETS - 1) * P].rearrange("(i p) -> p i", p=P)).then_inc(loaded, 16)
                    sp.dma_start(types_i[0:LAST, BUCKETS - 1:BUCKETS], k.node_type[(BUCKETS - 1) * P:N].rearrange("(p i) -> p i", i=1)).then_inc(loaded, 16)

            @block.vector
            def _(dve):
                nc.vector.memset(types_i[:], 0)
                dve.drain().then_inc(zeroed, 1)
                dve.wait_ge(loaded, 32)
                nc.vector.tensor_copy(types[:], types_i[:])
                dve.drain()
                for t in range(NODE_TYPES):
                    nc.vector.tensor_single_scalar(k.type_mask[:].rearrange("p (i t) -> p i t", t=NODE_TYPES)[:, :, t], types[:], float(t), op=ALU.is_equal)


def cut_output(nc, k):
    with Phase(nc, "cut") as f:
        written = f.dma_sem("written")
        f.start()
        with nc.Block() as block:
            @block.sync
            def _(sp):
                sp.dma_start(k.out, k.XO[0:N, :]).then_inc(written, 16)
                sp.wait_ge(written, 16)


_INS = {"x": "x", "src": "src", "dst": "dst", "edge_type_3": "edge_type", "node_type_4": "node_type",
        "L0_gnn_W_Q": "W_Q", "L0_gnn_W_K": "W_K", "L0_gnn_W_V": "W_V", "L0_gnn_W_E": "W_E", "L0_gnn_mu": "mu",
        "L0_gnn_Wo": "Wo", "L0_gnn_bo": "bo", "L0_gnn_ln1_g": "ln1_g", "L0_gnn_ln1_b": "ln1_b",
        "L0_gnn_ln2_g": "ln2_g", "L0_gnn_ln2_b": "ln2_b", "L0_gnn_w1": "w1", "L0_gnn_b1": "b1",
        "L0_gnn_w2": "w2", "L0_gnn_b2": "b2", "L0_gnn_out_g": "out_g", "L0_gnn_out_b": "out_b",
        "L0_ffn_W_gat": "W_gat", "L0_ffn_att_src": "att_src", "L0_ffn_att_dst": "att_dst", "L0_ffn_b_gat": "b_gat",
        "L0_ffn_ln_gamma": "ln_gamma", "L0_ffn_ln_beta": "ln_beta", "L0_ffn_W1": "W1", "L0_ffn_b1": "mb1",
        "L0_ffn_W2": "W2", "L0_ffn_b2": "mb2"}


def kernel(**inputs):
    import numpy as _np
    import concourse.bacc as _bacc
    from concourse.bass_utils import run_bass_kernel_spmd as _run

    nc = _bacc.Bacc("TRN2", target_bir_lowering=False, num_devices=1)
    arrays, aps = {}, {}

    def put(name, a):
        arrays[f"in_{name}"] = _np.ascontiguousarray(a)
        aps[name] = nc.dram_tensor(f"in_{name}", list(a.shape), mybir.dt.from_np(a.dtype), kind="ExternalInput").ap()

    for name, short in _INS.items():
        put(short, _np.asarray(inputs[name]))
    edges = _np.asarray(inputs["L0_ffn_edge_index"])
    put("edge_src", edges[0])
    put("edge_dst", edges[1])
    aps["out"] = nc.dram_tensor("out_x", [N, D], F32, kind="ExternalOutput").ap()
    program(nc, aps)
    r = _run(nc, [arrays], core_ids=[0])
    return r.results[0]["out_x"]
```

```python
from contextlib import ExitStack

import concourse.bass as bass
from concourse import mybir

F32 = mybir.dt.float32
I32 = mybir.dt.int32
U32 = mybir.dt.uint32
BF16 = mybir.dt.bfloat16
ALU = mybir.AluOpType
ACT = mybir.ActivationFunctionType
AX = mybir.AxisListType
ds = bass.ds

P = 128
D = 256
HEADS, HD = 8, 32
LAYERS, NODE_TYPES, EDGE_TYPES = 3, 4, 3
N = 6250
NODE_TILES = 52
NPAD = NODE_TILES * P
BUCKETS = 49
LAST = N - (BUCKETS - 1) * P
G = 8
GH, EXPERTS, GW = 4, 4, 16
MF = 512
DFF = 1024
AW = HEADS * (HD + 1)
KV = D + AW
NEG = -1.0e30
CREDIT = 2


class Space:
    pass


def edge_shape(edges, per_partition, group):
    tiles = (edges + (group * P - 1) * BUCKETS) // (group * P) * group
    tiles = -(-tiles // (2 * G)) * 2 * G
    e = Space()
    e.edges, e.per, e.tiles, e.group, e.groups = edges, per_partition, tiles, group, tiles // group
    e.steps, e.chunks = tiles // (2 * G), -(-tiles // P)
    return e


GNN = edge_shape(106250, 832, 4)
GAT = edge_shape(131072, 1024, 2)


class Phase:

    def __init__(self, nc, name, depth=2):
        self.depth = depth
        self.nc, self.name, self.ctx, self.sems, self.credited, self.per_step = nc, name, ExitStack(), [], [], {}

    def __enter__(self):
        self.ctx.__enter__()
        return self

    def __exit__(self, *a):
        return self.ctx.__exit__(*a)

    def sb(self, name, shape, dt=F32):
        return self.ctx.enter_context(self.nc.sbuf_tensor(f"{self.name}_{name}", shape, dt))

    def pair(self, name, shape, dt=F32):
        return [self.sb(f"{name}{g}", shape, dt) for g in range(2)]

    def ps(self, name, shape, dt=F32):
        return self.ctx.enter_context(self.nc.psum_tensor(f"{self.name}_{name}", shape, dt))

    def dma_sem(self, name):
        s = self.ctx.enter_context(self.nc.semaphore(f"{self.name}_{name}"))
        self.sems.append(s)
        return s

    def dma_pair(self, name):
        return [self.dma_sem(f"{name}{g}") for g in range(2)]

    def sem(self, name, per_step=1):
        s = self.dma_sem(name)
        self.credited.append((s, self.depth * per_step))
        self.per_step[s.name] = per_step
        return s

    def store_pair(self, name):
        pair = self.dma_pair(name)
        self.credited += [(s, 16) for s in pair]
        return pair

    def at(self, sem, step, event=None, back=0):
        per = self.per_step[sem.name]
        return step * per + ((self.depth - back) * per + (per if event is None else event + 1))

    def start(self):
        with self.nc.Block() as block:
            @block.gpsimd
            def _(pool):
                pool.dma_reset()
                for s in self.sems:
                    pool.sem_clear(s)
                for s, start in self.credited:
                    pool.sem_inc(s, start)


def constants(nc, k):
    k.ident = k.sb("ident", [P, P])
    k.iota_row = k.sb("iota_row", [P, P])
    k.iota_p = k.sb("iota_p", [P, 1])
    k.ones = k.sb("ones", [P, P])
    k.tri = k.sb("tri", [P, P])
    k.power = k.sb("power", [P, 1])
    with Phase(nc, "const") as f:
        made = f.dma_sem("made")
        copied = f.dma_sem("copied")
        ZR = 7
        zero = f.sb("zero", [(NPAD - N) // ZR, ZR * D])
        f.start()
        with nc.Block() as block:
            @block.gpsimd
            def _(pool):
                nc.gpsimd.memset(k.ident[:], 0.0)
                nc.gpsimd.memset(k.ones[:], 1.0)
                nc.gpsimd.memset(k.power[:], -0.5)
                nc.gpsimd.memset(k.tri[:], 1.0)
                nc.gpsimd.memset(zero[:], 0.0)
                nc.gpsimd.iota(k.iota_row[:], pattern=[[1, P]], base=0, channel_multiplier=0,
                               allow_small_or_imprecise_dtypes=True)
                nc.gpsimd.iota(k.iota_p[:], pattern=[[1, 1]], base=0, channel_multiplier=1,
                               allow_small_or_imprecise_dtypes=True)
                pool.drain()
                nc.gpsimd.affine_select(out=k.ident[:], in_=k.ident[:], compare_op=ALU.not_equal, fill=1.0,
                                        base=0, pattern=[[-1, P]], channel_multiplier=1)
                nc.gpsimd.affine_select(out=k.tri[:], in_=k.tri[:], compare_op=ALU.is_gt, fill=0.0,
                                        base=0, pattern=[[1, P]], channel_multiplier=-1)
                pool.drain()
                nc.gpsimd.memset(zero[:, 0:1], 0.0).then_inc(made, 1)

            @block.sync
            def _(sp):
                sp.wait_ge(made, 1)
                sp.dma_start(k.XP[0:N, :], k.x).then_inc(copied, 16)
                sp.dma_start(k.XP[N:NPAD, :].rearrange("(p r) c -> p (r c)", r=ZR), zero[:]).then_inc(copied, 16)
                sp.wait_ge(copied, 32)


def sort_edges(nc, k, name, e, src_in, dst_in, type_in, T):
    nc_, L, steps = nc, e.per, e.per // (2 * G)
    with Phase(nc, name) as f:
        pos = f.sb("pos", [P, L])
        pos_i = f.sb("pos_i", [P, L], I32)
        load = f.sb("load", [P, L, 4])
        hi = f.sb("hi", [P, L])
        ranked = f.dma_sem("ranked")
        counted = f.dma_sem("counted")
        filled = f.dma_sem("filled")
        numbered = f.dma_sem("numbered")
        mapped = f.dma_sem("mapped")
        loaded = f.dma_sem("loaded")
        with ExitStack() as tmp:
            def sb(n_, s, d=F32):
                return tmp.enter_context(nc.sbuf_tensor(f"{name}_{n_}", s, d))
            src_i, dst_i = sb("src_i", [P, L], I32), sb("dst_i", [P, L], I32)
            type_i = sb("type_i", [P, L], I32)
            work_i = sb("work_i", [P, L], I32)
            mask, cum = sb("mask", [P, L]), sb("cum", [P, L])
            fill = sb("fill", [P, e.tiles, 4])
            cnt, off, tiles, tend = (sb(x, [P, BUCKETS]) for x in ("cnt", "off", "tiles", "tend"))
            tiles_i = sb("tiles_i", [P, BUCKETS], I32)
            tile_no, owner = sb("tile_no", [P, e.chunks]), sb("owner", [P, e.chunks])
            owner_i = sb("owner_i", [P, e.chunks], I32)
            scrap = sb("scrap", [P, BUCKETS])
            sums = tmp.enter_context(nc.psum_tensor(f"{name}_sums", [P, 512], F32))
            f.start()
            full = e.edges // L
            rest = e.edges - full * L
            with nc.Block() as block:
                @block.gpsimd
                def _(pool):
                    nc.gpsimd.iota(tile_no[:], pattern=[[P, e.chunks]], base=0, channel_multiplier=1,
                                   allow_small_or_imprecise_dtypes=True).then_inc(numbered, 1)

                @block.sync
                def _(sp):
                    sp.wait_ge(filled, 1)
                    todo = [(dst_i, dst_in), (src_i, src_in)] + ([(type_i, type_in)] if type_in is not None else [])
                    for to, of in todo:
                        sp.dma_start(to[0:full, :], of[0:full * L].rearrange("(p l) -> p l", l=L)).then_inc(loaded, 16)
                        if rest:
                            sp.dma_start(to[full:full + 1, 0:rest],
                                         of[full * L:e.edges].rearrange("(p l) -> p l", p=1)).then_inc(loaded, 16)
                    sp.wait_ge(filled, 2)
                    sp.dma_start(T.edges.rearrange("(p r) c -> p (r c)", p=P), fill[:].rearrange("p r c -> p (r c)")).then_inc(mapped, 16)
                    sp.wait_ge(ranked, 1)
                    with nc.allow_non_contiguous_dma(reason="a few words"):
                        sp.dma_start(T.owner.rearrange("a (c p) -> (a p) c", p=P), owner_i[:]).then_inc(mapped, 16)
                    sp.wait_ge(mapped, 32)

                @block.tensor
                def _(pe):
                    pe.wait_ge(counted, 1)
                    nc.tensor.matmul(sums[:, 0:BUCKETS], k.tri[:], cnt[:], start=True, stop=True)
                    nc.tensor.matmul(sums[:, 64:64 + BUCKETS], k.ones[:], cnt[:], start=True, stop=True).then_inc(counted, 1)

                @block.vector
                def _(dve):
                    V = nc.vector
                    V.memset(dst_i[:], 1 << 20)
                    V.memset(src_i[:], 0)
                    V.memset(type_i[:], 0)
                    V.memset(pos[:], float(1 << 22))
                    V.memset(fill[:, :, 0], float(EDGE_TYPES * N))
                    V.memset(fill[:, :, 1], float(N))
                    V.memset(fill[:, :, 2:4], 999.0)
                    V.memset(load[:, :, 3], 0.0)
                    dve.drain()
                    V.memset(owner[:], 0.0).then_inc(filled, 1)
                    dve.drain()
                    V.memset(tiles[:], 0.0).then_inc(filled, 1)
                    n_in = (2 if type_in is None else 3) * (2 if rest else 1)
                    dve.wait_ge(loaded, 16 * n_in)
                    V.tensor_single_scalar(work_i[:], dst_i[:], 7, op=ALU.logical_shift_right)
                    dve.drain()
                    V.tensor_copy(hi[:], work_i[:])
                    dve.drain()
                    V.tensor_single_scalar(work_i[:], dst_i[:], P - 1, op=ALU.bitwise_and)
                    dve.drain()
                    V.tensor_copy(load[:, :, 2], work_i[:])
                    V.tensor_copy(mask[:], src_i[:])
                    dve.drain()
                    V.tensor_single_scalar(load[:, :, 1], mask[:], float(N - 1), op=ALU.min)
                    V.tensor_copy(cum[:], type_i[:])
                    dve.drain()
                    V.scalar_tensor_tensor(out=load[:, :, 0], in0=load[:, :, 1], scalar=float(EDGE_TYPES),
                                           in1=cum[:], op0=ALU.mult, op1=ALU.add)
                    dve.drain()
                    with dve.Fori(0, BUCKETS, 1) as b:
                        V.tensor_scalar(mask[:], hi[:], k.iota_row[:, ds(b, 1)], None, ALU.is_equal)
                        dve.drain()
                        V.tensor_tensor_scan(cum[:], k.ones[:, 0:1].to_broadcast([P, L]), mask[:], 0.0,
                                             ALU.mult, ALU.add)
                        dve.drain()
                        V.copy_predicated(pos[:], mask[:].bitcast(U32), cum[:])
                        V.tensor_copy(cnt[:, ds(b, 1)], cum[:, L - 1:L])
                        dve.drain()
                    V.memset(scrap[:, 0:1], 0.0).then_inc(counted, 1)
                    dve.wait_ge(counted, 2)
                    V.tensor_single_scalar(tiles[:], sums[:, 64:64 + BUCKETS], float(e.group * P - 1), op=ALU.add)
                    dve.drain()
                    V.tensor_copy(tiles_i[:], tiles[:])
                    dve.drain()
                    V.tensor_single_scalar(tiles_i[:], tiles_i[:], (e.group * P).bit_length() - 1, op=ALU.logical_shift_right)
                    dve.drain()
                    V.tensor_copy(tiles[:], tiles_i[:])
                    dve.drain()
                    V.tensor_tensor_scan(tend[:], k.ones[:, 0:1].to_broadcast([P, BUCKETS]), tiles[:], 0.0,
                                         ALU.mult, ALU.add)
                    dve.drain()
                    V.tensor_tensor(off[:], tend[:], tiles[:], ALU.subtract)
                    dve.drain()
                    V.scalar_tensor_tensor(out=off[:], in0=off[:], scalar=float(e.group * P), in1=sums[:, 0:BUCKETS],
                                           op0=ALU.mult, op1=ALU.add)
                    dve.drain()
                    V.tensor_single_scalar(off[:], off[:], -1.0, op=ALU.add)
                    dve.wait_ge(numbered, 1)
                    for c in range(e.chunks):
                        V.tensor_scalar(scrap[:], tend[:], tile_no[:, c:c + 1], None, ALU.is_le, ALU.add,
                                        accum_out=owner[:, c:c + 1])
                        dve.drain()
                    V.tensor_single_scalar(owner[:], owner[:], float(BUCKETS - 1), op=ALU.min)
                    dve.drain()
                    V.tensor_copy(owner_i[:], owner[:]).then_inc(ranked, 1)
                    dve.drain()
                    with dve.Fori(0, BUCKETS, 1) as b:
                        V.tensor_scalar(mask[:], hi[:], k.iota_row[:, ds(b, 1)], off[:, ds(b, 1)],
                                        ALU.is_equal, ALU.mult)
                        dve.drain()
                        V.tensor_tensor(pos[:], pos[:], mask[:], ALU.add)
                        dve.drain()
                    V.tensor_copy(pos_i[:], pos[:]).then_inc(ranked, 1)

        stage_pos, stage_rec = f.pair("stage_pos", [P, G], I32), f.pair("stage_rec", [P, G, 4])
        staged = [f.sem(f"staged{g}") for g in range(2)]
        issued = f.sem("issued")
        written = [f.dma_sem(f"written{g}") for g in range(2)]
        f.start()
        with nc.Block() as block:
            @block.vector
            def _(dve):
                V = nc.vector
                for g in range(2):
                    V.tensor_copy(stage_pos[g][:], pos_i[:, g * G:(g + 1) * G])
                    V.tensor_copy(stage_rec[g][:], load[:, g * G:(g + 1) * G, :]).then_inc(staged[g], 1)
                with dve.Fori(1, steps, 1) as i:
                    for g in range(2):
                        dve.wait_ge(written[g], i * (16 * G))
                        V.tensor_copy(stage_pos[g][:], pos_i[:, ds(i * 2 * G + g * G, G)])
                        dve.drain()
                        V.tensor_copy(stage_rec[g][:], load[:, ds(i * 2 * G + g * G, G), :]).then_inc(staged[g], 1)

            @block.gpsimd
            def _(pool):
                with pool.Fori(0, steps, 1) as i:
                    for g in range(2):
                        pool.wait_ge(staged[g], i + 1 + CREDIT)
                        pool.sem_inc(issued, 1)
                        for t in range(G):
                            pool.indirect_dma_start(
                                out=T.edges, out_offset=bass.IndirectOffsetOnAxis(ap=stage_pos[g][:, t:t + 1], axis=0),
                                in_=stage_rec[g][:, t, :], in_offset=None,
                                bounds_check=e.tiles * P - 1, oob_is_err=False).then_inc(written[g], 16)
                for g in range(2):
                    pool.wait_ge(written[g], 16 * G * steps)


def spread_edges(nc, k, name, e, T, gnn):
    with Phase(nc, name) as f:
        rec = f.pair("rec", [P, P, 4])
        rows = f.pair("rows", [P, P], BF16)
        last, reset = f.pair("last", [P, P]), f.pair("reset", [P, P])
        turned = [f.ps(f"turned{g}", [P, 4, P]) for g in range(2)]
        loaded, stored = f.dma_pair("loaded"), f.dma_pair("stored")
        flagged, transposed, taken = f.sem("flagged"), f.sem("transposed"), f.sem("taken")
        f.start()
        chunks = [(c, min(P, e.tiles - c * P)) for c in range(e.chunks)]
        with nc.Block() as block:
            @block.sync
            def _(sp):
                for c, n in chunks:
                    g = c % 2
                    if c >= 2:
                        sp.wait_ge(transposed, CREDIT + c - 1)
                        sp.wait_ge(flagged, CREDIT + c - 1)
                    sp.dma_start(rec[g][0:n, :, :].rearrange("p e c -> p (e c)"),
                                 T.edges[c * P * P:(c * P + n) * P, :].rearrange("(p e) c -> p (e c)", e=P)
                                 ).then_inc(loaded[g], 16)

            @block.vector
            def _(dve):
                V = nc.vector
                V.memset(T.idx_v[:, e.tiles:], 0)
                if gnn:
                    V.memset(T.idx_k[:, e.tiles:], 0)
                for c, n in chunks:
                    g = c % 2
                    dve.wait_ge(loaded[g], 16 * (c // 2 + 1))
                    if c >= 2:
                        dve.wait_ge(stored[g], (16 * (HEADS + 1) if gnn else 16) * (c // 2))
                        dve.wait_ge(transposed, CREDIT + c - 1)
                    rel = rec[g][0:n, :, 2]
                    if gnn:
                        V.memset(last[g][:, P - 1:P], 1.0)
                        V.memset(reset[g][:, 0:1], NEG)
                        V.tensor_tensor(last[g][0:n, 0:P - 1], rel[:, 0:P - 1], rel[:, 1:P], ALU.not_equal)
                        V.tensor_tensor(reset[g][0:n, 1:P], rel[:, 0:P - 1], rel[:, 1:P], ALU.not_equal)
                        dve.drain()
                        V.tensor_single_scalar(reset[g][0:n, 1:P], reset[g][0:n, 1:P], NEG, op=ALU.mult)
                        dve.drain()
                    V.tensor_copy(rows[g][0:n, :], rel).then_inc(flagged, 1)
                    dve.wait_ge(transposed, CREDIT + c + 1)
                    cols = slice(c * P, c * P + n)
                    V.tensor_copy(T.rel[:, cols], turned[g][:, 2, 0:n])
                    if gnn:
                        V.tensor_copy(T.idx_k[:, cols], turned[g][:, 0, 0:n])
                        V.tensor_copy(T.last[:, cols], turned[g][:, 3, 0:n])
                    V.tensor_copy(T.idx_v[:, cols], turned[g][:, 1, 0:n]).then_inc(taken, 1)

            @block.tensor
            def _(pe):
                for c, n in chunks:
                    g = c % 2
                    pe.wait_ge(flagged, CREDIT + c + 1)
                    if c >= 2:
                        pe.wait_ge(taken, CREDIT + c - 1)
                    for w in range(3):
                        last_op = nc.tensor.transpose(turned[g][:, w, 0:n], rec[g][0:n, :, w], k.ident[0:n, 0:n])
                    if gnn:
                        last_op = nc.tensor.transpose(turned[g][:, 3, 0:n], last[g][0:n, :], k.ident[0:n, 0:n])
                    last_op.then_inc(transposed, 1)

            @block.scalar
            def _(act):
                for c, n in chunks:
                    g = c % 2
                    act.wait_ge(flagged, CREDIT + c + 1)
                    act.dma_start(T.rows[c * P:c * P + n, :], rows[g][0:n, :]).then_inc(stored[g], 16)
                    if gnn:
                        for h in range(HEADS):
                            act.dma_start(T.resets[c * P:c * P + n, h, :], reset[g][0:n, :]).then_inc(stored[g], 16)
                for g in range(2):
                    act.wait_ge(stored[g], (16 * (HEADS + 1) if gnn else 16) * ((e.chunks + 1 - g) // 2))


class Step:

    def __init__(self, i, g, unroll, total):
        self.i, self.g, self.unroll, self.total = i, g, unroll, total

    def n(self, d=0):
        return self.i * self.unroll + (self.g + d)

    def slot(self, d=0):
        return (self.g + d) % self.unroll

    def turn(self, d=0):
        return self.i + (self.g + d) // self.unroll

    def real(self, d=0):
        return not isinstance(self.i, int) or 0 <= self.n(d) < self.total


def steps(eng, total, unroll, lead, lag, body):
    for g in range(-lead, unroll):
        body(Step(0, g, unroll, total))
    with eng.Fori(1, total // unroll - 1, 1) as i:
        for g in range(unroll):
            body(Step(i, g, unroll, total))
    for g in range(unroll + lag):
        body(Step(total // unroll - 1, g, unroll, total))


class Norm:

    def __init__(self, nc, k, f, name):
        self.nc, self.k = nc, k
        self.stats, self.mv, self.rstd = f.pair(name + "_stats", [P, 6]), f.pair(name + "_mv", [P, 2]), f.pair(name + "_rstd", [P, 1])
        self.measured, self.rooted = f.sem(name + "_measured"), f.sem(name + "_rooted")

    def moments(self, dve, g, x, eps=1e-5):
        nc = self.nc
        nc.vector.bn_stats(self.stats[g][:], x)
        dve.drain()
        nc.vector.bn_aggr(self.mv[g][:], self.stats[g][:])
        dve.drain()
        nc.vector.tensor_single_scalar(self.mv[g][:, 1:2], self.mv[g][:, 1:2], eps, op=ALU.add).then_inc(self.measured, 1)

    def root(self, pool, g, s):
        pool.wait_ge(self.measured, s + 1 + CREDIT)
        self.nc.gpsimd.tensor_tensor(self.rstd[g][:], self.mv[g][:, 1:2], self.k.power[:], ALU.pow).then_inc(self.rooted, 1)

    def apply(self, dve, g, s, out, x):
        dve.wait_ge(self.rooted, s + 1 + CREDIT)
        self.nc.vector.tensor_scalar(out, x, self.mv[g][:, 0:1], self.rstd[g][:], ALU.subtract, ALU.mult)


class PairNorm:

    def __init__(self, nc, k, f, name):
        self.nc, self.k, self.f = nc, k, f
        self.stats, self.mv, self.rstd = f.pair(name + "_stats", [P, 2, 6]), f.pair(name + "_mv", [P, 2, 2]), f.pair(name + "_rstd", [P, 2])
        self.measured, self.rooted = f.sem(name + "_measured"), f.sem(name + "_rooted")

    def moments(self, dve, r, x, eps=1e-5):
        V = self.nc.vector
        for g in range(2):
            V.bn_stats(self.stats[r][:, g, :], x[:, g, :])
        dve.drain()
        for g in range(2):
            V.bn_aggr(self.mv[r][:, g, :], self.stats[r][:, g, :])
        dve.drain()
        V.tensor_single_scalar(self.mv[r][:, :, 1], self.mv[r][:, :, 1], eps, op=ALU.add).then_inc(self.measured, 1)

    def root(self, pool, r, n):
        pool.wait_ge(self.measured, self.f.at(self.measured, n))
        self.nc.gpsimd.tensor_tensor(self.rstd[r][:], self.mv[r][:, :, 1], self.k.power[:].to_broadcast([P, 2]), ALU.pow).then_inc(self.rooted, 1)

    def apply(self, dve, r, n, out, x):
        dve.wait_ge(self.rooted, self.f.at(self.rooted, n))
        for g in range(2):
            self.nc.vector.tensor_scalar(out[:, g, :], x[:, g, :], self.mv[r][:, g, 0:1], self.rstd[r][:, g:g + 1], ALU.subtract, ALU.mult)


def rows_of(table, s, n=P):
    return table[ds(s * P, n), :]


def first_norm(nc, k):
    with Phase(nc, "first") as f:
        x, y = f.pair("x", [P, D]), f.pair("y", [P, D])
        norm = Norm(nc, k, f, "norm")
        loaded, stored, done = f.dma_pair("loaded"), f.store_pair("stored"), f.sem("done")
        f.start()
        with nc.Block() as block:
            @block.sync
            def _(sp):
                with sp.Fori(0, NODE_TILES // 2, 1) as i:
                    for g in range(2):
                        sp.wait_ge(done, i * 2 + g + 1)
                        sp.dma_start(x[g][:], rows_of(k.XP, i * 2 + g)).then_inc(loaded[g], 16)

            @block.gpsimd
            def _(pool):
                with pool.Fori(0, NODE_TILES // 2, 1) as i:
                    for g in range(2):
                        norm.root(pool, g, i * 2 + g)

            @block.vector
            def _(dve):
                with dve.Fori(0, NODE_TILES // 2, 1) as i:
                    for g in range(2):
                        dve.wait_ge(loaded[g], i * 16 + 16)
                        norm.moments(dve, g, x[g][:])
                    for g in range(2):
                        dve.wait_ge(stored[g], i * 16 + 16)
                        norm.apply(dve, g, i * 2 + g, y[g][:], x[g][:])
                        dve.drain().then_inc(done, 1)

            @block.scalar
            def _(act):
                with act.Fori(0, NODE_TILES // 2, 1) as i:
                    for g in range(2):
                        act.wait_ge(done, i * 2 + g + 1 + CREDIT)
                        act.dma_start(rows_of(k.X, i * 2 + g), y[g][:]).then_inc(stored[g], 16)
                for g in range(2):
                    act.wait_ge(stored[g], 16 * (NODE_TILES // 2) + 16)


def project(nc, k, l):
    QKV = 3 * HD
    with Phase(nc, "project") as f:
        wb = f.sb("wb", [P, HEADS, QKV])
        we = f.sb("we", [P, 2, EDGE_TYPES, P])
        mu = f.sb("mu", [P, HEADS, EDGE_TYPES])
        xt, xm, xmT = f.pair("xt", [P, D]), f.pair("xm", [P, HEADS, NODE_TYPES, HD]), f.pair("xmT", [P, HEADS, P])
        kk, kT, kp = f.pair("kk", [P, D]), f.pair("kT", [P, 2, P]), f.pair("kp", [P, EDGE_TYPES, KV])
        xT_ps = f.ps("xT_ps", [P, HEADS, P])
        qkv_ps = f.ps("qkv_ps", [P, 2, 512])
        kT_ps = f.ps("kT_ps", [P, 512])
        kp_ps = f.ps("kp_ps", [P, 2, 512])
        zeroed, weights = f.dma_sem("zeroed"), f.dma_sem("weights")
        loaded, stored = f.dma_pair("loaded"), f.store_pair("stored")
        masked, turned, copied, product = f.sem("masked"), f.sem("turned"), f.sem("copied"), f.sem("product")
        taken, k_turned, k_copied, k_product, k_scaled = (f.sem(x) for x in ("taken", "k_turned", "k_copied", "k_product", "k_scaled"))
        f.start()

        def heads(ps, q):
            return ps[:, :, 0:4 * QKV].rearrange("p a (h x) -> p a h x", x=QKV)[:, :, :, q * HD:(q + 1) * HD]

        with nc.Block() as block:
            @block.sync
            def _(sp):
                for t in range(NODE_TYPES):
                    for q, w in enumerate((k.W_Q, k.W_K, k.W_V)):
                        sp.dma_start(wb[t * HD:(t + 1) * HD, :, q * HD:(q + 1) * HD],
                                     w[ds(l, 1), t, :, :, :].rearrange("a h d e -> d (a h) e")).then_inc(weights, 16)
                sp.wait_ge(zeroed, 1)
                for half in range(2):
                    for h in range(4):
                        sp.dma_start(we[h * HD:(h + 1) * HD, half, :, h * HD:(h + 1) * HD],
                                     k.W_E[ds(l, 1), :, half * 4 + h, :, :].rearrange("a t d e -> d (a t) e")).then_inc(weights, 16)
                sp.dma_start(mu[:].rearrange("p h t -> p (h t)"),
                             k.mu[ds(l, 1), :, :].rearrange("a h t -> a (h t)").to_broadcast([P, HEADS * EDGE_TYPES])).then_inc(weights, 16)

                def body(st):
                    if st.real(2):
                        n, r = st.n(2), st.slot(2)
                        sp.wait_ge(masked, f.at(masked, n, back=2))
                        sp.dma_start(xt[r][:], rows_of(k.X, n)).then_inc(loaded[r], 16)
                    if st.real(-1):
                        n, r = st.n(-1), st.slot(-1)
                        sp.wait_ge(k_scaled, f.at(k_scaled, n))
                        sp.dma_start(k.KT[ds(n * P * EDGE_TYPES, P * EDGE_TYPES), :].rearrange("(p t) c -> p (t c)", t=EDGE_TYPES),
                                     kp[r][:].rearrange("p t c -> p (t c)")).then_inc(stored[r], 16)
                steps(sp, NODE_TILES, 2, 2, 1, body)
                for r in range(2):
                    sp.wait_ge(stored[r], 16 * (NODE_TILES // 2) + 16)

            @block.vector
            def _(dve):
                V = nc.vector
                V.memset(we[:], 0.0)
                for r in range(2):
                    V.memset(kp[r][:, :, D:KV], 1.0)
                dve.drain().then_inc(zeroed, 1)
                dve.wait_ge(weights, 16 * 21)
                V.tensor_single_scalar(mu[:], mu[:], float(HD) ** -0.5, op=ALU.mult)
                dve.drain()

                def body(st):
                    if st.real(1):
                        n, r = st.n(1), st.slot(1)
                        dve.wait_ge(loaded[r], st.turn(1) * 16 + 16)
                        dve.wait_ge(turned, f.at(turned, n, back=2))
                        for t in range(NODE_TYPES):
                            V.tensor_scalar(xm[r][:, :, t, :], xt[r][:].rearrange("p (h d) -> p h d", d=HD),
                                            k.type_mask[:, ds(n * NODE_TYPES + t, 1)], None, ALU.mult)
                        dve.drain().then_inc(masked, 1)
                    if st.real(-1):
                        n, r = st.n(-1), st.slot(-1)
                        dve.wait_ge(k_turned, f.at(k_turned, n))
                        dve.wait_ge(k_product, f.at(k_product, n, back=2))
                        V.tensor_copy(kT[r][:].rearrange("p a c -> p (a c)"), kT_ps[:, 0:2 * P]).then_inc(k_copied, 1)
                        V.tensor_copy(kp[r][:, 1:EDGE_TYPES, D:KV], kp[r][:, 0, D:KV].unsqueeze(1).to_broadcast([P, EDGE_TYPES - 1, AW]))
                        dve.wait_ge(k_product, f.at(k_product, n))
                        for half in range(2):
                            V.tensor_tensor(kp[r][:, :, half * P:(half + 1) * P].rearrange("p t (h e) -> p t h e", e=HD),
                                            kp_ps[:, half, 0:EDGE_TYPES * P].rearrange("p (t h e) -> p t h e", t=EDGE_TYPES, e=HD),
                                            mu[:, half * 4:(half + 1) * 4, :].rearrange("p h t -> p t h").unsqueeze(3)
                                            .to_broadcast([P, EDGE_TYPES, 4, HD]), ALU.mult)
                        dve.drain().then_inc(k_scaled, 1)
                steps(dve, NODE_TILES, 2, 1, 1, body)

            @block.tensor
            def _(pe):
                T = nc.tensor
                pe.wait_ge(weights, 16 * 21)

                def body(st):
                    if st.real(-1):
                        n, r = st.n(-1), st.slot(-1)
                        pe.wait_ge(taken, f.at(taken, n))
                        pe.wait_ge(k_copied, f.at(k_copied, n, back=1))
                        for half in range(2):
                            op = T.transpose(kT_ps[:, half * P:(half + 1) * P], kk[r][:, half * P:(half + 1) * P], k.ident[:])
                        op.then_inc(k_turned, 1)
                    if st.real(1):
                        n, r = st.n(1), st.slot(1)
                        pe.wait_ge(masked, f.at(masked, n))
                        pe.wait_ge(copied, f.at(copied, n, back=1))
                        for h in range(HEADS):
                            op = T.transpose(xT_ps[:, h, :], xm[r][:, h, :, :].rearrange("p t d -> p (t d)"), k.ident[:])
                        op.then_inc(turned, 1)
                    if st.real(-1):
                        n, r = st.n(-1), st.slot(-1)
                        pe.wait_ge(k_copied, f.at(k_copied, n))
                        pe.wait_ge(k_scaled, f.at(k_scaled, n, back=1))
                        for half in range(2):
                            op = T.matmul(kp_ps[:, half, 0:EDGE_TYPES * P], kT[r][:, half, :],
                                          we[:, half, :, :].rearrange("p t c -> p (t c)"), start=True, stop=True)
                        op.then_inc(k_product, 1)
                    if st.real(1):
                        n, r = st.n(1), st.slot(1)
                        pe.wait_ge(copied, f.at(copied, n))
                        pe.wait_ge(taken, f.at(taken, n, back=1))
                        for h in range(HEADS):
                            op = T.matmul(qkv_ps[:, h // 4, (h % 4) * QKV:(h % 4 + 1) * QKV], xmT[r][:, h, :], wb[:, h, :], start=True, stop=True)
                        op.then_inc(product, 1)
                steps(pe, NODE_TILES, 2, 1, 1, body)

            @block.scalar
            def _(act):
                A = nc.scalar
                act.wait_ge(zeroed, 1)

                def body(st):
                    if st.real(1):
                        n, r = st.n(1), st.slot(1)
                        act.wait_ge(turned, f.at(turned, n))
                        act.wait_ge(product, f.at(product, n, back=2))
                        A.copy(xmT[r][:, 0:4, :], xT_ps[:, 0:4, :])
                        A.copy(xmT[r][:, 4:8, :], xT_ps[:, 4:8, :])
                        act.drain().then_inc(copied, 1)
                        act.wait_ge(product, f.at(product, n))
                        act.wait_ge(k_turned, f.at(k_turned, n, back=2))
                        A.copy(kk[r][:].rearrange("p (a h d) -> p a h d", a=2, d=HD), heads(qkv_ps, 1))
                        A.copy(k.q_all[:, ds(n * D, D)].rearrange("p (a h d) -> p a h d", a=2, d=HD), heads(qkv_ps, 0))
                        act.wait_ge(stored[r], st.turn(1) * 16 + 16)
                        A.copy(kp[r][:, 0, D:KV].rearrange("p (a h d) -> p a h d", a=2, d=HD + 1)[:, :, :, 0:HD], heads(qkv_ps, 2))
                        act.drain().then_inc(taken, 1)
                steps(act, NODE_TILES, 2, 1, 0, body)


def load_owners(eng, owner, s, regs):
    eng.load(regs, owner[0:1, ds(s * (G // 2), G // 2)])


def one_hots(nc, k, dve, T, s, g, dst_rows, to_node, to_edge):
    nc.vector.tensor_scalar(to_edge[g][:], dst_rows[g][:], k.iota_p[:], None, ALU.is_equal)
    nc.vector.tensor_tensor(to_node[g][:], T.rel[:, ds(s * G, G)].unsqueeze(2).to_broadcast([P, G, P]),
                            k.iota_row[:].unsqueeze(1).to_broadcast([P, G, P]), ALU.is_equal)


def attend(nc, k, T):
    e, R = GNN, 4
    B = e.group
    ROWS = B * HEADS
    with Phase(nc, "attend", R) as f:
        def ring(name, shape, dt=F32, n=R):
            return [f.sb(f"{name}{r}", shape, dt) for r in range(n)]

        stage, dst_rows, resets = ring("stage", [P, B], I32), ring("dst_rows", [P, B * P], BF16), ring("resets", [ROWS, P])
        kv = ring("kv", [P, B, KV])
        qs = ring("qs", [P, D])
        to_edge, to_node = ring("to_edge", [P, B * P]), ring("to_node", [P, B, P])
        sg, run, tops = ring("sg", [P, B, HEADS]), ring("run", [ROWS, P]), ring("tops", [P, B, HEADS + 1])
        absent, mv, gm = ring("absent", [P, B]), ring("mv", [P, B, HEADS]), ring("gm", [P, HEADS])
        mn, drop, shift, ws = ring("mn", [P, HEADS]), ring("drop", [P, HEADS]), ring("shift", [P, B, HEADS]), ring("ws", [P, B, HEADS])
        scaled_down = ring("scaled_down", [P, HEADS, HD + 1], n=2)
        q_ps = f.ps("q_ps", [P, 2, 2, D])
        hot_ps, sT_ps, run_ps, top_ps, m_ps, sum_ps = (f.ps(n, [P, 512]) for n in ("hot_ps", "sT_ps", "run_ps", "top_ps", "m_ps", "sum_ps"))
        gathered, rows_in, resets_in, staged = ([f.dma_sem(f"{n}{r}") for r in range(R)] for n in ("gathered", "rows_in", "resets_in", "staged"))
        go, turns, fell = f.sem("go"), f.sem("turns"), f.sem("fell")
        cleared = f.dma_sem("cleared")
        q_taken, hot, hot_turned, hot_copied, scored, s_turned, ran, r_turned, topped = (
            f.sem(n) for n in ("q_taken", "hot", "hot_turned", "hot_copied", "scored", "s_turned", "ran", "r_turned", "topped"))
        at_nodes, merged, dropped, brought, shifted, weighed, scaled, summed, added = (
            f.sem(n) for n in ("at_nodes", "merged", "dropped", "brought", "shifted", "weighed", "scaled", "summed", "added"))
        queried, multiplied = f.sem("queried", 2), f.sem("multiplied", 2)
        f.start()
        with nc.Block() as block:
            @block.sync
            def _(sp):
                def body(st):
                    s, r = st.n(), st.slot()
                    sp.wait_ge(hot, f.at(hot, s, back=R))
                    sp.dma_start(dst_rows[r][:], T.rows[ds(s * B, B), :].rearrange("(a t) e -> a (t e)", a=1)
                                 .to_broadcast([P, B * P])).then_inc(rows_in[r], 16)
                    sp.wait_ge(scored, f.at(scored, s, back=R))
                    sp.dma_start(stage[r][:], T.idx_k[:, ds(s * B, B)]).then_inc(staged[r], 16)
                    sp.wait_ge(ran, f.at(ran, s, back=R))
                    sp.dma_start(resets[r][:], T.resets[ds(s * B, B), :, :].rearrange("t h e -> (t h) e")).then_inc(resets_in[r], 16)
                steps(sp, e.groups, R, 0, 0, body)

            @block.gpsimd
            def _(pool):
                pool.wait_ge(cleared, 1)

                def body(st):
                    s, r = st.n(), st.slot()
                    pool.wait_ge(staged[r], st.turn() * 16 + 16)
                    pool.sem_inc(go, 1)
                    pool.wait_ge(summed, f.at(summed, s, back=R))
                    pool.sem_inc(go, 1)
                    for t in range(B):
                        pool.indirect_dma_start(out=kv[r][:, t, :], out_offset=None, in_=k.KT,
                                                in_offset=bass.IndirectOffsetOnAxis(ap=stage[r][:, t:t + 1], axis=0),
                                                bounds_check=N * EDGE_TYPES - 1, oob_is_err=False).then_inc(gathered[r], 16)
                steps(pool, e.groups, R, 0, 0, body)

            @block.vector
            def _(dve):
                V = nc.vector
                for r in range(R):
                    V.memset(kv[r][:], 0.0)
                V.memset(k.a_all[:], 0.0)
                V.memset(k.m_all[:], -1e9)
                dve.drain().then_inc(cleared, 1)
                regs = [dve.alloc_register(f"attend_owner{r}") for r in range(R)]

                def owner_of(r):
                    return dve.snap(regs[r], min_val=0, max_val=BUCKETS - 1)

                def sums_of(r):
                    return k.a_all[:, ds(owner_of(r) * AW, AW)].rearrange("p (h e) -> p h e", e=HD + 1)

                def body(st):
                    if st.real():
                        dve.load([regs[st.slot()]], T.owner[0:1, ds(st.n(), 1)])
                    if st.real():
                        n, r = st.n(), st.slot()
                        dve.wait_ge(gathered[r], st.turn() * (16 * B) + 16 * B)
                        for j in range(2):
                            dve.wait_ge(queried, f.at(queried, n, j))
                            V.tensor_tensor(kv[r][:, 2 * j:2 * j + 2, 0:D], q_ps[:, j, :, :], kv[r][:, 2 * j:2 * j + 2, 0:D], ALU.mult).then_inc(multiplied, 1)
                    if st.real(-3):
                        r = st.slot(-3)
                        dve.wait_ge(dropped, f.at(dropped, st.n(-3)))
                        V.tensor_tensor(scaled_down[r % 2][:], sums_of(r), drop[r][:].unsqueeze(2).to_broadcast([P, HEADS, HD + 1]), ALU.mult)
                    if st.real(-1):
                        n, r = st.n(-1), st.slot(-1)
                        dve.wait_ge(r_turned, f.at(r_turned, n))
                        V.tensor_tensor(tops[r][:, :, 0:HEADS], run_ps[:, 0:ROWS].rearrange("p (t h) -> p t h", h=HEADS),
                                        T.last[:, ds(n * B, B)].unsqueeze(2).to_broadcast([P, B, HEADS]), ALU.mult)
                        V.tensor_copy(tops[r][:, :, HEADS], T.last[:, ds(n * B, B)])
                        dve.drain().then_inc(topped, 1)
                    else:
                        dve.drain()
                    if st.real(-2):
                        n, r = st.n(-2), st.slot(-2)
                        dve.wait_ge(brought, f.at(brought, n))
                        V.tensor_tensor(shift[r][:].rearrange("p t h -> p (t h)"), sg[r][:].rearrange("p t h -> p (t h)"),
                                        m_ps[:, 0:ROWS], ALU.subtract).then_inc(shifted, 1)
                        V.tensor_copy(k.m_all[:, ds(owner_of(r) * HEADS, HEADS)], mn[r][:])
                    if st.real():
                        r = st.slot()
                        V.tensor_reduce(sg[r][:].rearrange("p t h -> p (t h)"), kv[r][:, :, 0:D].rearrange("p t (h e) -> p t h e", e=HD),
                                        AX.X, ALU.add).then_inc(scored, 1)
                    if st.real(-3):
                        n, r = st.n(-3), st.slot(-3)
                        dve.wait_ge(summed, f.at(summed, n))
                        V.tensor_tensor(sums_of(r), scaled_down[r % 2][:], sum_ps[:, 0:AW].rearrange("p (h e) -> p h e", e=HD + 1), ALU.add).then_inc(added, 1)
                    at = top_ps[:, 0:B * (HEADS + 1)].rearrange("p (t h) -> p t h", h=HEADS + 1)
                    if st.real(-1):
                        n, r = st.n(-1), st.slot(-1)
                        dve.wait_ge(at_nodes, f.at(at_nodes, n))
                        V.tensor_scalar(absent[r][:], at[:, :, HEADS], -1.0, 0.0, ALU.add, ALU.min)
                    dve.drain()
                    if st.real(-1):
                        r = st.slot(-1)
                        V.scalar_tensor_tensor(out=mv[r][:], in0=absent[r][:].unsqueeze(2).to_broadcast([P, B, HEADS]), scalar=-NEG,
                                               in1=at[:, :, 0:HEADS], op0=ALU.mult, op1=ALU.add)
                        dve.drain()
                        V.tensor_reduce(gm[r][:], mv[r][:].rearrange("p t h -> p h t"), AX.X, ALU.max)
                    if st.real(-2):
                        n, r = st.n(-2), st.slot(-2)
                        dve.wait_ge(weighed, f.at(weighed, n))
                        v = kv[r][:, :, D:KV].rearrange("p t (h e) -> p t h e", e=HD + 1)
                        V.tensor_tensor(v, v, ws[r][:].unsqueeze(3).to_broadcast([P, B, HEADS, HD + 1]), ALU.mult).then_inc(scaled, 1)
                    if st.real(-1):
                        r = st.slot(-1)
                        m = k.m_all[:, ds(owner_of(r) * HEADS, HEADS)]
                        dve.drain()
                        V.tensor_tensor(mn[r][:], m, gm[r][:], ALU.max).then_inc(merged, 1)
                        dve.drain()
                        V.tensor_tensor(drop[r][:], m, mn[r][:], ALU.subtract).then_inc(fell, 1)
                    if st.real():
                        n, r = st.n(), st.slot()
                        dve.wait_ge(s_turned, f.at(s_turned, n))
                        dve.wait_ge(resets_in[r], st.turn() * 16 + 16)
                        V.tensor_tensor_scan(run[r][:], resets[r][:], sT_ps[0:ROWS, 0:P], NEG, ALU.add, ALU.max).then_inc(ran, 1)
                    if st.real(2):
                        n, r = st.n(2), st.slot(2)
                        dve.wait_ge(rows_in[r], st.turn(2) * 16 + 16)
                        dve.wait_ge(brought, f.at(brought, n, back=R))
                        V.tensor_scalar(to_edge[r][:], dst_rows[r][:], k.iota_p[:], None, ALU.is_equal).then_inc(hot, 1)
                steps(dve, e.groups, R, 2, 3, body)

            @block.scalar
            def _(act):
                A = nc.scalar
                reg = act.alloc_register("attend_q_owner")

                def body(st):
                    if st.real(-2):
                        n, r = st.n(-2), st.slot(-2)
                        act.wait_ge(shifted, f.at(shifted, n))
                        act.wait_ge(scaled, f.at(scaled, n, back=R))
                        A.activation(ws[r][:], shift[r][:], ACT.Exp).then_inc(weighed, 1)
                    if st.real(2):
                        n, r = st.n(2), st.slot(2)
                        act.load([reg], T.owner[0:1, ds(n, 1)])
                        owner = act.snap(reg, min_val=0, max_val=BUCKETS - 1)
                        act.wait_ge(queried, f.at(queried, n, back=R))
                        A.copy(qs[r][:], k.q_all[:, ds(owner * D, D)]).then_inc(q_taken, 1)
                    if st.real(1):
                        n, r = st.n(1), st.slot(1)
                        act.wait_ge(hot_turned, f.at(hot_turned, n))
                        act.wait_ge(summed, f.at(summed, n, back=R))
                        A.copy(to_node[r][:].rearrange("p t n -> p (t n)"), hot_ps[:]).then_inc(hot_copied, 1)
                    if st.real(-1):
                        n, r = st.n(-1), st.slot(-1)
                        act.wait_ge(fell, f.at(fell, n))
                        A.activation(drop[r][:], drop[r][:], ACT.Exp).then_inc(dropped, 1)
                steps(act, e.groups, R, 2, 2, body)

            @block.tensor
            def _(pe):
                T_ = nc.tensor

                def bring_q(n, r, j):
                    pe.wait_ge(multiplied, f.at(multiplied, n, j, back=1))
                    for t in (2 * j, 2 * j + 1):
                        op = T_.matmul(q_ps[:, j, t % 2, :], to_edge[r][:, t * P:(t + 1) * P], qs[r][:], start=True, stop=True)
                    op.then_inc(queried, 1)

                def body(st):
                    if st.real(-1):
                        n, r = st.n(-1), st.slot(-1)
                        pe.wait_ge(topped, f.at(topped, n))
                        pe.wait_ge(fell, f.at(fell, n, back=1))
                        for t in range(B):
                            op = T_.matmul(top_ps[:, t * (HEADS + 1):(t + 1) * (HEADS + 1)], to_node[r][:, t, :], tops[r][:, t, :],
                                           start=True, stop=True)
                        op.then_inc(at_nodes, 1)
                    if st.real(1):
                        n, r = st.n(1), st.slot(1)
                        pe.wait_ge(hot, f.at(hot, n))
                        pe.wait_ge(q_taken, f.at(q_taken, n))
                        bring_q(n, r, 0)
                        bring_q(n, r, 1)
                    if st.real():
                        n, r = st.n(), st.slot()
                        pe.wait_ge(scored, f.at(scored, n))
                        pe.wait_ge(ran, f.at(ran, n, back=1))
                        pe.sem_inc(turns, 1)
                        T_.transpose(sT_ps[0:ROWS, 0:P], sg[r][:].rearrange("p t h -> p (t h)"), k.ident[:]).then_inc(s_turned, 1)
                    if st.real(1):
                        n, r = st.n(1), st.slot(1)
                        pe.wait_ge(hot_copied, f.at(hot_copied, n, back=1))
                        for t in range(B):
                            op = T_.transpose(hot_ps[:, t * P:(t + 1) * P], to_edge[r][:, t * P:(t + 1) * P], k.ident[:])
                        op.then_inc(hot_turned, 1)
                    if st.real(-1):
                        n, r = st.n(-1), st.slot(-1)
                        pe.wait_ge(merged, f.at(merged, n))
                        pe.wait_ge(shifted, f.at(shifted, n, back=1))
                        for t in range(B):
                            op = T_.matmul(m_ps[:, t * HEADS:(t + 1) * HEADS], to_edge[r][:, t * P:(t + 1) * P], mn[r][:], start=True, stop=True)
                        op.then_inc(brought, 1)
                    if st.real():
                        n, r = st.n(), st.slot()
                        pe.wait_ge(ran, f.at(ran, n))
                        pe.wait_ge(topped, f.at(topped, n, back=1))
                        pe.sem_inc(turns, 1)
                        T_.transpose(run_ps[:, 0:ROWS], run[r][:], k.ident[0:ROWS, 0:ROWS]).then_inc(r_turned, 1)
                    if st.real(-2):
                        n, r = st.n(-2), st.slot(-2)
                        pe.wait_ge(scaled, f.at(scaled, n))
                        pe.wait_ge(added, f.at(added, n, back=1))
                        for t in range(B):
                            op = T_.matmul(sum_ps[:, 0:AW], to_node[r][:, t, :], kv[r][:, t, D:KV], start=(t == 0), stop=(t == B - 1))
                        op.then_inc(summed, 1)
                steps(pe, e.groups, R, 1, 2, body)


def row_of(w, l):
    return w[ds(l, 1), :].to_broadcast([P, w.shape[1]])


def finish_layer(nc, k, l):
    FC = DFF // P
    PAIRS = NODE_TILES // 2
    with Phase(nc, "finish") as f:
        wo, w1, w2 = f.sb("wo", [P, 2, D]), f.sb("w1", [P, 2, DFF]), f.sb("w2", [P, FC, D])
        b1 = f.sb("b1", [P, FC])
        rows = {n: f.sb(n, [P, 2, D]) for n in ("bo", "g1", "s1", "b2", "g2", "s2")}
        den, at = f.pair("den", [P, 2, HEADS]), f.pair("at", [P, 2, D])
        aT = f.pair("aT", [P, 2, 2, P])
        xt, y, x1, y2, z = (f.pair(n, [P, 2, D]) for n in ("xt", "y", "x1", "y2", "z"))
        x1T, hT = f.pair("x1T", [P, 2, 2, P]), f.sb("hT", [P, FC, 2 * P])
        norm1, norm2 = PairNorm(nc, k, f, "norm1"), PairNorm(nc, k, f, "norm2")
        turn_ps = f.ps("turn_ps", [P, 2, 2, D])
        aT_ps = turn_ps[:, :, 0, :].rearrange("p g (c n) -> p g c n", n=P)
        o_ps = turn_ps[:, :, 1, :]
        h_ps = f.ps("h_ps", [P, FC, 2 * P])
        y_ps = f.ps("y_ps", [P, 2, 512])
        weights, loaded, stored = f.dma_sem("weights"), f.dma_pair("loaded"), f.store_pair("stored")
        divided, a_turned, a_copied, projected, attended = (
            f.sem(x) for x in ("divided", "a_turned", "a_copied", "projected", "attended"))
        x_ready, x_turned, x_copied, contracted, finished, read = (
            f.sem(x) for x in ("x_ready", "x_turned", "x_copied", "contracted", "finished", "read"))
        hidden, activated = f.sem("hidden", FC // 2), f.sem("activated", FC // 2)
        f.start()
        with nc.Block() as block:
            @block.sync
            def _(sp):
                one = ds(l, 1)
                for to, of in ((wo[:], k.Wo[one, :, :].rearrange("a (c p) n -> p (a c) n", p=P)),
                               (w1[:], k.w1[one, :, :].rearrange("a (c p) n -> p (a c) n", p=P)),
                               (w2[:], k.w2[one, :, :].rearrange("a (c p) n -> p (a c) n", p=P))):
                    sp.dma_start(to, of).then_inc(weights, 16)
                with nc.allow_non_contiguous_dma(reason="1024 words"):
                    sp.dma_start(b1[:], k.b1[one, :].rearrange("a (c p) -> p (a c)", p=P)).then_inc(weights, 16)
                for n, w in (("bo", k.bo), ("g1", k.ln1_g), ("s1", k.ln1_b), ("b2", k.b2), ("g2", k.ln2_g), ("s2", k.ln2_b)):
                    for g in range(2):
                        sp.dma_start(rows[n][:, g, :], row_of(w, l)).then_inc(weights, 16)

                def body(st):
                    n, r = st.n(), st.slot()
                    sp.wait_ge(attended, f.at(attended, n, back=2))
                    sp.dma_start(xt[r][:], k.X[ds(n * 2 * P, 2 * P), :].rearrange("(g p) c -> p g c", p=P)).then_inc(loaded[r], 16)
                steps(sp, PAIRS, 2, 0, 0, body)

            @block.gpsimd
            def _(pool):
                def body(st):
                    if st.real(1):
                        norm1.root(pool, st.slot(1), st.n(1))
                    if st.real():
                        norm2.root(pool, st.slot(), st.n())
                steps(pool, PAIRS, 2, 1, 0, body)

            @block.vector
            def _(dve):
                V = nc.vector
                dve.wait_ge(weights, 16 * 16)

                def body(st):
                    if st.real(1):
                        n, r = st.n(1), st.slot(1)
                        sums = k.a_all[:, ds(n * 2 * AW, 2 * AW)].rearrange("p (x e) -> p x e", e=HD + 1)
                        V.tensor_single_scalar(den[r][:].rearrange("p g h -> p (g h)"), sums[:, :, HD], 1e-10, op=ALU.add)
                        dve.drain()
                        V.reciprocal(den[r][:], den[r][:])
                        dve.drain()
                        dve.wait_ge(a_turned, f.at(a_turned, n, back=2))
                        V.tensor_tensor(at[r][:].rearrange("p g (h e) -> p (g h) e", e=HD), sums[:, :, 0:HD],
                                        den[r][:].rearrange("p g h -> p (g h)").unsqueeze(2).to_broadcast([P, 2 * HEADS, HD]), ALU.mult).then_inc(divided, 1)
                        dve.wait_ge(loaded[r], st.turn(1) * 16 + 16)
                        V.tensor_tensor(xt[r][:], xt[r][:], rows["bo"][:], ALU.add)
                        dve.drain()
                        dve.wait_ge(projected, f.at(projected, n))
                        V.tensor_tensor(y[r][:], o_ps, xt[r][:], ALU.add).then_inc(attended, 1)
                        dve.drain()
                        norm1.moments(dve, r, y[r])
                        norm1.apply(dve, r, n, x1[r], y[r])
                        dve.drain()
                        V.tensor_tensor(x1[r][:], x1[r][:], rows["g1"][:], ALU.mult)
                        dve.drain()
                        V.tensor_tensor(x1[r][:], x1[r][:], rows["s1"][:], ALU.add).then_inc(x_ready, 1)
                        dve.drain()
                        V.tensor_tensor(y2[r][:], x1[r][:], rows["b2"][:], ALU.add)
                        dve.drain()
                    if st.real():
                        n, r = st.n(), st.slot()
                        dve.wait_ge(contracted, f.at(contracted, n))
                        V.tensor_tensor(y2[r][:], y_ps[:, :, 0:D], y2[r][:], ALU.add).then_inc(read, 1)
                        dve.drain()
                        norm2.moments(dve, r, y2[r])
                        dve.wait_ge(stored[r], st.turn() * 16 + 16)
                        norm2.apply(dve, r, n, z[r], y2[r])
                        dve.drain()
                        V.tensor_tensor(z[r][:], z[r][:], rows["g2"][:], ALU.mult)
                        dve.drain()
                        V.tensor_tensor(z[r][:], z[r][:], rows["s2"][:], ALU.add).then_inc(finished, 1)
                steps(dve, PAIRS, 2, 1, 0, body)

            @block.tensor
            def _(pe):
                T = nc.tensor
                pe.wait_ge(weights, 16 * 16)

                def body(st):
                    if st.real():
                        n, r = st.n(), st.slot()
                        pe.wait_ge(x_copied, f.at(x_copied, n))
                        for c in range(FC):
                            if c % 2 == 0:
                                pe.wait_ge(activated, f.at(activated, n, c // 2, back=1))
                            for half in range(2):
                                op = T.matmul(h_ps[:, c, :], w1[:, half, c * P:(c + 1) * P], x1T[r][:, half, :, :].rearrange("p g n -> p (g n)"),
                                              start=(half == 0), stop=(half == 1))
                            if c % 2:
                                op.then_inc(hidden, 1)
                    if st.real(1):
                        n, r = st.n(1), st.slot(1)
                        pe.wait_ge(divided, f.at(divided, n))
                        pe.wait_ge(x_copied, f.at(x_copied, n, back=1))
                        for g in range(2):
                            for half in range(2):
                                op = T.transpose(aT_ps[:, g, half, :], at[r][:, g, half * P:(half + 1) * P], k.ident[:])
                        op.then_inc(a_turned, 1)
                        pe.wait_ge(a_copied, f.at(a_copied, n))
                        for g in range(2):
                            for half in range(2):
                                op = T.matmul(o_ps[:, g, :], aT[r][:, g, half, :], wo[:, half, :], start=(half == 0), stop=(half == 1))
                        op.then_inc(projected, 1)
                    if st.real():
                        n, r = st.n(), st.slot()
                        pe.wait_ge(read, f.at(read, n, back=1))
                        for g in range(2):
                            for c in range(FC):
                                if g == 0 and c % 2 == 0:
                                    pe.wait_ge(activated, f.at(activated, n, c // 2))
                                op = T.matmul(y_ps[:, g, 0:D], hT[:, c, g * P:(g + 1) * P], w2[:, c, :], start=(c == 0), stop=(c == FC - 1))
                        op.then_inc(contracted, 1)
                    if st.real(1):
                        n, r = st.n(1), st.slot(1)
                        pe.wait_ge(x_ready, f.at(x_ready, n))
                        for g in range(2):
                            for half in range(2):
                                op = T.transpose(aT_ps[:, g, half, :], x1[r][:, g, half * P:(half + 1) * P], k.ident[:])
                        op.then_inc(x_turned, 1)
                steps(pe, PAIRS, 2, 1, 0, body)

            @block.scalar
            def _(act):
                A = nc.scalar
                act.wait_ge(weights, 16 * 16)

                def body(st):
                    if st.real():
                        n = st.n()
                        act.wait_ge(contracted, f.at(contracted, n, back=1))
                        for c in range(FC):
                            if c % 2 == 0:
                                act.wait_ge(hidden, f.at(hidden, n, c // 2))
                            A.activation(hT[:, c, :], h_ps[:, c, :], ACT.Gelu, bias=b1[:, c:c + 1])
                            if c % 2:
                                act.drain().then_inc(activated, 1)
                    if st.real(1):
                        n, r = st.n(1), st.slot(1)
                        act.wait_ge(a_turned, f.at(a_turned, n))
                        act.wait_ge(projected, f.at(projected, n, back=2))
                        A.copy(aT[r][:], aT_ps).then_inc(a_copied, 1)
                    if st.real(1):
                        n, r = st.n(1), st.slot(1)
                        act.wait_ge(x_turned, f.at(x_turned, n))
                        act.wait_ge(hidden, f.at(hidden, n, back=2))
                        A.copy(x1T[r][:].rearrange("p a g n -> p g a n"), aT_ps).then_inc(x_copied, 1)
                    if st.real():
                        n, r = st.n(), st.slot()
                        act.wait_ge(finished, f.at(finished, n))
                        act.dma_start(k.X[ds(n * 2 * P, 2 * P), :].rearrange("(g p) c -> p g c", p=P), z[r][:]).then_inc(stored[r], 16)
                steps(act, PAIRS, 2, 1, 0, body)
                for r in range(2):
                    act.wait_ge(stored[r], 16 * (PAIRS // 2) + 16)


def route_inputs(nc, k):
    PAIRS = NODE_TILES // 2
    ROW = GW + GH
    with Phase(nc, "inputs") as f:
        wg = f.sb("wg", [P, 2, GW])
        att = f.sb("att", [P, 2, GW])
        og, ob = f.sb("og", [P, D]), f.sb("ob", [P, D])
        xt, x0, y, x2, xn = (f.pair(n, [P, D]) for n in ("xt", "x0", "y", "x2", "xn"))
        xT, tab, prod = f.pair("xT", [P, 2, P]), f.pair("tab", [P, ROW]), f.pair("prod", [P, 2, GW])
        norm1, norm2 = Norm(nc, k, f, "norm1"), Norm(nc, k, f, "norm2")
        xT_ps, h_ps = f.ps("xT_ps", [P, 2, 4, P]), f.ps("h_ps", [P, 2, 512])
        weights, loaded = f.dma_sem("weights"), f.dma_pair("loaded")
        stored = f.store_pair("stored")
        ready, normed, turned, copied, product, tabled = (f.sem(x) for x in ("ready", "normed", "turned", "copied", "product", "tabled"))
        f.start()
        with nc.Block() as block:
            @block.sync
            def _(sp):
                sp.dma_start(wg[:], k.W_gat.rearrange("(c p) n -> p c n", p=P)).then_inc(weights, 16)
                for n, w in enumerate((k.att_src, k.att_dst)):
                    sp.dma_start(att[:, n, :], w.rearrange("(a h) e -> a (h e)", a=1).to_broadcast([P, GW])).then_inc(weights, 16)
                sp.dma_start(og[:], k.out_g.rearrange("(a n) -> a n", a=1).to_broadcast([P, D])).then_inc(weights, 16)
                sp.dma_start(ob[:], k.out_b.rearrange("(a n) -> a n", a=1).to_broadcast([P, D])).then_inc(weights, 16)
                with sp.Fori(0, PAIRS, 1) as i:
                    for g in range(2):
                        s = i * 2 + g
                        sp.wait_ge(ready, s + 1)
                        sp.dma_start(xt[g][:], rows_of(k.X, s)).then_inc(loaded[g], 16)
                        sp.dma_start(x0[g][:], rows_of(k.XP, s)).then_inc(loaded[g], 16)

            @block.gpsimd
            def _(pool):
                with pool.Fori(0, PAIRS, 1) as i:
                    for norm in (norm1, norm2):
                        for g in range(2):
                            norm.root(pool, g, i * 2 + g)

            @block.vector
            def _(dve):
                V = nc.vector
                dve.wait_ge(weights, 16 * 5)
                with dve.Fori(0, PAIRS, 1) as i:
                    for g in range(2):
                        dve.wait_ge(loaded[g], i * 32 + 32)
                        norm1.moments(dve, g, xt[g][:])
                    for g in range(2):
                        norm1.apply(dve, g, i * 2 + g, y[g][:], xt[g][:])
                    dve.drain()
                    for g in range(2):
                        V.tensor_tensor(y[g][:], y[g][:], og[:], ALU.mult)
                    dve.drain()
                    for g in range(2):
                        V.tensor_tensor(y[g][:], y[g][:], ob[:], ALU.add)
                    dve.drain()
                    for g in range(2):
                        dve.wait_ge(stored[g], i * 48 + 16)
                        V.tensor_tensor(x2[g][:], y[g][:], x0[g][:], ALU.add).then_inc(ready, 1)
                    dve.drain()
                    for g in range(2):
                        norm2.moments(dve, g, x2[g][:])
                    for g in range(2):
                        norm2.apply(dve, g, i * 2 + g, xn[g][:], x2[g][:])
                        dve.drain().then_inc(normed, 1)
                    for g in range(2):
                        s = i * 2 + g
                        dve.wait_ge(product, s + 1 + CREDIT)
                        V.tensor_copy(tab[g][:, 0:GW], h_ps[:, g, 0:GW])
                    dve.drain()
                    for g in range(2):
                        V.tensor_tensor(prod[g][:], tab[g][:, 0:GW].unsqueeze(1).to_broadcast([P, 2, GW]), att[:], ALU.mult)
                    dve.drain()
                    for g in range(2):
                        s = i * 2 + g
                        pr = prod[g][:].rearrange("p a (h e) -> p a h e", e=EXPERTS)
                        V.tensor_reduce(tab[g][:, GW:ROW], pr[:, 0, :, :], AX.X, ALU.add)
                        V.tensor_reduce(k.dst_term[:, ds(s * GH, GH)], pr[:, 1, :, :], AX.X, ALU.add)
                    dve.drain()
                    for g in range(2):
                        s = i * 2 + g
                        V.tensor_copy(k.h_all[:, ds(s * ROW, ROW)], tab[g][:])
                    dve.drain().then_inc(tabled, 1)

            @block.tensor
            def _(pe):
                T = nc.tensor
                pe.wait_ge(weights, 16 * 5)
                with pe.Fori(0, PAIRS, 1) as i:
                    for g in range(2):
                        s = i * 2 + g
                        pe.wait_ge(normed, s + 1 + CREDIT)
                        pe.wait_ge(copied, s + 1)
                        for half in range(2):
                            op = T.transpose(xT_ps[:, g, half, :], xn[g][:, half * P:(half + 1) * P], k.ident[:])
                        op.then_inc(turned, 1)
                    for g in range(2):
                        s = i * 2 + g
                        pe.wait_ge(copied, s + 1 + CREDIT)
                        pe.wait_ge(tabled, i + CREDIT)
                        for half in range(2):
                            op = T.matmul(h_ps[:, g, 0:GW], xT[g][:, half, :], wg[:, half, :], start=(half == 0), stop=(half == 1))
                        op.then_inc(product, 1)

            @block.scalar
            def _(act):
                with act.Fori(0, PAIRS, 1) as i:
                    for g in range(2):
                        s = i * 2 + g
                        act.wait_ge(turned, s + 1 + CREDIT)
                        act.wait_ge(product, s + 1)
                        nc.scalar.copy(xT[g][:], xT_ps[:, g, 0:2, :]).then_inc(copied, 1)
                    act.wait_ge(tabled, i + 1 + CREDIT)
                    for g in range(2):
                        s = i * 2 + g
                        act.dma_start(rows_of(k.X2, s), x2[g][:]).then_inc(stored[g], 16)
                        act.dma_start(rows_of(k.XN, s), xn[g][:]).then_inc(stored[g], 16)
                        act.dma_start(rows_of(k.HT, s), tab[g][:]).then_inc(stored[g], 16)
                for g in range(2):
                    act.wait_ge(stored[g], 48 * PAIRS + 16)


def route_maxima(nc, k, T):
    e, ROW = GAT, GW + GH
    PAIRS = G // 2
    R = 4
    with Phase(nc, "maxima", R) as f:
        def ring(name, shape, dt=F32):
            return [f.sb(f"{name}{r}", shape, dt) for r in range(R)]

        stage = ring("stage", [P, G], I32)
        gb = ring("gb", [P, G, ROW])
        dst_rows, other = ring("dst_rows", [P, G * P], BF16), ring("other", [P, G, P], BF16)
        ident = f.sb("ident", [P, P], BF16)
        mt, mp = ring("mt", [P, PAIRS, 2, GH]), ring("mp", [P, PAIRS, GH])
        spread_ps = f.ps("spread_ps", [P, G, GH * P])
        staged, gathered, rows_in = ([f.dma_sem(f"{n}{r}") for r in range(R)] for n in ("staged", "gathered", "rows_in"))
        go = f.sem("go")
        compared, kept, ready = f.sem("compared"), f.sem("kept"), f.dma_sem("ready")
        spread, reduced = f.sem("spread", G), f.sem("reduced", G)
        f.start()
        with nc.Block() as block:
            @block.sync
            def _(sp):
                def body(st):
                    s, r = st.n(), st.slot()
                    sp.wait_ge(kept, f.at(kept, s, back=R))
                    sp.dma_start(stage[r][:], T.idx_v[:, ds(s * G, G)]).then_inc(staged[r], 16)
                    sp.wait_ge(compared, f.at(compared, s, back=R))
                    sp.dma_start(dst_rows[r][:], T.rows[ds(s * G, G), :].rearrange("(a t) e -> a (t e)", a=1)
                                 .to_broadcast([P, G * P])).then_inc(rows_in[r], 16)
                steps(sp, 2 * e.steps, R, 0, 0, body)

            @block.gpsimd
            def _(pool):
                def body(st):
                    s, r = st.n(), st.slot()
                    pool.wait_ge(staged[r], st.turn() * 16 + 16)
                    pool.sem_inc(go, 1)
                    pool.wait_ge(spread, f.at(spread, s, back=R))
                    pool.sem_inc(go, 1)
                    pool.wait_ge(kept, f.at(kept, s, back=R))
                    pool.sem_inc(go, 1)
                    for t in range(G):
                        pool.indirect_dma_start(out=gb[r][:, t, :], out_offset=None, in_=k.HT,
                                                in_offset=bass.IndirectOffsetOnAxis(ap=stage[r][:, t:t + 1], axis=0)
                                                ).then_inc(gathered[r], 16)
                steps(pool, 2 * e.steps, R, 0, 0, body)

            @block.vector
            def _(dve):
                V = nc.vector
                V.tensor_copy(k.gm_all[:].rearrange("p (n h) -> p n h", h=GH),
                              k.h_all[:].rearrange("p (n r) -> p n r", r=ROW)[:, :, GW:ROW])
                V.tensor_copy(ident[:], k.ident[:]).then_inc(ready, 1)
                dve.drain()
                regs = [[dve.alloc_register(f"max_owner{r}_{t}") for t in range(PAIRS)] for r in range(R)]

                def body(st):
                    if st.real():
                        n, r = st.n(), st.slot()
                        load_owners(dve, T.owner, n, regs[r])
                        for t in range(G):
                            dve.wait_ge(spread, f.at(spread, n, t))
                            V.tensor_reduce(mt[r][:, t // 2, t % 2, :], spread_ps[:, t, :].rearrange("p (h e) -> p h e", e=P),
                                            AX.X, ALU.max).then_inc(reduced, 1)
                    if st.real(1):
                        n, r = st.n(1), st.slot(1)
                        dve.wait_ge(rows_in[r], st.turn(1) * 16 + 16)
                        dve.wait_ge(spread, f.at(spread, n, back=R))
                        V.tensor_scalar(other[r][:].rearrange("p t e -> p (t e)"), dst_rows[r][:], k.iota_p[:], NEG,
                                        ALU.not_equal, ALU.mult).then_inc(compared, 1)
                    if st.real():
                        r = st.slot()
                        dve.drain()
                        V.tensor_tensor(mp[r][:], mt[r][:, :, 0, :], mt[r][:, :, 1, :], ALU.max)
                        for t in range(PAIRS):
                            owner = dve.snap(regs[r][t], min_val=0, max_val=BUCKETS - 1)
                            m = k.gm_all[:, ds(owner * GH, GH)]
                            dve.drain()
                            V.tensor_tensor(m, m, mp[r][:, t, :], ALU.max)
                steps(dve, 2 * e.steps, R, 1, 0, body)

            @block.scalar
            def _(act):
                def body(st):
                    n, r = st.n(), st.slot()
                    act.wait_ge(gathered[r], st.turn() * (16 * G) + 16 * G)
                    nc.scalar.copy(k.g_all[:, ds(n * G * ROW, G * ROW)], gb[r][:].rearrange("p t r -> p (t r)")).then_inc(kept, 1)
                steps(act, 2 * e.steps, R, 0, 0, body)

            @block.tensor
            def _(pe):
                pe.wait_ge(ready, 1)

                def body(st):
                    n, r = st.n(), st.slot()
                    pe.wait_ge(compared, f.at(compared, n))
                    pe.wait_ge(gathered[r], st.turn() * (16 * G) + 16 * G)
                    for t in range(G):
                        pe.wait_ge(reduced, f.at(reduced, n, t, back=1))
                        nc.tensor.matmul(spread_ps[:, t, :].rearrange("p (h e) -> p h e", e=P), ident[:],
                                         other[r][:, t, :].unsqueeze(1).to_broadcast([P, GH, P]), start=True, stop=False)
                        for h in range(GH):
                            op = nc.tensor.matmul(spread_ps[:, t, h * P:(h + 1) * P],
                                                  gb[r][:, t, GW + h:GW + h + 1].to_broadcast([P, P]), k.ident[:], start=False, stop=(h == GH - 1))
                        op.then_inc(spread, 1)
                steps(pe, 2 * e.steps, R, 0, 0, body)


def route_sums(nc, k, T):
    e, ROW, ALL = GAT, GW + GH, NODE_TILES
    PAIRS = G // 2
    R = 4
    with Phase(nc, "route", R) as f:
        def ring(name, shape, dt=F32):
            return [f.sb(f"{name}{r}", shape, dt) for r in range(R)]

        dst_rows = ring("dst_rows", [P, G * P], BF16)
        to_node, to_edge = ring("to_node", [P, G, P]), ring("to_edge", [P, G * P], BF16)
        parts = f.sb("parts", [P, ALL, 3, 2 * GH], BF16)
        left = f.sb("left", [P, ALL, 2 * GH])
        own = f.sb("own", [P, ALL, GH])
        tmp = f.sb("tmp", [P, ALL, GH])
        terms = ring("terms", [P, G, GH])
        wv = ring("wv", [P, G, ROW])
        back_ps, sum_ps = f.ps("back_ps", [P, 512]), f.ps("sum_ps", [P, 512])
        rows_in, split = [f.dma_sem(f"rows_in{r}") for r in range(R)], f.dma_sem("split")
        own_ready, own_exp, hot, fetched, formed, weighed, scaled, summed, added = (
            f.sem(x) for x in ("own_ready", "own_exp", "hot", "fetched", "formed", "weighed", "scaled", "summed", "added"))
        both = k.t2_all[:].rearrange("p (n x) -> p n x", x=2 * GH)
        h_rows = k.h_all[:].rearrange("p (n r) -> p n r", r=ROW)
        f.start()
        with nc.Block() as block:
            @block.sync
            def _(sp):
                def body(st):
                    s, r = st.n(), st.slot()
                    sp.wait_ge(hot, f.at(hot, s, back=R))
                    sp.dma_start(dst_rows[r][:], T.rows[ds(s * G, G), :].rearrange("(a t) e -> a (t e)", a=1)
                                 .to_broadcast([P, G * P])).then_inc(rows_in[r], 16)
                steps(sp, 2 * e.steps, R, 0, 0, body)

            @block.vector
            def _(dve):
                V = nc.vector

                def leaky(out, tmp_, x):
                    V.tensor_single_scalar(tmp_, x, 0.2, op=ALU.mult)
                    dve.drain()
                    V.tensor_tensor(out, x, tmp_, ALU.max)
                    dve.drain()

                dst = k.dst_term[:].rearrange("p (n h) -> p n h", h=GH)
                top = k.gm_all[:].rearrange("p (n h) -> p n h", h=GH)
                V.tensor_copy(both[:, :, 0:GH], dst)
                V.tensor_tensor(top, top, dst, ALU.add)
                dve.drain()
                leaky(both[:, :, GH:2 * GH], tmp[:], top)
                V.tensor_tensor(own[:], h_rows[:, :, GW:ROW], dst, ALU.add)
                dve.drain()
                leaky(own[:], tmp[:], own[:])
                V.tensor_tensor(own[:], own[:], both[:, :, GH:2 * GH], ALU.subtract)
                dve.drain().then_inc(own_ready, 1)
                V.tensor_copy(parts[:, :, 0, :], both)
                dve.drain()
                V.tensor_tensor(left[:], both, parts[:, :, 0, :], ALU.subtract)
                dve.drain()
                V.tensor_copy(parts[:, :, 1, :], left[:])
                dve.drain()
                V.tensor_tensor(left[:], left[:], parts[:, :, 1, :], ALU.subtract)
                dve.drain()
                V.tensor_copy(parts[:, :, 2, :], left[:])
                dve.drain().then_inc(split, 1)
                dve.wait_ge(own_exp, 1 + R)
                sums = k.gs_all[:].rearrange("p (n r) -> p n r", r=ROW)
                V.tensor_copy(sums[:, :, GW:ROW], own[:])
                V.tensor_tensor(sums[:, :, 0:GW].rearrange("p n (h x) -> p n h x", x=EXPERTS),
                                h_rows[:, :, 0:GW].rearrange("p n (h x) -> p n h x", x=EXPERTS),
                                own[:].unsqueeze(3).to_broadcast([P, ALL, GH, EXPERTS]), ALU.mult)
                dve.drain()
                regs = [[dve.alloc_register(f"route_owner{r}_{t}") for t in range(PAIRS)] for r in range(R)]

                def body(st):
                    if st.real():
                        n, r = st.n(), st.slot()
                        load_owners(dve, T.owner, n, regs[r])
                        dve.wait_ge(fetched, f.at(fetched, n))
                        rows = k.g_all[:, ds(n * G * ROW, G * ROW)].rearrange("p (t r) -> p t r", r=ROW)
                        back = back_ps[:, 0:G * 2 * GH].rearrange("p (t x) -> p t x", x=2 * GH)
                        t_ = terms[r]
                        V.tensor_tensor(t_[:], rows[:, :, GW:ROW], back[:, :, 0:GH], ALU.add)
                        dve.drain()
                        V.scalar_tensor_tensor(out=t_[:], in0=t_[:], scalar=0.2, in1=t_[:], op0=ALU.mult, op1=ALU.max)
                        dve.drain()
                        V.tensor_tensor(t_[:], t_[:], back[:, :, GH:2 * GH], ALU.subtract).then_inc(formed, 1)
                    if st.real(1):
                        n, r = st.n(1), st.slot(1)
                        dve.wait_ge(rows_in[r], st.turn(1) * 16 + 16)
                        dve.wait_ge(summed, f.at(summed, n, back=R))
                        one_hots(nc, k, dve, T, n, r, dst_rows, to_node, to_edge)
                        dve.drain().then_inc(hot, 1)
                    if st.real():
                        n, r = st.n(), st.slot()
                        dve.wait_ge(weighed, f.at(weighed, n))
                        V.tensor_tensor(wv[r][:, :, 0:GW].rearrange("p t (h x) -> p t h x", x=EXPERTS),
                                        rows[:, :, 0:GW].rearrange("p t (h x) -> p t h x", x=EXPERTS),
                                        wv[r][:, :, GW:ROW].unsqueeze(3).to_broadcast([P, G, GH, EXPERTS]), ALU.mult).then_inc(scaled, 1)
                    if st.real(-1):
                        n, r = st.n(-1), st.slot(-1)
                        dve.wait_ge(summed, f.at(summed, n))
                        for t in range(PAIRS):
                            owner = dve.snap(regs[r][t], min_val=0, max_val=BUCKETS - 1)
                            a = k.gs_all[:, ds(owner * ROW, ROW)]
                            V.tensor_tensor(a, a, sum_ps[:, t * ROW:(t + 1) * ROW], ALU.add)
                            if t == PAIRS - 1:
                                dve.drain().then_inc(added, 1)
                            else:
                                dve.drain()
                steps(dve, 2 * e.steps, R, 1, 1, body)

            @block.scalar
            def _(act):
                act.wait_ge(own_ready, 1 + R)
                nc.scalar.activation(own[:], own[:], ACT.Exp).then_inc(own_exp, 1)

                def body(st):
                    n, r = st.n(), st.slot()
                    act.wait_ge(formed, f.at(formed, n))
                    act.wait_ge(summed, f.at(summed, n, back=R))
                    nc.scalar.activation(wv[r][:, :, GW:ROW], terms[r][:], ACT.Exp).then_inc(weighed, 1)
                steps(act, 2 * e.steps, R, 0, 0, body)

            @block.tensor
            def _(pe):
                regs = [pe.alloc_register(f"route_fetch_owner{t}") for t in range(PAIRS)]
                pe.wait_ge(split, 1)

                def body(st):
                    if st.real(1):
                        n, r = st.n(1), st.slot(1)
                        load_owners(pe, T.owner, n, regs)
                        pe.wait_ge(hot, f.at(hot, n))
                        pe.wait_ge(formed, f.at(formed, n, back=1))
                        for t in range(G):
                            owner = pe.snap(regs[t // 2], min_val=0, max_val=BUCKETS - 1)
                            for part in range(3):
                                op = nc.tensor.matmul(back_ps[:, t * 2 * GH:(t + 1) * 2 * GH], to_edge[r][:, t * P:(t + 1) * P],
                                                      parts[:, ds(owner, 1), part, :].rearrange("p a x -> p (a x)"),
                                                      start=(part == 0), stop=(part == 2))
                        op.then_inc(fetched, 1)
                    if st.real():
                        n, r = st.n(), st.slot()
                        pe.wait_ge(scaled, f.at(scaled, n))
                        pe.wait_ge(added, f.at(added, n, back=1))
                        for t in range(G):
                            op = nc.tensor.matmul(sum_ps[:, t // 2 * ROW:(t // 2 + 1) * ROW], to_node[r][:, t, :], wv[r][:, t, :],
                                                  start=(t % 2 == 0), stop=(t % 2 == 1))
                        op.then_inc(summed, 1)
                steps(pe, 2 * e.steps, R, 1, 0, body)


def route_gates(nc, k):
    ROW, ALL = GW + GH, NODE_TILES
    with Phase(nc, "gates") as f:
        bg, gam, bet = (f.sb(n, [P, GW]) for n in ("bg", "gam", "bet"))
        agg, dev, sq = (f.sb(n, [P, ALL, GW]) for n in ("agg", "dev", "sq"))
        den = f.sb("den", [P, ALL, GH])
        mean, var, rstd, top, tot = (f.sb(n, [P, ALL]) for n in ("mean", "var", "rstd", "top", "tot"))
        sc, rank, cmp = (f.sb(n, [P, ALL, EXPERTS]) for n in ("sc", "rank", "cmp"))
        eq = f.sb("eq", [P, ALL])
        weights, var_ready, rooted, shifted, exps = f.dma_sem("weights"), f.sem("var_ready"), f.sem("rooted"), f.sem("shifted"), f.sem("exps")
        gates = k.gates[:].rearrange("p (n x) -> p n x", x=EXPERTS)
        f.start()
        with nc.Block() as block:
            @block.sync
            def _(sp):
                for to, of in ((bg, k.b_gat), (gam, k.ln_gamma), (bet, k.ln_beta)):
                    sp.dma_start(to[:], of.rearrange("(a n) -> a n", a=1).to_broadcast([P, GW])).then_inc(weights, 16)

            @block.gpsimd
            def _(pool):
                pool.wait_ge(var_ready, 1 + CREDIT)
                nc.gpsimd.tensor_tensor(rstd[:], var[:], k.power[:].to_broadcast([P, ALL]), ALU.pow).then_inc(rooted, 1)

            @block.scalar
            def _(act):
                act.wait_ge(shifted, 1 + CREDIT)
                nc.scalar.activation(cmp[:], cmp[:], ACT.Exp).then_inc(exps, 1)

            @block.vector
            def _(dve):
                V = nc.vector
                sums = k.gs_all[:].rearrange("p (n r) -> p n r", r=ROW)

                def step(op):
                    dve.drain()

                def wide(row):
                    return row[:].unsqueeze(1).to_broadcast([P, ALL, GW])

                def along(x, n):
                    return x[:].unsqueeze(2).to_broadcast([P, ALL, n])

                dve.wait_ge(weights, 48)
                step(V.tensor_single_scalar(den[:], sums[:, :, GW:ROW], 1e-16, op=ALU.add))
                step(V.reciprocal(den[:], den[:]))
                step(V.tensor_tensor(agg[:].rearrange("p n (h x) -> p n h x", x=EXPERTS),
                                     sums[:, :, 0:GW].rearrange("p n (h x) -> p n h x", x=EXPERTS),
                                     den[:].unsqueeze(3).to_broadcast([P, ALL, GH, EXPERTS]), ALU.mult))
                step(V.tensor_tensor(agg[:], agg[:], wide(bg), ALU.add))
                step(V.tensor_reduce(mean[:], agg[:], AX.X, ALU.add))
                step(V.tensor_single_scalar(mean[:], mean[:], 1.0 / GW, op=ALU.mult))
                step(V.tensor_tensor(dev[:], agg[:], along(mean, GW), ALU.subtract))
                step(V.tensor_tensor(sq[:], dev[:], dev[:], ALU.mult))
                step(V.tensor_reduce(var[:], sq[:], AX.X, ALU.add))
                V.tensor_scalar(var[:], var[:], 1.0 / GW, 1e-5, ALU.mult, ALU.add).then_inc(var_ready, 1)
                dve.wait_ge(rooted, 1 + CREDIT)
                step(V.tensor_tensor(dev[:], dev[:], along(rstd, GW), ALU.mult))
                step(V.tensor_tensor(dev[:], dev[:], wide(gam), ALU.mult))
                step(V.tensor_tensor(dev[:], dev[:], wide(bet), ALU.add))
                step(V.tensor_reduce(sc[:], dev[:].rearrange("p n (h x) -> p n x h", x=EXPERTS), AX.X, ALU.add))
                step(V.tensor_single_scalar(sc[:], sc[:], 1.0 / GH, op=ALU.mult))
                V.memset(rank[:], 0.0)
                for j in range(EXPERTS):
                    step(V.tensor_tensor(cmp[:], sc[:, :, j:j + 1].to_broadcast([P, ALL, EXPERTS]), sc[:], ALU.is_gt))
                    step(V.tensor_tensor(rank[:], rank[:], cmp[:], ALU.add))
                for i_ in range(1, EXPERTS):
                    for j in range(i_):
                        step(V.tensor_tensor(eq[:], sc[:, :, j], sc[:, :, i_], ALU.is_equal))
                        step(V.tensor_tensor(rank[:, :, i_], rank[:, :, i_], eq[:], ALU.add))
                step(V.tensor_single_scalar(rank[:], rank[:], 1.5, op=ALU.is_lt))
                step(V.tensor_reduce(top[:], sc[:], AX.X, ALU.max))
                V.tensor_tensor(cmp[:], sc[:], along(top, EXPERTS), ALU.subtract).then_inc(shifted, 1)
                dve.wait_ge(exps, 1 + CREDIT)
                step(V.tensor_tensor(cmp[:], cmp[:], rank[:], ALU.mult))
                step(V.tensor_reduce(tot[:], cmp[:], AX.X, ALU.add))
                step(V.reciprocal(tot[:], tot[:]))
                step(V.tensor_tensor(gates, cmp[:], along(tot, EXPERTS), ALU.mult))


def experts(nc, k):
    PAIRS, MC = NODE_TILES // 2, MF // P
    with Phase(nc, "experts") as f:
        w1, w2 = f.sb("w1", [P, EXPERTS, 2, MF]), f.sb("w2", [P, EXPERTS, MC, D])
        b1, b2 = f.sb("b1", [P, EXPERTS * MC]), f.sb("b2", [P, EXPERTS, D])
        xn, o, y = f.pair("xn", [P, D]), f.pair("o", [P, D]), f.pair("y", [P, D])
        xT = f.sb("xT", [P, 2, 2, P])
        hT = f.pair("hT", [P, MC, 2 * P])
        xT_ps = f.ps("xT_ps", [P, 2, 2, P])
        h_ps = [f.ps(f"h_ps{b}", [P, MC, 2 * P]) for b in range(2)]
        y_ps = [f.ps(f"y_ps{b}", [P, 2, D]) for b in range(2)]
        weights, loaded, o_loaded, stored = f.dma_sem("weights"), f.dma_pair("loaded"), f.dma_pair("o_loaded"), f.store_pair("stored")
        turned, copied = f.sem("turned"), f.sem("copied")
        BANKS = MC // 2
        hidden, activated = f.sem("hidden", EXPERTS * BANKS), f.sem("activated", EXPERTS * BANKS)
        contracted, added = f.sem("contracted", EXPERTS), f.sem("added", EXPERTS)
        f.start()
        with nc.Block() as block:
            @block.sync
            def _(sp):
                for x in range(EXPERTS):
                    sp.dma_start(w1[:, x, :, :], k.W1[x, :, :].rearrange("(c p) n -> p c n", p=P)).then_inc(weights, 16)
                    sp.dma_start(w2[:, x, :, :], k.W2[x, :, :].rearrange("(c p) n -> p c n", p=P)).then_inc(weights, 16)
                with nc.allow_non_contiguous_dma(reason="2048 words"):
                    sp.dma_start(b1[:], k.mb1.rearrange("x (c p) -> p (x c)", p=P)).then_inc(weights, 16)
                sp.dma_start(b2[:].rearrange("p x n -> p (x n)"), k.mb2.rearrange("(a x) n -> a (x n)", a=1).to_broadcast([P, EXPERTS * D])).then_inc(weights, 16)
                with sp.Fori(0, PAIRS, 1) as i:
                    for g in range(2):
                        s = i * 2 + g
                        sp.wait_ge(turned, i + CREDIT)
                        sp.dma_start(xn[g][:], rows_of(k.XN, s)).then_inc(loaded[g], 16)
                        sp.wait_ge(stored[g], i * 16 + 16)
                        sp.dma_start(o[g][:], rows_of(k.X2, s)).then_inc(o_loaded[g], 16)

            @block.vector
            def _(dve):
                V = nc.vector
                dve.wait_ge(weights, 16 * 10)
                with dve.Fori(0, PAIRS, 1) as i:
                    for g in range(2):
                        dve.wait_ge(o_loaded[g], i * 16 + 16)
                    for x in range(EXPERTS):
                        dve.wait_ge(contracted, f.at(contracted, i, x))
                        for g in range(2):
                            V.tensor_tensor(y[g][:], y_ps[x % 2][:, g, :], b2[:, x, :], ALU.add)
                        dve.drain()
                        for g in range(2):
                            V.scalar_tensor_tensor(out=o[g][:], in0=y[g][:], scalar=k.gates[:, ds((i * 2 + g) * EXPERTS + x, 1)],
                                                   in1=o[g][:], op0=ALU.mult, op1=ALU.add)
                        dve.drain().then_inc(added, 1)

            @block.tensor
            def _(pe):
                T = nc.tensor
                pe.wait_ge(weights, 16 * 10)
                with pe.Fori(0, PAIRS, 1) as i:
                    for g in range(2):
                        pe.wait_ge(loaded[g], i * 16 + 16)
                    pe.wait_ge(copied, i + CREDIT)
                    for g in range(2):
                        for half in range(2):
                            op = T.transpose(xT_ps[:, half, g, :], xn[g][:, half * P:(half + 1) * P], k.ident[:])
                    op.then_inc(turned, 1)
                    pe.wait_ge(copied, i + 1 + CREDIT)

                    def up(x):
                        for c in range(MC):
                            n = x * BANKS + c // 2
                            if c % 2 == 0:
                                pe.wait_ge(activated, f.at(activated, i, n - 2 * BANKS) if x >= 2 else f.at(activated, i, n + 2 * BANKS, back=1))
                            for half in range(2):
                                op = T.matmul(h_ps[x % 2][:, c, :], w1[:, x, half, c * P:(c + 1) * P],
                                              xT[:, half, :, :].rearrange("p g n -> p (g n)"), start=(half == 0), stop=(half == 1))
                            if c % 2:
                                op.then_inc(hidden, 1)

                    def down(x):
                        pe.wait_ge(added, f.at(added, i, x - 2) if x >= 2 else f.at(added, i, x + 2, back=1))
                        for g in range(2):
                            for c in range(MC):
                                if g == 0 and c % 2 == 0:
                                    pe.wait_ge(activated, f.at(activated, i, x * BANKS + c // 2))
                                op = T.matmul(y_ps[x % 2][:, g, :], hT[x % 2][:, c, g * P:(g + 1) * P], w2[:, x, c, :],
                                              start=(c == 0), stop=(c == MC - 1))
                        op.then_inc(contracted, 1)

                    up(0)
                    for x in range(1, EXPERTS):
                        up(x)
                        down(x - 1)
                    down(EXPERTS - 1)

            @block.scalar
            def _(act):
                A = nc.scalar
                act.wait_ge(weights, 16 * 10)
                with act.Fori(0, PAIRS, 1) as i:
                    act.wait_ge(turned, i + 1 + CREDIT)
                    act.wait_ge(hidden, f.at(hidden, i, back=1))
                    A.copy(xT[:].rearrange("p a g n -> p (a g n)"), xT_ps[:].rearrange("p a g n -> p (a g n)")).then_inc(copied, 1)
                    for x in range(EXPERTS):
                        act.wait_ge(contracted, f.at(contracted, i, x - 2) if x >= 2 else f.at(contracted, i, x + 2, back=1))
                        for c in range(MC):
                            n = x * MC + c
                            if c % 2 == 0:
                                act.wait_ge(hidden, f.at(hidden, i, n // 2))
                            A.activation(hT[x % 2][:, c, :], h_ps[x % 2][:, c, :], ACT.Gelu, bias=b1[:, n:n + 1])
                            if c % 2:
                                act.drain().then_inc(activated, 1)
                    act.wait_ge(added, f.at(added, i))
                    for g in range(2):
                        act.dma_start(rows_of(k.XO, i * 2 + g), o[g][:]).then_inc(stored[g], 16)
                for g in range(2):
                    act.wait_ge(stored[g], 16 * PAIRS + 16)


def program(nc, A):
    k = Space()
    k.x, k.src, k.dst, k.edge_type, k.node_type = (A["x"], A["src"], A["dst"], A["edge_type"], A["node_type"])
    k.W_Q, k.W_K, k.W_V, k.W_E, k.mu = (A["W_Q"], A["W_K"], A["W_V"], A["W_E"], A["mu"])
    k.Wo, k.bo, k.ln1_g, k.ln1_b, k.ln2_g = (A["Wo"], A["bo"], A["ln1_g"], A["ln1_b"], A["ln2_g"])
    k.ln2_b, k.w1, k.b1, k.w2, k.b2 = (A["ln2_b"], A["w1"], A["b1"], A["w2"], A["b2"])
    k.out_g, k.out_b, k.W_gat, k.att_src, k.att_dst = (A["out_g"], A["out_b"], A["W_gat"], A["att_src"], A["att_dst"])
    k.b_gat, k.ln_gamma, k.ln_beta, k.W1, k.mb1 = (A["b_gat"], A["ln_gamma"], A["ln_beta"], A["W1"], A["mb1"])
    k.W2, k.mb2, k.edge_src, k.edge_dst, k.out = (A["W2"], A["mb2"], A["edge_src"], A["edge_dst"], A["out"])
    with ExitStack() as ctx:
        k.sb = lambda name, shape, dt=F32: ctx.enter_context(nc.sbuf_tensor(name, shape, dt))

        def dram(name, shape, dt=F32):
            return nc.dram_tensor(name, shape, dt).ap()

        k.XP, k.X, k.X2, k.XN, k.XO = (dram(n, [NPAD, D]) for n in ("x_padded", "x_layer", "x_residual", "x_routed", "x_out"))
        k.KT, k.HT = dram("kv_table", [NPAD * EDGE_TYPES, KV]), dram("h_table", [NPAD, GW + GH])
        constants(nc, k)

        def tables(name, e, gnn, scope):
            def sb(n, shape, dt=F32):
                return scope.enter_context(nc.sbuf_tensor(f"{name}_{n}", shape, dt))
            T = Space()
            T.edges, T.owner = dram(name + "_edges", [e.tiles * P, 4]), dram(name + "_owner", [1, e.chunks * P], I32)
            T.rows = dram(name + "_rows", [e.tiles, P], BF16)
            T.idx_v, T.rel = sb("idx_v", [P, e.tiles + 2 * G], I32), sb("rel", [P, e.tiles])
            if gnn:
                T.resets = dram(name + "_resets", [e.tiles, HEADS, P])
                T.idx_k, T.last = sb("idx_k", [P, e.tiles + 2 * G], I32), sb("last", [P, e.tiles])
            return T

        with ExitStack() as scope:
            T = tables("gnn", GNN, True, scope)
            sort_edges(nc, k, "gnn_sort", GNN, k.src, k.dst, k.edge_type, T)
            spread_edges(nc, k, "gnn_spread", GNN, T, True)

            def sb(n, shape, dt=F32):
                return scope.enter_context(nc.sbuf_tensor(n, shape, dt))
            k.type_mask = sb("type_mask", [P, NODE_TILES * NODE_TYPES])
            k.q_all, k.a_all = sb("q_all", [P, NODE_TILES * D]), sb("a_all", [P, NODE_TILES * AW])
            k.m_all = sb("m_all", [P, NODE_TILES * HEADS])
            node_types(nc, k)
            first_norm(nc, k)
            with nc.Fori(0, LAYERS, 1) as l:
                project(nc, k, l)
                attend(nc, k, T)
                finish_layer(nc, k, l)
        with ExitStack() as scope:
            def sb(n, shape, dt=F32):
                return scope.enter_context(nc.sbuf_tensor(n, shape, dt))
            k.gates = sb("gates", [P, NODE_TILES * EXPERTS])
            with ExitStack() as inner:
                T = tables("gat", GAT, False, inner)
                sort_edges(nc, k, "gat_sort", GAT, k.edge_src, k.edge_dst, None, T)
                spread_edges(nc, k, "gat_spread", GAT, T, False)

                def sbi(n, shape, dt=F32):
                    return inner.enter_context(nc.sbuf_tensor(n, shape, dt))
                k.h_all, k.gs_all = (sbi(n, [P, NODE_TILES * (GW + GH)]) for n in ("h_all", "gs_all"))
                k.dst_term, k.gm_all = (sbi(n, [P, NODE_TILES * GH]) for n in ("dst_term", "gm_all"))
                k.t2_all = sbi("t2_all", [P, NODE_TILES * 2 * GH])
                k.g_all = sbi("g_all", [P, GAT.tiles * (GW + GH)])
                route_inputs(nc, k)
                route_maxima(nc, k, T)
                route_sums(nc, k, T)
                route_gates(nc, k)
            experts(nc, k)
            cut_output(nc, k)


def node_types(nc, k):
    with Phase(nc, "types") as f:
        types_i, types = f.sb("types_i", [P, NODE_TILES], I32), f.sb("types", [P, NODE_TILES])
        zeroed, loaded = f.dma_sem("zeroed"), f.dma_sem("loaded")
        f.start()
        with nc.Block() as block:
            @block.sync
            def _(sp):
                sp.wait_ge(zeroed, 1)
                with nc.allow_non_contiguous_dma(reason="6250 words"):
                    sp.dma_start(types_i[:, 0:BUCKETS - 1], k.node_type[0:(BUCKETS - 1) * P].rearrange("(i p) -> p i", p=P)).then_inc(loaded, 16)
                    sp.dma_start(types_i[0:LAST, BUCKETS - 1:BUCKETS], k.node_type[(BUCKETS - 1) * P:N].rearrange("(p i) -> p i", i=1)).then_inc(loaded, 16)

            @block.vector
            def _(dve):
                nc.vector.memset(types_i[:], 0)
                dve.drain().then_inc(zeroed, 1)
                dve.wait_ge(loaded, 32)
                nc.vector.tensor_copy(types[:], types_i[:])
                dve.drain()
                for t in range(NODE_TYPES):
                    nc.vector.tensor_single_scalar(k.type_mask[:].rearrange("p (i t) -> p i t", t=NODE_TYPES)[:, :, t], types[:], float(t), op=ALU.is_equal)


def cut_output(nc, k):
    with Phase(nc, "cut") as f:
        written = f.dma_sem("written")
        f.start()
        with nc.Block() as block:
            @block.sync
            def _(sp):
                sp.dma_start(k.out, k.XO[0:N, :]).then_inc(written, 16)
                sp.wait_ge(written, 16)


_INS = {"x": "x", "src": "src", "dst": "dst", "edge_type_3": "edge_type", "node_type_4": "node_type",
        "L0_gnn_W_Q": "W_Q", "L0_gnn_W_K": "W_K", "L0_gnn_W_V": "W_V", "L0_gnn_W_E": "W_E", "L0_gnn_mu": "mu",
        "L0_gnn_Wo": "Wo", "L0_gnn_bo": "bo", "L0_gnn_ln1_g": "ln1_g", "L0_gnn_ln1_b": "ln1_b",
        "L0_gnn_ln2_g": "ln2_g", "L0_gnn_ln2_b": "ln2_b", "L0_gnn_w1": "w1", "L0_gnn_b1": "b1",
        "L0_gnn_w2": "w2", "L0_gnn_b2": "b2", "L0_gnn_out_g": "out_g", "L0_gnn_out_b": "out_b",
        "L0_ffn_W_gat": "W_gat", "L0_ffn_att_src": "att_src", "L0_ffn_att_dst": "att_dst", "L0_ffn_b_gat": "b_gat",
        "L0_ffn_ln_gamma": "ln_gamma", "L0_ffn_ln_beta": "ln_beta", "L0_ffn_W1": "W1", "L0_ffn_b1": "mb1",
        "L0_ffn_W2": "W2", "L0_ffn_b2": "mb2"}


def kernel(**inputs):
    import numpy as _np
    import concourse.bacc as _bacc
    from concourse.bass_utils import run_bass_kernel_spmd as _run

    nc = _bacc.Bacc("TRN2", target_bir_lowering=False, num_devices=1)
    arrays, aps = {}, {}

    def put(name, a):
        arrays[f"in_{name}"] = _np.ascontiguousarray(a)
        aps[name] = nc.dram_tensor(f"in_{name}", list(a.shape), mybir.dt.from_np(a.dtype), kind="ExternalInput").ap()

    for name, short in _INS.items():
        put(short, _np.asarray(inputs[name]))
    edges = _np.asarray(inputs["L0_ffn_edge_index"])
    put("edge_src", edges[0])
    put("edge_dst", edges[1])
    aps["out"] = nc.dram_tensor("out_x", [N, D], F32, kind="ExternalOutput").ap()
    program(nc, aps)
    r = _run(nc, [arrays], core_ids=[0])
    return r.results[0]["out_x"]
```

```python
from contextlib import ExitStack

import concourse.bass as bass
from concourse import mybir

F32 = mybir.dt.float32
I32 = mybir.dt.int32
U32 = mybir.dt.uint32
BF16 = mybir.dt.bfloat16
ALU = mybir.AluOpType
ACT = mybir.ActivationFunctionType
AX = mybir.AxisListType
ds = bass.ds

P = 128
D = 256
HEADS, HD = 8, 32
LAYERS, NODE_TYPES, EDGE_TYPES = 3, 4, 3
N = 6250
NODE_TILES = 52
NPAD = NODE_TILES * P
BUCKETS = 49
LAST = N - (BUCKETS - 1) * P
G = 8
GH, EXPERTS, GW = 4, 4, 16
MF = 512
DFF = 1024
AW = HEADS * (HD + 1)
KV = D + AW
NEG = -1.0e30
CREDIT = 2


class Space:
    pass


def edge_shape(edges, per_partition, padded, group):
    tiles = (edges + (group * P - 1) * BUCKETS) // (group * P) * group
    tiles = -(-tiles // (2 * G)) * 2 * G
    e = Space()
    e.edges, e.per, e.tiles, e.group, e.groups = edges, per_partition, tiles, group, tiles // group
    e.padded, e.steps, e.chunks = padded, tiles // (2 * G), -(-tiles // P)
    return e


GNN = edge_shape(106250, 832, 832, 4)
BY_TILE, BY_PAIR = 4, 6
BY_TILES = BY_TILE * LAYERS * NODE_TILES
GAT = edge_shape(131072, 1024, BY_TILES + BY_PAIR * LAYERS * NODE_TILES // 2, 2)


class Phase:

    def __init__(self, nc, name, depth=2):
        self.depth = depth
        self.nc, self.name, self.ctx, self.sems, self.credited, self.per_step = nc, name, ExitStack(), [], [], {}

    def __enter__(self):
        self.ctx.__enter__()
        return self

    def __exit__(self, *a):
        return self.ctx.__exit__(*a)

    def sb(self, name, shape, dt=F32):
        return self.ctx.enter_context(self.nc.sbuf_tensor(f"{self.name}_{name}", shape, dt))

    def pair(self, name, shape, dt=F32):
        return [self.sb(f"{name}{g}", shape, dt) for g in range(2)]

    def ps(self, name, shape, dt=F32):
        return self.ctx.enter_context(self.nc.psum_tensor(f"{self.name}_{name}", shape, dt))

    def dma_sem(self, name):
        s = self.ctx.enter_context(self.nc.semaphore(f"{self.name}_{name}"))
        self.sems.append(s)
        return s

    def dma_pair(self, name):
        return [self.dma_sem(f"{name}{g}") for g in range(2)]

    def sem(self, name, per_step=1):
        s = self.dma_sem(name)
        self.credited.append((s, self.depth * per_step))
        self.per_step[s.name] = per_step
        return s

    def store_pair(self, name):
        pair = self.dma_pair(name)
        self.credited += [(s, 16) for s in pair]
        return pair

    def at(self, sem, step, event=None, back=0):
        per = self.per_step[sem.name]
        return step * per + ((self.depth - back) * per + (per if event is None else event + 1))

    def start(self):
        with self.nc.Block() as block:
            @block.gpsimd
            def _(pool):
                pool.dma_reset()
                for s in self.sems:
                    pool.sem_clear(s)
                for s, start in self.credited:
                    pool.sem_inc(s, start)


def constants(nc, k):
    k.ident = k.sb("ident", [P, P])
    k.iota_row = k.sb("iota_row", [P, P])
    k.iota_p = k.sb("iota_p", [P, 1])
    k.ones = k.sb("ones", [P, P])
    k.tri = k.sb("tri", [P, P])
    k.power = k.sb("power", [P, 1])
    with Phase(nc, "const") as f:
        made = f.dma_sem("made")
        copied = f.dma_sem("copied")
        ZR = 7
        zero = f.sb("zero", [(NPAD - N) // ZR, ZR * D])
        f.start()
        with nc.Block() as block:
            @block.gpsimd
            def _(pool):
                nc.gpsimd.memset(k.ident[:], 0.0)
                nc.gpsimd.memset(k.ones[:], 1.0)
                nc.gpsimd.memset(k.power[:], -0.5)
                nc.gpsimd.memset(k.tri[:], 1.0)
                nc.gpsimd.memset(zero[:], 0.0)
                nc.gpsimd.iota(k.iota_row[:], pattern=[[1, P]], base=0, channel_multiplier=0,
                               allow_small_or_imprecise_dtypes=True)
                nc.gpsimd.iota(k.iota_p[:], pattern=[[1, 1]], base=0, channel_multiplier=1,
                               allow_small_or_imprecise_dtypes=True)
                pool.drain()
                nc.gpsimd.affine_select(out=k.ident[:], in_=k.ident[:], compare_op=ALU.not_equal, fill=1.0,
                                        base=0, pattern=[[-1, P]], channel_multiplier=1)
                nc.gpsimd.affine_select(out=k.tri[:], in_=k.tri[:], compare_op=ALU.is_gt, fill=0.0,
                                        base=0, pattern=[[1, P]], channel_multiplier=-1)
                pool.drain()
                nc.gpsimd.memset(zero[:, 0:1], 0.0).then_inc(made, 1)

            @block.sync
            def _(sp):
                sp.wait_ge(made, 1)
                sp.dma_start(k.XP[0:N, :], k.x).then_inc(copied, 16)
                sp.dma_start(k.XP[N:NPAD, :].rearrange("(p r) c -> p (r c)", r=ZR), zero[:]).then_inc(copied, 16)
                sp.wait_ge(copied, 32)


class Scatter:

    def __init__(self, nc, f, e, T, width):
        self.nc, self.e, self.T, self.width = nc, e, T, width
        self.pos, self.rec = f.pair("stage_pos", [P, width], I32), f.pair("stage_rec", [P, width, 4])
        self.staged, self.written = f.dma_pair("staged"), f.dma_pair("written")
        self.go = f.sem("scatter_go")

    def stage(self, eng, r, turn, first):
        if not isinstance(turn, int) or turn:
            eng.wait_ge(self.written[r], turn * (16 * self.width))
        eng.dma_start(self.pos[r][:], self.T.pos[:, ds(first, self.width)]).then_inc(self.staged[r], 16)
        eng.dma_start(self.rec[r][:], self.T.load[:, ds(first, self.width), :]).then_inc(self.staged[r], 16)

    def write(self, pool, r, turn):
        pool.wait_ge(self.staged[r], turn * 32 + 32)
        pool.sem_inc(self.go, 1)
        for t in range(self.width):
            pool.indirect_dma_start(
                out=self.T.edges, out_offset=bass.IndirectOffsetOnAxis(ap=self.pos[r][:, t:t + 1], axis=0),
                in_=self.rec[r][:, t, :], in_offset=None,
                bounds_check=self.e.tiles * P - 1, oob_is_err=False).then_inc(self.written[r], 16)

    def finish(self, pool, turns):
        for r in range(2):
            pool.wait_ge(self.written[r], 16 * self.width * turns)


def rank_edges(nc, k, name, e, src_in, dst_in, type_in, T, other=None):
    L = e.per
    with Phase(nc, name) as f:
        if other is not None:
            scatter = Scatter(nc, f, other[0], other[1], G)
            turns = other[0].per // (2 * G)
        pos = f.sb("pos", [P, L])
        pos_i = f.sb("pos_i", [P, L], I32)
        load = f.sb("load", [P, L, 4])
        hi = f.sb("hi", [P, L])
        ranked = f.dma_sem("ranked")
        counted = f.dma_sem("counted")
        filled = f.dma_sem("filled")
        numbered = f.dma_sem("numbered")
        mapped = f.dma_sem("mapped")
        loaded = f.dma_sem("loaded")
        with ExitStack() as tmp:
            def sb(n_, s, d=F32):
                return tmp.enter_context(nc.sbuf_tensor(f"{name}_{n_}", s, d))
            src_i, dst_i = sb("src_i", [P, L], I32), sb("dst_i", [P, L], I32)
            type_i = sb("type_i", [P, L], I32)
            work_i = sb("work_i", [P, L], I32)
            mask, cum = sb("mask", [P, L]), sb("cum", [P, L])
            fill = sb("fill", [P, e.tiles, 4])
            cnt, off, tiles, tend = (sb(x, [P, BUCKETS]) for x in ("cnt", "off", "tiles", "tend"))
            tiles_i = sb("tiles_i", [P, BUCKETS], I32)
            tile_no, owner = sb("tile_no", [P, e.chunks]), sb("owner", [P, e.chunks])
            owner_i = sb("owner_i", [P, e.chunks], I32)
            scrap = sb("scrap", [P, BUCKETS])
            if e.padded > L:
                beyond = sb("beyond", [P, e.padded - L], I32)
            sums = tmp.enter_context(nc.psum_tensor(f"{name}_sums", [P, 512], F32))
            f.start()
            full = e.edges // L
            rest = e.edges - full * L
            with nc.Block() as block:
                if other is not None:
                    @block.scalar
                    def _(act):
                        def body(st):
                            scatter.stage(act, st.slot(), st.turn(), st.n() * G)
                        steps(act, 2 * turns, 2, 0, 0, body)

                @block.gpsimd
                def _(pool):
                    nc.gpsimd.iota(tile_no[:], pattern=[[P, e.chunks]], base=0, channel_multiplier=1,
                                   allow_small_or_imprecise_dtypes=True).then_inc(numbered, 1)
                    if other is not None:
                        def body(st):
                            scatter.write(pool, st.slot(), st.turn())
                        steps(pool, 2 * turns, 2, 0, 0, body)
                        scatter.finish(pool, turns)

                @block.sync
                def _(sp):
                    sp.wait_ge(filled, 1)
                    todo = [(dst_i, dst_in), (src_i, src_in)] + ([(type_i, type_in)] if type_in is not None else [])
                    for to, of in todo:
                        sp.dma_start(to[0:full, :], of[0:full * L].rearrange("(p l) -> p l", l=L)).then_inc(loaded, 16)
                        if rest:
                            sp.dma_start(to[full:full + 1, 0:rest],
                                         of[full * L:e.edges].rearrange("(p l) -> p l", p=1)).then_inc(loaded, 16)
                    sp.wait_ge(filled, 2)
                    sp.dma_start(T.edges.rearrange("(p r) c -> p (r c)", p=P), fill[:].rearrange("p r c -> p (r c)")).then_inc(mapped, 16)
                    sp.wait_ge(ranked, 1)
                    with nc.allow_non_contiguous_dma(reason="a few words"):
                        sp.dma_start(T.owner.rearrange("a (c p) -> (a p) c", p=P), owner_i[:]).then_inc(mapped, 16)
                    sp.wait_ge(ranked, 2)
                    sp.dma_start(T.pos[:, 0:L], pos_i[:]).then_inc(mapped, 16)
                    sp.dma_start(T.load[:, 0:L, :], load[:]).then_inc(mapped, 16)
                    if e.padded > L:
                        sp.dma_start(T.pos[:, L:e.padded], beyond[:]).then_inc(mapped, 16)
                        sp.dma_start(T.load[:, L:e.padded, :], load[:, 0:e.padded - L, :]).then_inc(mapped, 16)
                    sp.wait_ge(mapped, 64 + (32 if e.padded > L else 0))

                @block.tensor
                def _(pe):
                    pe.wait_ge(counted, 1)
                    nc.tensor.matmul(sums[:, 0:BUCKETS], k.tri[:], cnt[:], start=True, stop=True)
                    nc.tensor.matmul(sums[:, 64:64 + BUCKETS], k.ones[:], cnt[:], start=True, stop=True).then_inc(counted, 1)

                @block.vector
                def _(dve):
                    V = nc.vector
                    V.memset(dst_i[:], 1 << 20)
                    V.memset(src_i[:], 0)
                    V.memset(type_i[:], 0)
                    V.memset(pos[:], float(1 << 22))
                    V.memset(fill[:, :, 0], float(EDGE_TYPES * N))
                    V.memset(fill[:, :, 1], float(N))
                    V.memset(fill[:, :, 2:4], 999.0)
                    V.memset(load[:, :, 3], 0.0)
                    if e.padded > L:
                        V.memset(beyond[:], 1 << 22)
                    dve.drain()
                    V.memset(owner[:], 0.0).then_inc(filled, 1)
                    dve.drain()
                    V.memset(tiles[:], 0.0).then_inc(filled, 1)
                    n_in = (2 if type_in is None else 3) * (2 if rest else 1)
                    dve.wait_ge(loaded, 16 * n_in)
                    V.tensor_single_scalar(work_i[:], dst_i[:], 7, op=ALU.logical_shift_right)
                    dve.drain()
                    V.tensor_copy(hi[:], work_i[:])
                    dve.drain()
                    V.tensor_single_scalar(work_i[:], dst_i[:], P - 1, op=ALU.bitwise_and)
                    dve.drain()
                    V.tensor_copy(load[:, :, 2], work_i[:])
                    V.tensor_copy(mask[:], src_i[:])
                    dve.drain()
                    V.tensor_single_scalar(load[:, :, 1], mask[:], float(N - 1), op=ALU.min)
                    V.tensor_copy(cum[:], type_i[:])
                    dve.drain()
                    V.scalar_tensor_tensor(out=load[:, :, 0], in0=load[:, :, 1], scalar=float(EDGE_TYPES),
                                           in1=cum[:], op0=ALU.mult, op1=ALU.add)
                    dve.drain()
                    with dve.Fori(0, BUCKETS, 1) as b:
                        V.tensor_scalar(mask[:], hi[:], k.iota_row[:, ds(b, 1)], None, ALU.is_equal)
                        dve.drain()
                        V.tensor_tensor_scan(cum[:], k.ones[:, 0:1].to_broadcast([P, L]), mask[:], 0.0,
                                             ALU.mult, ALU.add)
                        dve.drain()
                        V.copy_predicated(pos[:], mask[:].bitcast(U32), cum[:])
                        V.tensor_copy(cnt[:, ds(b, 1)], cum[:, L - 1:L])
                        dve.drain()
                    V.memset(scrap[:, 0:1], 0.0).then_inc(counted, 1)
                    dve.wait_ge(counted, 2)
                    V.tensor_single_scalar(tiles[:], sums[:, 64:64 + BUCKETS], float(e.group * P - 1), op=ALU.add)
                    dve.drain()
                    V.tensor_copy(tiles_i[:], tiles[:])
                    dve.drain()
                    V.tensor_single_scalar(tiles_i[:], tiles_i[:], (e.group * P).bit_length() - 1, op=ALU.logical_shift_right)
                    dve.drain()
                    V.tensor_copy(tiles[:], tiles_i[:])
                    dve.drain()
                    V.tensor_tensor_scan(tend[:], k.ones[:, 0:1].to_broadcast([P, BUCKETS]), tiles[:], 0.0,
                                         ALU.mult, ALU.add)
                    dve.drain()
                    V.tensor_tensor(off[:], tend[:], tiles[:], ALU.subtract)
                    dve.drain()
                    V.scalar_tensor_tensor(out=off[:], in0=off[:], scalar=float(e.group * P), in1=sums[:, 0:BUCKETS],
                                           op0=ALU.mult, op1=ALU.add)
                    dve.drain()
                    V.tensor_single_scalar(off[:], off[:], -1.0, op=ALU.add)
                    dve.wait_ge(numbered, 1)
                    for c in range(e.chunks):
                        V.tensor_scalar(scrap[:], tend[:], tile_no[:, c:c + 1], None, ALU.is_le, ALU.add,
                                        accum_out=owner[:, c:c + 1])
                        dve.drain()
                    V.tensor_single_scalar(owner[:], owner[:], float(BUCKETS - 1), op=ALU.min)
                    dve.drain()
                    V.tensor_copy(owner_i[:], owner[:]).then_inc(ranked, 1)
                    dve.drain()
                    with dve.Fori(0, BUCKETS, 1) as b:
                        V.tensor_scalar(mask[:], hi[:], k.iota_row[:, ds(b, 1)], off[:, ds(b, 1)],
                                        ALU.is_equal, ALU.mult)
                        dve.drain()
                        V.tensor_tensor(pos[:], pos[:], mask[:], ALU.add)
                        dve.drain()
                    V.tensor_copy(pos_i[:], pos[:]).then_inc(ranked, 1)


def spread_edges(nc, k, name, e, T, gnn):
    with Phase(nc, name) as f:
        rec = f.pair("rec", [P, P, 4])
        rows = f.pair("rows", [P, P], BF16)
        last, reset = f.pair("last", [P, P]), f.pair("reset", [P, P])
        turned = [f.ps(f"turned{g}", [P, 4, P]) for g in range(2)]
        loaded, stored = f.dma_pair("loaded"), f.dma_pair("stored")
        flagged, transposed, taken = f.sem("flagged"), f.sem("transposed"), f.sem("taken")
        f.start()
        chunks = [(c, min(P, e.tiles - c * P)) for c in range(e.chunks)]
        with nc.Block() as block:
            @block.sync
            def _(sp):
                for c, n in chunks:
                    g = c % 2
                    if c >= 2:
                        sp.wait_ge(transposed, CREDIT + c - 1)
                        sp.wait_ge(flagged, CREDIT + c - 1)
                    sp.dma_start(rec[g][0:n, :, :].rearrange("p e c -> p (e c)"),
                                 T.edges[c * P * P:(c * P + n) * P, :].rearrange("(p e) c -> p (e c)", e=P)
                                 ).then_inc(loaded[g], 16)

            @block.vector
            def _(dve):
                V = nc.vector
                V.memset(T.idx_v[:, e.tiles:], 0)
                if gnn:
                    V.memset(T.idx_k[:, e.tiles:], 0)
                for c, n in chunks:
                    g = c % 2
                    dve.wait_ge(loaded[g], 16 * (c // 2 + 1))
                    if c >= 2:
                        dve.wait_ge(stored[g], (16 * (HEADS + 1) if gnn else 16) * (c // 2))
                        dve.wait_ge(transposed, CREDIT + c - 1)
                    rel = rec[g][0:n, :, 2]
                    if gnn:
                        V.memset(last[g][:, P - 1:P], 1.0)
                        V.memset(reset[g][:, 0:1], NEG)
                        V.tensor_tensor(last[g][0:n, 0:P - 1], rel[:, 0:P - 1], rel[:, 1:P], ALU.not_equal)
                        V.tensor_tensor(reset[g][0:n, 1:P], rel[:, 0:P - 1], rel[:, 1:P], ALU.not_equal)
                        dve.drain()
                        V.tensor_single_scalar(reset[g][0:n, 1:P], reset[g][0:n, 1:P], NEG, op=ALU.mult)
                        dve.drain()
                    V.tensor_copy(rows[g][0:n, :], rel).then_inc(flagged, 1)
                    dve.wait_ge(transposed, CREDIT + c + 1)
                    cols = slice(c * P, c * P + n)
                    V.tensor_copy(T.rel[:, cols], turned[g][:, 2, 0:n])
                    if gnn:
                        V.tensor_copy(T.idx_k[:, cols], turned[g][:, 0, 0:n])
                        V.tensor_copy(T.last[:, cols], turned[g][:, 3, 0:n])
                    V.tensor_copy(T.idx_v[:, cols], turned[g][:, 1, 0:n]).then_inc(taken, 1)

            @block.tensor
            def _(pe):
                for c, n in chunks:
                    g = c % 2
                    pe.wait_ge(flagged, CREDIT + c + 1)
                    if c >= 2:
                        pe.wait_ge(taken, CREDIT + c - 1)
                    for w in range(3):
                        last_op = nc.tensor.transpose(turned[g][:, w, 0:n], rec[g][0:n, :, w], k.ident[0:n, 0:n])
                    if gnn:
                        last_op = nc.tensor.transpose(turned[g][:, 3, 0:n], last[g][0:n, :], k.ident[0:n, 0:n])
                    last_op.then_inc(transposed, 1)

            @block.scalar
            def _(act):
                for c, n in chunks:
                    g = c % 2
                    act.wait_ge(flagged, CREDIT + c + 1)
                    act.dma_start(T.rows[c * P:c * P + n, :], rows[g][0:n, :]).then_inc(stored[g], 16)
                    if gnn:
                        for h in range(HEADS):
                            act.dma_start(T.resets[c * P:c * P + n, h, :], reset[g][0:n, :]).then_inc(stored[g], 16)
                for g in range(2):
                    act.wait_ge(stored[g], (16 * (HEADS + 1) if gnn else 16) * ((e.chunks + 1 - g) // 2))


class Step:

    def __init__(self, i, g, unroll, total, ring):
        self.i, self.g, self.unroll, self.total, self.ring = i, g, unroll, total, ring

    def place(self, d=0):
        return (self.g + d) % self.unroll

    def n(self, d=0):
        return self.i * self.unroll + (self.g + d)

    def slot(self, d=0):
        return (self.g + d) % self.ring

    def turn(self, d=0):
        return self.i * (self.unroll // self.ring) + (self.g + d) // self.ring

    def real(self, d=0):
        return not isinstance(self.i, int) or 0 <= self.n(d) < self.total


def steps(eng, total, unroll, lead, lag, body, ring=None):
    ring = ring or unroll
    for g in range(-lead, unroll):
        body(Step(0, g, unroll, total, ring))
    with eng.Fori(1, total // unroll - 1, 1) as i:
        for g in range(unroll):
            body(Step(i, g, unroll, total, ring))
    for g in range(unroll + lag):
        body(Step(total // unroll - 1, g, unroll, total, ring))


class Norm:

    def __init__(self, nc, k, f, name):
        self.nc, self.k = nc, k
        self.stats, self.mv, self.rstd = f.pair(name + "_stats", [P, 6]), f.pair(name + "_mv", [P, 2]), f.pair(name + "_rstd", [P, 1])
        self.measured, self.rooted = f.sem(name + "_measured"), f.sem(name + "_rooted")

    def moments(self, dve, g, x, eps=1e-5):
        nc = self.nc
        nc.vector.bn_stats(self.stats[g][:], x)
        dve.drain()
        nc.vector.bn_aggr(self.mv[g][:], self.stats[g][:])
        dve.drain()
        nc.vector.tensor_single_scalar(self.mv[g][:, 1:2], self.mv[g][:, 1:2], eps, op=ALU.add).then_inc(self.measured, 1)

    def root(self, pool, g, s):
        pool.wait_ge(self.measured, s + 1 + CREDIT)
        self.nc.gpsimd.tensor_tensor(self.rstd[g][:], self.mv[g][:, 1:2], self.k.power[:], ALU.pow).then_inc(self.rooted, 1)

    def apply(self, dve, g, s, out, x):
        dve.wait_ge(self.rooted, s + 1 + CREDIT)
        self.nc.vector.tensor_scalar(out, x, self.mv[g][:, 0:1], self.rstd[g][:], ALU.subtract, ALU.mult)


class PairNorm:

    def __init__(self, nc, k, f, name):
        self.nc, self.k, self.f = nc, k, f
        self.stats, self.mv, self.rstd = f.pair(name + "_stats", [P, 2, 6]), f.pair(name + "_mv", [P, 2, 2]), f.pair(name + "_rstd", [P, 2])
        self.measured, self.rooted = f.sem(name + "_measured"), f.sem(name + "_rooted")

    def moments(self, dve, r, x, eps=1e-5):
        V = self.nc.vector
        for g in range(2):
            V.bn_stats(self.stats[r][:, g, :], x[:, g, :])
        dve.drain()
        for g in range(2):
            V.bn_aggr(self.mv[r][:, g, :], self.stats[r][:, g, :])
        dve.drain()
        V.tensor_single_scalar(self.mv[r][:, :, 1], self.mv[r][:, :, 1], eps, op=ALU.add).then_inc(self.measured, 1)

    def root(self, pool, r, n):
        pool.wait_ge(self.measured, self.f.at(self.measured, n))
        self.nc.gpsimd.tensor_tensor(self.rstd[r][:], self.mv[r][:, :, 1], self.k.power[:].to_broadcast([P, 2]), ALU.pow).then_inc(self.rooted, 1)

    def apply(self, dve, r, n, out, x):
        dve.wait_ge(self.rooted, self.f.at(self.rooted, n))
        for g in range(2):
            self.nc.vector.tensor_scalar(out[:, g, :], x[:, g, :], self.mv[r][:, g, 0:1], self.rstd[r][:, g:g + 1], ALU.subtract, ALU.mult)


def rows_of(table, s, n=P):
    return table[ds(s * P, n), :]


def pair_of(table, n):
    return table[ds(n * 2 * P, 2 * P), :].rearrange("(g p) c -> p g c", p=P)


def first_norm(nc, k):
    with Phase(nc, "first") as f:
        x, y = f.pair("x", [P, D]), f.pair("y", [P, D])
        norm = Norm(nc, k, f, "norm")
        loaded, stored, done = f.dma_pair("loaded"), f.store_pair("stored"), f.sem("done")
        f.start()
        with nc.Block() as block:
            @block.sync
            def _(sp):
                with sp.Fori(0, NODE_TILES // 2, 1) as i:
                    for g in range(2):
                        sp.wait_ge(done, i * 2 + g + 1)
                        sp.dma_start(x[g][:], rows_of(k.XP, i * 2 + g)).then_inc(loaded[g], 16)

            @block.gpsimd
            def _(pool):
                with pool.Fori(0, NODE_TILES // 2, 1) as i:
                    for g in range(2):
                        norm.root(pool, g, i * 2 + g)

            @block.vector
            def _(dve):
                with dve.Fori(0, NODE_TILES // 2, 1) as i:
                    for g in range(2):
                        dve.wait_ge(loaded[g], i * 16 + 16)
                        norm.moments(dve, g, x[g][:])
                    for g in range(2):
                        dve.wait_ge(stored[g], i * 16 + 16)
                        norm.apply(dve, g, i * 2 + g, y[g][:], x[g][:])
                        dve.drain().then_inc(done, 1)

            @block.scalar
            def _(act):
                with act.Fori(0, NODE_TILES // 2, 1) as i:
                    for g in range(2):
                        act.wait_ge(done, i * 2 + g + 1 + CREDIT)
                        act.dma_start(rows_of(k.X, i * 2 + g), y[g][:]).then_inc(stored[g], 16)
                for g in range(2):
                    act.wait_ge(stored[g], 16 * (NODE_TILES // 2) + 16)


def project(nc, k, l, TG):
    QKV = 3 * HD
    with Phase(nc, "project") as f:
        wb = f.sb("wb", [P, HEADS, QKV])
        we = f.sb("we", [P, 2, EDGE_TYPES, P])
        mu = f.sb("mu", [P, HEADS, EDGE_TYPES])
        xt, xm, xmT = f.pair("xt", [P, D]), f.pair("xm", [P, HEADS, NODE_TYPES, HD]), f.pair("xmT", [P, HEADS, P])
        kk, kT, kp = f.pair("kk", [P, D]), f.pair("kT", [P, 2, P]), f.pair("kp", [P, EDGE_TYPES, KV])
        xT_ps = f.ps("xT_ps", [P, HEADS, P])
        qkv_ps = f.ps("qkv_ps", [P, 2, 512])
        kT_ps = f.ps("kT_ps", [P, 512])
        kp_ps = f.ps("kp_ps", [P, 2, 512])
        scatter = Scatter(nc, f, GAT, TG, BY_TILE)
        zeroed, weights = f.dma_sem("zeroed"), f.dma_sem("weights")
        loaded, stored = f.dma_pair("loaded"), f.store_pair("stored")
        masked, turned, copied, product = f.sem("masked"), f.sem("turned"), f.sem("copied"), f.sem("product")
        taken, k_turned, k_copied, k_product, k_scaled = (f.sem(x) for x in ("taken", "k_turned", "k_copied", "k_product", "k_scaled"))
        f.start()

        def heads(ps, q):
            return ps[:, :, 0:4 * QKV].rearrange("p a (h x) -> p a h x", x=QKV)[:, :, :, q * HD:(q + 1) * HD]

        with nc.Block() as block:
            @block.sync
            def _(sp):
                for t in range(NODE_TYPES):
                    for q, w in enumerate((k.W_Q, k.W_K, k.W_V)):
                        sp.dma_start(wb[t * HD:(t + 1) * HD, :, q * HD:(q + 1) * HD],
                                     w[ds(l, 1), t, :, :, :].rearrange("a h d e -> d (a h) e")).then_inc(weights, 16)
                sp.wait_ge(zeroed, 1)
                for half in range(2):
                    for h in range(4):
                        sp.dma_start(we[h * HD:(h + 1) * HD, half, :, h * HD:(h + 1) * HD],
                                     k.W_E[ds(l, 1), :, half * 4 + h, :, :].rearrange("a t d e -> d (a t) e")).then_inc(weights, 16)
                sp.dma_start(mu[:].rearrange("p h t -> p (h t)"),
                             k.mu[ds(l, 1), :, :].rearrange("a h t -> a (h t)").to_broadcast([P, HEADS * EDGE_TYPES])).then_inc(weights, 16)

                def body(st):
                    if st.real(2):
                        n, r = st.n(2), st.slot(2)
                        sp.wait_ge(masked, f.at(masked, n, back=2))
                        sp.dma_start(xt[r][:], rows_of(k.X, n)).then_inc(loaded[r], 16)
                    if st.real():
                        scatter.stage(sp, st.slot(), st.turn(), (l * NODE_TILES + st.n()) * BY_TILE)
                    if st.real(-1):
                        n, r = st.n(-1), st.slot(-1)
                        sp.wait_ge(k_scaled, f.at(k_scaled, n))
                        sp.dma_start(k.KT[ds(n * P * EDGE_TYPES, P * EDGE_TYPES), :].rearrange("(p t) c -> p (t c)", t=EDGE_TYPES),
                                     kp[r][:].rearrange("p t c -> p (t c)")).then_inc(stored[r], 16)
                steps(sp, NODE_TILES, 2, 2, 1, body)
                for r in range(2):
                    sp.wait_ge(stored[r], 16 * (NODE_TILES // 2) + 16)

            @block.gpsimd
            def _(pool):
                def body(st):
                    scatter.write(pool, st.slot(), st.turn())
                steps(pool, NODE_TILES, 2, 0, 0, body)
                scatter.finish(pool, NODE_TILES // 2)

            @block.vector
            def _(dve):
                V = nc.vector
                V.memset(we[:], 0.0)
                for r in range(2):
                    V.memset(kp[r][:, :, D:KV], 1.0)
                dve.drain().then_inc(zeroed, 1)
                dve.wait_ge(weights, 16 * 21)
                V.tensor_single_scalar(mu[:], mu[:], float(HD) ** -0.5, op=ALU.mult)
                dve.drain()

                def body(st):
                    if st.real(-1):
                        n, r = st.n(-1), st.slot(-1)
                        dve.wait_ge(k_turned, f.at(k_turned, n))
                        dve.wait_ge(k_product, f.at(k_product, n, back=2))
                        V.tensor_copy(kT[r][:].rearrange("p a c -> p (a c)"), kT_ps[:, 0:2 * P]).then_inc(k_copied, 1)
                        V.tensor_copy(kp[r][:, 1:EDGE_TYPES, D:KV], kp[r][:, 0, D:KV].unsqueeze(1).to_broadcast([P, EDGE_TYPES - 1, AW]))
                        dve.wait_ge(k_product, f.at(k_product, n))
                        for half in range(2):
                            V.tensor_tensor(kp[r][:, :, half * P:(half + 1) * P].rearrange("p t (h e) -> p t h e", e=HD),
                                            kp_ps[:, half, 0:EDGE_TYPES * P].rearrange("p (t h e) -> p t h e", t=EDGE_TYPES, e=HD),
                                            mu[:, half * 4:(half + 1) * 4, :].rearrange("p h t -> p t h").unsqueeze(3)
                                            .to_broadcast([P, EDGE_TYPES, 4, HD]), ALU.mult)
                        dve.drain().then_inc(k_scaled, 1)
                    if st.real(2):
                        n, r = st.n(2), st.slot(2)
                        dve.wait_ge(loaded[r], st.turn(2) * 16 + 16)
                        dve.wait_ge(turned, f.at(turned, n, back=2))
                        for t in range(NODE_TYPES):
                            V.tensor_scalar(xm[r][:, :, t, :], xt[r][:].rearrange("p (h d) -> p h d", d=HD),
                                            k.type_mask[:, ds(n * NODE_TYPES + t, 1)], None, ALU.mult)
                        dve.drain().then_inc(masked, 1)
                steps(dve, NODE_TILES, 2, 2, 1, body)

            @block.tensor
            def _(pe):
                T = nc.tensor
                pe.wait_ge(weights, 16 * 21)

                def body(st):
                    if st.real():
                        n, r = st.n(), st.slot()
                        pe.wait_ge(copied, f.at(copied, n))
                        pe.wait_ge(taken, f.at(taken, n, back=1))
                        for h in range(HEADS):
                            op = T.matmul(qkv_ps[:, h // 4, (h % 4) * QKV:(h % 4 + 1) * QKV], xmT[r][:, h, :], wb[:, h, :], start=True, stop=True)
                        op.then_inc(product, 1)
                    if st.real(-1):
                        n, r = st.n(-1), st.slot(-1)
                        pe.wait_ge(taken, f.at(taken, n))
                        pe.wait_ge(k_copied, f.at(k_copied, n, back=1))
                        for half in range(2):
                            op = T.transpose(kT_ps[:, half * P:(half + 1) * P], kk[r][:, half * P:(half + 1) * P], k.ident[:])
                        op.then_inc(k_turned, 1)
                    if st.real(1):
                        n, r = st.n(1), st.slot(1)
                        pe.wait_ge(masked, f.at(masked, n))
                        pe.wait_ge(copied, f.at(copied, n, back=1))
                        for h in range(HEADS):
                            op = T.transpose(xT_ps[:, h, :], xm[r][:, h, :, :].rearrange("p t d -> p (t d)"), k.ident[:])
                        op.then_inc(turned, 1)
                    if st.real(-1):
                        n, r = st.n(-1), st.slot(-1)
                        pe.wait_ge(k_copied, f.at(k_copied, n))
                        pe.wait_ge(k_scaled, f.at(k_scaled, n, back=1))
                        for half in range(2):
                            op = T.matmul(kp_ps[:, half, 0:EDGE_TYPES * P], kT[r][:, half, :],
                                          we[:, half, :, :].rearrange("p t c -> p (t c)"), start=True, stop=True)
                        op.then_inc(k_product, 1)
                steps(pe, NODE_TILES, 2, 1, 1, body)

            @block.scalar
            def _(act):
                A = nc.scalar
                act.wait_ge(zeroed, 1)

                def body(st):
                    if st.real():
                        n, r = st.n(), st.slot()
                        act.wait_ge(product, f.at(product, n))
                        act.wait_ge(k_turned, f.at(k_turned, n, back=2))
                        A.copy(kk[r][:].rearrange("p (a h d) -> p a h d", a=2, d=HD), heads(qkv_ps, 1))
                        A.copy(k.q_all[:, ds(n * D, D)].rearrange("p (a h d) -> p a h d", a=2, d=HD), heads(qkv_ps, 0))
                    if st.real(1):
                        n, r = st.n(1), st.slot(1)
                        act.wait_ge(turned, f.at(turned, n))
                        act.wait_ge(product, f.at(product, n, back=2))
                        A.copy(xmT[r][:, 0:4, :], xT_ps[:, 0:4, :])
                        A.copy(xmT[r][:, 4:8, :], xT_ps[:, 4:8, :])
                        act.drain().then_inc(copied, 1)
                    if st.real():
                        r = st.slot()
                        act.wait_ge(stored[r], st.turn() * 16 + 16)
                        A.copy(kp[r][:, 0, D:KV].rearrange("p (a h d) -> p a h d", a=2, d=HD + 1)[:, :, :, 0:HD], heads(qkv_ps, 2))
                        act.drain().then_inc(taken, 1)
                steps(act, NODE_TILES, 2, 1, 0, body)


def load_owners(eng, owner, s, regs):
    eng.load(regs, owner[0:1, ds(s * (G // 2), G // 2)])


def one_hots(nc, k, dve, T, s, g, dst_rows, to_node, to_edge):
    nc.vector.tensor_scalar(to_edge[g][:], dst_rows[g][:], k.iota_p[:], None, ALU.is_equal)
    nc.vector.tensor_tensor(to_node[g][:], T.rel[:, ds(s * G, G)].unsqueeze(2).to_broadcast([P, G, P]),
                            k.iota_row[:].unsqueeze(1).to_broadcast([P, G, P]), ALU.is_equal)


def attend(nc, k, T):
    e, R = GNN, 4
    B = e.group
    ROWS = B * HEADS
    with Phase(nc, "attend", R) as f:
        def ring(name, shape, dt=F32, n=R):
            return [f.sb(f"{name}{r}", shape, dt) for r in range(n)]

        stage, dst_rows, resets = ring("stage", [P, B], I32), ring("dst_rows", [P, B * P], BF16), ring("resets", [ROWS, P])
        kv = ring("kv", [P, B, KV])
        minus_p, apart = f.sb("minus_p", [P, 1]), ring("apart", [P, B * P], n=2)
        weighed_v = ring("weighed_v", [P, B, AW], n=2)
        qs = ring("qs", [P, D])
        to_edge, to_node = ring("to_edge", [P, B * P]), ring("to_node", [P, B, P])
        sg, run, tops = ring("sg", [P, B, HEADS]), ring("run", [ROWS, P]), ring("tops", [P, B, HEADS + 1])
        absent, mv, gm = ring("absent", [P, B]), ring("mv", [P, B, HEADS]), ring("gm", [P, HEADS])
        mn, drop, shift, ws = ring("mn", [P, HEADS]), ring("drop", [P, HEADS]), ring("shift", [P, B, HEADS]), ring("ws", [P, B, HEADS])
        scaled_down = ring("scaled_down", [P, HEADS, HD + 1], n=2)
        q_ps = f.ps("q_ps", [P, 2, 2, D])
        hot_ps, sT_ps, run_ps, top_ps, m_ps, sum_ps = (f.ps(n, [P, 512]) for n in ("hot_ps", "sT_ps", "run_ps", "top_ps", "m_ps", "sum_ps"))
        gathered, rows_in, resets_in, staged = ([f.dma_sem(f"{n}{r}") for r in range(R)] for n in ("gathered", "rows_in", "resets_in", "staged"))
        go, turns, fell = f.sem("go"), f.sem("turns"), f.sem("fell")
        cleared, half_scaled = f.dma_sem("cleared"), f.sem("half_scaled")
        OWN = 1

        def weigh(eng, r, first, end):
            return eng.tensor_tensor(weighed_v[r % 2][:, first:end, :].rearrange("p t (h e) -> p t h e", e=HD + 1),
                                     kv[r][:, first:end, D:KV].rearrange("p t (h e) -> p t h e", e=HD + 1),
                                     ws[r][:, first:end, :].unsqueeze(3).to_broadcast([P, end - first, HEADS, HD + 1]), ALU.mult)

        q_taken, hot, hot_turned, hot_copied, scored, s_turned, ran, r_turned, topped = (
            f.sem(n) for n in ("q_taken", "hot", "hot_turned", "hot_copied", "scored", "s_turned", "ran", "r_turned", "topped"))
        at_nodes, merged, dropped, brought, shifted, weighed, scaled, summed, added = (
            f.sem(n) for n in ("at_nodes", "merged", "dropped", "brought", "shifted", "weighed", "scaled", "summed", "added"))
        queried, multiplied = f.sem("queried", 2), f.sem("multiplied", 2)
        f.start()
        with nc.Block() as block:
            @block.sync
            def _(sp):
                def body(st):
                    s, r = st.n(), st.slot()
                    sp.wait_ge(hot, f.at(hot, s, back=R))
                    sp.dma_start(dst_rows[r][:], T.rows[ds(s * B, B), :].rearrange("(a t) e -> a (t e)", a=1)
                                 .to_broadcast([P, B * P])).then_inc(rows_in[r], 16)
                    sp.wait_ge(scored, f.at(scored, s, back=R))
                    sp.dma_start(stage[r][:], T.idx_k[:, ds(s * B, B)]).then_inc(staged[r], 16)
                    sp.wait_ge(ran, f.at(ran, s, back=R))
                    sp.dma_start(resets[r][:], T.resets[ds(s * B, B), :, :].rearrange("t h e -> (t h) e")).then_inc(resets_in[r], 16)
                steps(sp, e.groups, R, 0, 0, body)

            @block.gpsimd
            def _(pool):
                pool.wait_ge(cleared, 1)

                def body(st):
                    if st.real(-2):
                        n, r = st.n(-2), st.slot(-2)
                        pool.wait_ge(gathered[r], st.turn(-2) * (16 * B) + 16 * B)
                        pool.sem_inc(go, 1)
                        pool.wait_ge(weighed, f.at(weighed, n))
                        pool.sem_inc(go, 1)
                        pool.wait_ge(summed, f.at(summed, n, back=2))
                        weigh(nc.gpsimd, r, OWN, B).then_inc(scaled, 1)
                    if st.real(2):
                        n, r = st.n(2), st.slot(2)
                        pool.wait_ge(staged[r], st.turn(2) * 16 + 16)
                        pool.sem_inc(go, 1)
                        pool.wait_ge(scaled, f.at(scaled, n, back=R))
                        pool.sem_inc(go, 1)
                        pool.wait_ge(half_scaled, f.at(half_scaled, n, back=R))
                        pool.sem_inc(go, 1)
                        for t in range(B):
                            pool.indirect_dma_start(out=kv[r][:, t, :], out_offset=None, in_=k.KT,
                                                    in_offset=bass.IndirectOffsetOnAxis(ap=stage[r][:, t:t + 1], axis=0),
                                                    bounds_check=N * EDGE_TYPES - 1, oob_is_err=False).then_inc(gathered[r], 16)
                steps(pool, e.groups, R, 2, 2, body)

            @block.vector
            def _(dve):
                V = nc.vector
                for r in range(R):
                    V.memset(kv[r][:], 0.0)
                V.tensor_single_scalar(minus_p[:], k.iota_p[:], -1.0, op=ALU.mult)
                V.memset(k.a_all[:], 0.0)
                V.memset(k.m_all[:], -1e9)
                dve.drain().then_inc(cleared, 1)
                regs = [dve.alloc_register(f"attend_owner{r}") for r in range(2 * R)]

                def owner_of(place):
                    return dve.snap(regs[place], min_val=0, max_val=BUCKETS - 1)

                def sums_of(place):
                    return k.a_all[:, ds(owner_of(place) * AW, AW)].rearrange("p (h e) -> p h e", e=HD + 1)

                def body(st):
                    if st.real():
                        n, r = st.n(), st.slot()
                        dve.wait_ge(gathered[r], st.turn() * (16 * B) + 16 * B)
                        for j in range(2):
                            dve.wait_ge(queried, f.at(queried, n, j))
                            V.tensor_tensor(kv[r][:, 2 * j:2 * j + 2, 0:D], q_ps[:, j, :, :], kv[r][:, 2 * j:2 * j + 2, 0:D], ALU.mult).then_inc(multiplied, 1)
                    if st.real(-3):
                        r = st.slot(-3)
                        dve.wait_ge(dropped, f.at(dropped, st.n(-3)))
                        V.tensor_tensor(scaled_down[r % 2][:], sums_of(st.place(-3)), drop[r][:].unsqueeze(2).to_broadcast([P, HEADS, HD + 1]), ALU.mult)
                    if st.real(-1):
                        n, r = st.n(-1), st.slot(-1)
                        dve.wait_ge(r_turned, f.at(r_turned, n))
                        V.tensor_tensor(tops[r][:, :, 0:HEADS], run_ps[:, 0:ROWS].rearrange("p (t h) -> p t h", h=HEADS),
                                        T.last[:, ds(n * B, B)].unsqueeze(2).to_broadcast([P, B, HEADS]), ALU.mult)
                        V.tensor_copy(tops[r][:, :, HEADS], T.last[:, ds(n * B, B)])
                        dve.drain().then_inc(topped, 1)
                    else:
                        dve.drain()
                    if st.real(-2):
                        n, r = st.n(-2), st.slot(-2)
                        dve.wait_ge(brought, f.at(brought, n))
                        V.tensor_tensor(shift[r][:].rearrange("p t h -> p (t h)"), sg[r][:].rearrange("p t h -> p (t h)"),
                                        m_ps[:, 0:ROWS], ALU.subtract).then_inc(shifted, 1)
                        V.tensor_copy(k.m_all[:, ds(owner_of(st.place(-2)) * HEADS, HEADS)], mn[r][:])
                    if st.real():
                        r = st.slot()
                        V.tensor_reduce(sg[r][:].rearrange("p t h -> p (t h)"), kv[r][:, :, 0:D].rearrange("p t (h e) -> p t h e", e=HD),
                                        AX.X, ALU.add).then_inc(scored, 1)
                    if st.real(1) and st.place() in (R - 1, 2 * R - 1):
                        first = st.place(1)
                        dve.load(regs[first:first + R], T.owner[0:1, ds(st.n(1), R)])
                    if st.real(-3):
                        n, r = st.n(-3), st.slot(-3)
                        dve.wait_ge(summed, f.at(summed, n))
                        V.tensor_tensor(sums_of(st.place(-3)), scaled_down[r % 2][:], sum_ps[:, 0:AW].rearrange("p (h e) -> p h e", e=HD + 1), ALU.add).then_inc(added, 1)
                    at = top_ps[:, 0:B * (HEADS + 1)].rearrange("p (t h) -> p t h", h=HEADS + 1)
                    if st.real(-1):
                        n, r = st.n(-1), st.slot(-1)
                        dve.wait_ge(at_nodes, f.at(at_nodes, n))
                        V.tensor_scalar(absent[r][:], at[:, :, HEADS], -1.0, 0.0, ALU.add, ALU.min)
                    dve.drain()
                    if st.real(-1):
                        r = st.slot(-1)
                        V.scalar_tensor_tensor(out=mv[r][:], in0=absent[r][:].unsqueeze(2).to_broadcast([P, B, HEADS]), scalar=-NEG,
                                               in1=at[:, :, 0:HEADS], op0=ALU.mult, op1=ALU.add)
                        dve.drain()
                        V.tensor_reduce(gm[r][:], mv[r][:].rearrange("p t h -> p h t"), AX.X, ALU.max)
                    if st.real(-2):
                        n, r = st.n(-2), st.slot(-2)
                        dve.wait_ge(weighed, f.at(weighed, n))
                        dve.wait_ge(summed, f.at(summed, n, back=2))
                        weigh(V, r, 0, OWN).then_inc(half_scaled, 1)
                    if st.real(-1):
                        r = st.slot(-1)
                        m = k.m_all[:, ds(owner_of(st.place(-1)) * HEADS, HEADS)]
                        dve.drain()
                        V.tensor_tensor(mn[r][:], m, gm[r][:], ALU.max).then_inc(merged, 1)
                        dve.drain()
                        V.tensor_tensor(drop[r][:], m, mn[r][:], ALU.subtract).then_inc(fell, 1)
                    if st.real():
                        n, r = st.n(), st.slot()
                        dve.wait_ge(s_turned, f.at(s_turned, n))
                        dve.wait_ge(resets_in[r], st.turn() * 16 + 16)
                        V.tensor_tensor_scan(run[r][:], resets[r][:], sT_ps[0:ROWS, 0:P], NEG, ALU.add, ALU.max).then_inc(ran, 1)
                steps(dve, e.groups, 2 * R, 2, 3, body, ring=R)

            @block.scalar
            def _(act):
                A = nc.scalar
                reg = act.alloc_register("attend_q_owner")
                act.wait_ge(cleared, 1)

                def body(st):
                    if st.real(2):
                        n, r = st.n(2), st.slot(2)
                        act.wait_ge(rows_in[r], st.turn(2) * 16 + 16)
                        A.activation(apart[r % 2][:], dst_rows[r][:], ACT.Abs, bias=minus_p[:])
                        act.drain()
                        act.wait_ge(brought, f.at(brought, n, back=R))
                        A.activation(to_edge[r][:], apart[r % 2][:], ACT.Relu, bias=k.ones[:, 0:1], scale=-1.0).then_inc(hot, 1)
                    if st.real(-2):
                        n, r = st.n(-2), st.slot(-2)
                        act.wait_ge(shifted, f.at(shifted, n))
                        act.wait_ge(scaled, f.at(scaled, n, back=R))
                        act.wait_ge(half_scaled, f.at(half_scaled, n, back=R))
                        A.activation(ws[r][:], shift[r][:], ACT.Exp).then_inc(weighed, 1)
                    if st.real(2):
                        n, r = st.n(2), st.slot(2)
                        act.load([reg], T.owner[0:1, ds(n, 1)])
                        owner = act.snap(reg, min_val=0, max_val=BUCKETS - 1)
                        act.wait_ge(queried, f.at(queried, n, back=R))
                        A.copy(qs[r][:], k.q_all[:, ds(owner * D, D)]).then_inc(q_taken, 1)
                    if st.real(1):
                        n, r = st.n(1), st.slot(1)
                        act.wait_ge(hot_turned, f.at(hot_turned, n))
                        act.wait_ge(summed, f.at(summed, n, back=R))
                        A.copy(to_node[r][:].rearrange("p t n -> p (t n)"), hot_ps[:]).then_inc(hot_copied, 1)
                    if st.real(-1):
                        n, r = st.n(-1), st.slot(-1)
                        act.wait_ge(fell, f.at(fell, n))
                        A.activation(drop[r][:], drop[r][:], ACT.Exp).then_inc(dropped, 1)
                steps(act, e.groups, R, 2, 2, body)

            @block.tensor
            def _(pe):
                T_ = nc.tensor

                def bring_q(n, r, j):
                    pe.wait_ge(multiplied, f.at(multiplied, n, j, back=1))
                    for t in (2 * j, 2 * j + 1):
                        op = T_.matmul(q_ps[:, j, t % 2, :], to_edge[r][:, t * P:(t + 1) * P], qs[r][:], start=True, stop=True)
                    op.then_inc(queried, 1)

                def body(st):
                    if st.real(-1):
                        n, r = st.n(-1), st.slot(-1)
                        pe.wait_ge(topped, f.at(topped, n))
                        pe.wait_ge(fell, f.at(fell, n, back=1))
                        for t in range(B):
                            op = T_.matmul(top_ps[:, t * (HEADS + 1):(t + 1) * (HEADS + 1)], to_node[r][:, t, :], tops[r][:, t, :],
                                           start=True, stop=True)
                        op.then_inc(at_nodes, 1)
                    if st.real(1):
                        n, r = st.n(1), st.slot(1)
                        pe.wait_ge(hot, f.at(hot, n))
                        pe.wait_ge(q_taken, f.at(q_taken, n))
                        bring_q(n, r, 0)
                        bring_q(n, r, 1)
                    if st.real():
                        n, r = st.n(), st.slot()
                        pe.wait_ge(scored, f.at(scored, n))
                        pe.wait_ge(ran, f.at(ran, n, back=1))
                        pe.sem_inc(turns, 1)
                        T_.transpose(sT_ps[0:ROWS, 0:P], sg[r][:].rearrange("p t h -> p (t h)"), k.ident[:]).then_inc(s_turned, 1)
                    if st.real(1):
                        n, r = st.n(1), st.slot(1)
                        pe.wait_ge(hot_copied, f.at(hot_copied, n, back=1))
                        for t in range(B):
                            op = T_.transpose(hot_ps[:, t * P:(t + 1) * P], to_edge[r][:, t * P:(t + 1) * P], k.ident[:])
                        op.then_inc(hot_turned, 1)
                    if st.real(-1):
                        n, r = st.n(-1), st.slot(-1)
                        pe.wait_ge(merged, f.at(merged, n))
                        pe.wait_ge(shifted, f.at(shifted, n, back=1))
                        for t in range(B):
                            op = T_.matmul(m_ps[:, t * HEADS:(t + 1) * HEADS], to_edge[r][:, t * P:(t + 1) * P], mn[r][:], start=True, stop=True)
                        op.then_inc(brought, 1)
                    if st.real():
                        n, r = st.n(), st.slot()
                        pe.wait_ge(ran, f.at(ran, n))
                        pe.wait_ge(topped, f.at(topped, n, back=1))
                        pe.sem_inc(turns, 1)
                        T_.transpose(run_ps[:, 0:ROWS], run[r][:], k.ident[0:ROWS, 0:ROWS]).then_inc(r_turned, 1)
                    if st.real(-2):
                        n, r = st.n(-2), st.slot(-2)
                        pe.wait_ge(half_scaled, f.at(half_scaled, n))
                        pe.wait_ge(scaled, f.at(scaled, n))
                        pe.wait_ge(added, f.at(added, n, back=1))
                        for t in range(B):
                            op = T_.matmul(sum_ps[:, 0:AW], to_node[r][:, t, :], weighed_v[r % 2][:, t, :], start=(t == 0), stop=(t == B - 1))
                        op.then_inc(summed, 1)
                steps(pe, e.groups, R, 1, 2, body)


def row_of(w, l):
    return w[ds(l, 1), :].to_broadcast([P, w.shape[1]])


def finish_layer(nc, k, l, TG):
    FC = DFF // P
    PAIRS = NODE_TILES // 2
    with Phase(nc, "finish") as f:
        wo, w1, w2 = f.sb("wo", [P, 2, D]), f.sb("w1", [P, 2, DFF]), f.sb("w2", [P, FC, D])
        b1 = f.sb("b1", [P, FC])
        rows = {n: f.sb(n, [P, 2, D]) for n in ("bo", "g1", "s1", "b2", "g2", "s2")}
        den, at = f.pair("den", [P, 2, HEADS]), f.pair("at", [P, 2, D])
        aT = f.pair("aT", [P, 2, 2, P])
        xt, y, x1, y2, z = (f.pair(n, [P, 2, D]) for n in ("xt", "y", "x1", "y2", "z"))
        x1T, hT = f.pair("x1T", [P, 2, 2, P]), f.sb("hT", [P, FC, 2 * P])
        norm1, norm2 = PairNorm(nc, k, f, "norm1"), PairNorm(nc, k, f, "norm2")
        scatter = Scatter(nc, f, GAT, TG, BY_PAIR)
        turn_ps = f.ps("turn_ps", [P, 2, 2, D])
        aT_ps = turn_ps[:, :, 0, :].rearrange("p g (c n) -> p g c n", n=P)
        o_ps = turn_ps[:, :, 1, :]
        h_ps = f.ps("h_ps", [P, FC, 2 * P])
        y_ps = f.ps("y_ps", [P, 2, 512])
        weights, loaded, stored = f.dma_sem("weights"), f.dma_pair("loaded"), f.store_pair("stored")
        divided, a_turned, a_copied, projected, attended = (
            f.sem(x) for x in ("divided", "a_turned", "a_copied", "projected", "attended"))
        x_ready, x_turned, x_copied, contracted, finished, read = (
            f.sem(x) for x in ("x_ready", "x_turned", "x_copied", "contracted", "finished", "read"))
        hidden, activated = f.sem("hidden", FC // 2), f.sem("activated", FC // 2)
        f.start()
        with nc.Block() as block:
            @block.sync
            def _(sp):
                one = ds(l, 1)
                for to, of in ((wo[:], k.Wo[one, :, :].rearrange("a (c p) n -> p (a c) n", p=P)),
                               (w1[:], k.w1[one, :, :].rearrange("a (c p) n -> p (a c) n", p=P)),
                               (w2[:], k.w2[one, :, :].rearrange("a (c p) n -> p (a c) n", p=P))):
                    sp.dma_start(to, of).then_inc(weights, 16)
                with nc.allow_non_contiguous_dma(reason="1024 words"):
                    sp.dma_start(b1[:], k.b1[one, :].rearrange("a (c p) -> p (a c)", p=P)).then_inc(weights, 16)
                for n, w in (("bo", k.bo), ("g1", k.ln1_g), ("s1", k.ln1_b), ("b2", k.b2), ("g2", k.ln2_g), ("s2", k.ln2_b)):
                    for g in range(2):
                        sp.dma_start(rows[n][:, g, :], row_of(w, l)).then_inc(weights, 16)

                def body(st):
                    n, r = st.n(), st.slot()
                    sp.wait_ge(attended, f.at(attended, n, back=2))
                    sp.dma_start(xt[r][:], pair_of(k.X, n)).then_inc(loaded[r], 16)
                    scatter.stage(sp, r, st.turn(), (l * PAIRS + n) * BY_PAIR + BY_TILES)
                steps(sp, PAIRS, 2, 0, 0, body)

            @block.gpsimd
            def _(pool):
                def body(st):
                    if st.real(1):
                        norm1.root(pool, st.slot(1), st.n(1))
                    if st.real():
                        scatter.write(pool, st.slot(), st.turn())
                        norm2.root(pool, st.slot(), st.n())
                steps(pool, PAIRS, 2, 1, 0, body)
                scatter.finish(pool, PAIRS // 2)

            @block.vector
            def _(dve):
                V = nc.vector
                dve.wait_ge(weights, 16 * 16)

                def body(st):
                    if st.real(1):
                        n, r = st.n(1), st.slot(1)
                        dve.wait_ge(loaded[r], st.turn(1) * 16 + 16)
                        V.tensor_tensor(xt[r][:], xt[r][:], rows["bo"][:], ALU.add)
                        dve.drain()
                        dve.wait_ge(projected, f.at(projected, n))
                        V.tensor_tensor(y[r][:], o_ps, xt[r][:], ALU.add).then_inc(attended, 1)
                        dve.drain()
                        norm1.moments(dve, r, y[r])
                        norm1.apply(dve, r, n, x1[r], y[r])
                        dve.drain()
                        V.tensor_tensor(x1[r][:], x1[r][:], rows["g1"][:], ALU.mult)
                        dve.drain()
                        V.tensor_tensor(x1[r][:], x1[r][:], rows["s1"][:], ALU.add).then_inc(x_ready, 1)
                        dve.drain()
                        V.tensor_tensor(y2[r][:], x1[r][:], rows["b2"][:], ALU.add)
                        dve.drain()
                    if st.real(2):
                        n, r = st.n(2), st.slot(2)
                        sums = k.a_all[:, ds(n * 2 * AW, 2 * AW)].rearrange("p (x e) -> p x e", e=HD + 1)
                        V.tensor_single_scalar(den[r][:].rearrange("p g h -> p (g h)"), sums[:, :, HD], 1e-10, op=ALU.add)
                        dve.drain()
                        V.reciprocal(den[r][:], den[r][:])
                        dve.drain()
                        dve.wait_ge(a_turned, f.at(a_turned, n, back=2))
                        V.tensor_tensor(at[r][:].rearrange("p g (h e) -> p (g h) e", e=HD), sums[:, :, 0:HD],
                                        den[r][:].rearrange("p g h -> p (g h)").unsqueeze(2).to_broadcast([P, 2 * HEADS, HD]), ALU.mult).then_inc(divided, 1)
                    if st.real():
                        n, r = st.n(), st.slot()
                        dve.wait_ge(contracted, f.at(contracted, n))
                        V.tensor_tensor(y2[r][:], y_ps[:, :, 0:D], y2[r][:], ALU.add).then_inc(read, 1)
                        dve.drain()
                        norm2.moments(dve, r, y2[r])
                        dve.wait_ge(stored[r], st.turn() * 16 + 16)
                        norm2.apply(dve, r, n, z[r], y2[r])
                        dve.drain()
                        V.tensor_tensor(z[r][:], z[r][:], rows["g2"][:], ALU.mult)
                        dve.drain()
                        V.tensor_tensor(z[r][:], z[r][:], rows["s2"][:], ALU.add).then_inc(finished, 1)
                steps(dve, PAIRS, 2, 2, 0, body)

            @block.tensor
            def _(pe):
                T = nc.tensor
                pe.wait_ge(weights, 16 * 16)

                def turn_x(n, r):
                    pe.wait_ge(x_ready, f.at(x_ready, n))
                    for g in range(2):
                        for half in range(2):
                            op = T.transpose(aT_ps[:, g, half, :], x1[r][:, g, half * P:(half + 1) * P], k.ident[:])
                    op.then_inc(x_turned, 1)

                def body(st):
                    if st.real(1):
                        n, r = st.n(1), st.slot(1)
                        pe.wait_ge(divided, f.at(divided, n))
                        pe.wait_ge(x_copied, f.at(x_copied, n, back=1))
                        for g in range(2):
                            for half in range(2):
                                op = T.transpose(aT_ps[:, g, half, :], at[r][:, g, half * P:(half + 1) * P], k.ident[:])
                        op.then_inc(a_turned, 1)
                    if st.real():
                        n, r = st.n(), st.slot()
                        pe.wait_ge(x_copied, f.at(x_copied, n))
                        for c in range(FC):
                            if c % 2 == 0:
                                pe.wait_ge(activated, f.at(activated, n, c // 2, back=1))
                            for half in range(2):
                                op = T.matmul(h_ps[:, c, :], w1[:, half, c * P:(c + 1) * P], x1T[r][:, half, :, :].rearrange("p g n -> p (g n)"),
                                              start=(half == 0), stop=(half == 1))
                            if c % 2:
                                op.then_inc(hidden, 1)
                    if st.real(1):
                        n, r = st.n(1), st.slot(1)
                        pe.wait_ge(a_copied, f.at(a_copied, n))
                        for g in range(2):
                            for half in range(2):
                                op = T.matmul(o_ps[:, g, :], aT[r][:, g, half, :], wo[:, half, :], start=(half == 0), stop=(half == 1))
                        op.then_inc(projected, 1)
                    if st.real():
                        n, r = st.n(), st.slot()
                        pe.wait_ge(read, f.at(read, n, back=1))
                        for g in range(2):
                            for c in range(FC):
                                if g == 0 and c % 2 == 0:
                                    pe.wait_ge(activated, f.at(activated, n, c // 2))
                                if (g, c) == (1, FC // 2) and st.real(1):
                                    turn_x(st.n(1), st.slot(1))
                                op = T.matmul(y_ps[:, g, 0:D], hT[:, c, g * P:(g + 1) * P], w2[:, c, :], start=(c == 0), stop=(c == FC - 1))
                        op.then_inc(contracted, 1)
                    elif st.real(1):
                        turn_x(st.n(1), st.slot(1))
                steps(pe, PAIRS, 2, 1, 0, body)

            @block.scalar
            def _(act):
                A = nc.scalar
                act.wait_ge(weights, 16 * 16)

                def body(st):
                    if st.real(1):
                        n, r = st.n(1), st.slot(1)
                        act.wait_ge(a_turned, f.at(a_turned, n))
                        act.wait_ge(projected, f.at(projected, n, back=2))
                        A.copy(aT[r][:], aT_ps).then_inc(a_copied, 1)
                    if st.real():
                        n = st.n()
                        act.wait_ge(contracted, f.at(contracted, n, back=1))
                        for c in range(FC):
                            if c % 2 == 0:
                                act.wait_ge(hidden, f.at(hidden, n, c // 2))
                            A.activation(hT[:, c, :], h_ps[:, c, :], ACT.Gelu, bias=b1[:, c:c + 1])
                            if c % 2:
                                act.drain().then_inc(activated, 1)
                    if st.real(1):
                        n, r = st.n(1), st.slot(1)
                        act.wait_ge(x_turned, f.at(x_turned, n))
                        act.wait_ge(hidden, f.at(hidden, n, back=2))
                        A.copy(x1T[r][:].rearrange("p a g n -> p g a n"), aT_ps).then_inc(x_copied, 1)
                    if st.real():
                        n, r = st.n(), st.slot()
                        act.wait_ge(finished, f.at(finished, n))
                        act.dma_start(pair_of(k.X, n), z[r][:]).then_inc(stored[r], 16)
                steps(act, PAIRS, 2, 1, 0, body)
                for r in range(2):
                    act.wait_ge(stored[r], 16 * (PAIRS // 2) + 16)


def route_inputs(nc, k):
    PAIRS = NODE_TILES // 2
    ROW = GW + GH
    with Phase(nc, "inputs") as f:
        wg = f.sb("wg", [P, 2, GW])
        att = f.sb("att", [P, 2, GW])
        og, ob = f.sb("og", [P, D]), f.sb("ob", [P, D])
        xt, x0, y, x2, xn = (f.pair(n, [P, D]) for n in ("xt", "x0", "y", "x2", "xn"))
        xT, tab, prod = f.pair("xT", [P, 2, P]), f.pair("tab", [P, ROW]), f.pair("prod", [P, 2, GW])
        norm1, norm2 = Norm(nc, k, f, "norm1"), Norm(nc, k, f, "norm2")
        xT_ps, h_ps = f.ps("xT_ps", [P, 2, 4, P]), f.ps("h_ps", [P, 2, 512])
        weights, loaded = f.dma_sem("weights"), f.dma_pair("loaded")
        stored = f.store_pair("stored")
        ready, normed, turned, copied, product, tabled = (f.sem(x) for x in ("ready", "normed", "turned", "copied", "product", "tabled"))
        f.start()
        with nc.Block() as block:
            @block.sync
            def _(sp):
                sp.dma_start(wg[:], k.W_gat.rearrange("(c p) n -> p c n", p=P)).then_inc(weights, 16)
                for n, w in enumerate((k.att_src, k.att_dst)):
                    sp.dma_start(att[:, n, :], w.rearrange("(a h) e -> a (h e)", a=1).to_broadcast([P, GW])).then_inc(weights, 16)
                sp.dma_start(og[:], k.out_g.rearrange("(a n) -> a n", a=1).to_broadcast([P, D])).then_inc(weights, 16)
                sp.dma_start(ob[:], k.out_b.rearrange("(a n) -> a n", a=1).to_broadcast([P, D])).then_inc(weights, 16)
                with sp.Fori(0, PAIRS, 1) as i:
                    for g in range(2):
                        s = i * 2 + g
                        sp.wait_ge(ready, s + 1)
                        sp.dma_start(xt[g][:], rows_of(k.X, s)).then_inc(loaded[g], 16)
                        sp.dma_start(x0[g][:], rows_of(k.XP, s)).then_inc(loaded[g], 16)

            @block.gpsimd
            def _(pool):
                with pool.Fori(0, PAIRS, 1) as i:
                    for norm in (norm1, norm2):
                        for g in range(2):
                            norm.root(pool, g, i * 2 + g)

            @block.vector
            def _(dve):
                V = nc.vector
                dve.wait_ge(weights, 16 * 5)
                with dve.Fori(0, PAIRS, 1) as i:
                    for g in range(2):
                        dve.wait_ge(loaded[g], i * 32 + 32)
                        norm1.moments(dve, g, xt[g][:])
                    for g in range(2):
                        norm1.apply(dve, g, i * 2 + g, y[g][:], xt[g][:])
                    dve.drain()
                    for g in range(2):
                        V.tensor_tensor(y[g][:], y[g][:], og[:], ALU.mult)
                    dve.drain()
                    for g in range(2):
                        V.tensor_tensor(y[g][:], y[g][:], ob[:], ALU.add)
                    dve.drain()
                    for g in range(2):
                        dve.wait_ge(stored[g], i * 48 + 16)
                        V.tensor_tensor(x2[g][:], y[g][:], x0[g][:], ALU.add).then_inc(ready, 1)
                    dve.drain()
                    for g in range(2):
                        norm2.moments(dve, g, x2[g][:])
                    for g in range(2):
                        norm2.apply(dve, g, i * 2 + g, xn[g][:], x2[g][:])
                        dve.drain().then_inc(normed, 1)
                    for g in range(2):
                        s = i * 2 + g
                        dve.wait_ge(product, s + 1 + CREDIT)
                        V.tensor_copy(tab[g][:, 0:GW], h_ps[:, g, 0:GW])
                    dve.drain()
                    for g in range(2):
                        V.tensor_tensor(prod[g][:], tab[g][:, 0:GW].unsqueeze(1).to_broadcast([P, 2, GW]), att[:], ALU.mult)
                    dve.drain()
                    for g in range(2):
                        s = i * 2 + g
                        pr = prod[g][:].rearrange("p a (h e) -> p a h e", e=EXPERTS)
                        V.tensor_reduce(tab[g][:, GW:ROW], pr[:, 0, :, :], AX.X, ALU.add)
                        V.tensor_reduce(k.dst_term[:, ds(s * GH, GH)], pr[:, 1, :, :], AX.X, ALU.add)
                    dve.drain()
                    for g in range(2):
                        s = i * 2 + g
                        V.tensor_copy(k.h_all[:, ds(s * ROW, ROW)], tab[g][:])
                    dve.drain().then_inc(tabled, 1)

            @block.tensor
            def _(pe):
                T = nc.tensor
                pe.wait_ge(weights, 16 * 5)
                with pe.Fori(0, PAIRS, 1) as i:
                    for g in range(2):
                        s = i * 2 + g
                        pe.wait_ge(normed, s + 1 + CREDIT)
                        pe.wait_ge(copied, s + 1)
                        for half in range(2):
                            op = T.transpose(xT_ps[:, g, half, :], xn[g][:, half * P:(half + 1) * P], k.ident[:])
                        op.then_inc(turned, 1)
                    for g in range(2):
                        s = i * 2 + g
                        pe.wait_ge(copied, s + 1 + CREDIT)
                        pe.wait_ge(tabled, i + CREDIT)
                        for half in range(2):
                            op = T.matmul(h_ps[:, g, 0:GW], xT[g][:, half, :], wg[:, half, :], start=(half == 0), stop=(half == 1))
                        op.then_inc(product, 1)

            @block.scalar
            def _(act):
                with act.Fori(0, PAIRS, 1) as i:
                    for g in range(2):
                        s = i * 2 + g
                        act.wait_ge(turned, s + 1 + CREDIT)
                        act.wait_ge(product, s + 1)
                        nc.scalar.copy(xT[g][:], xT_ps[:, g, 0:2, :]).then_inc(copied, 1)
                    act.wait_ge(tabled, i + 1 + CREDIT)
                    for g in range(2):
                        s = i * 2 + g
                        act.dma_start(rows_of(k.X2, s), x2[g][:]).then_inc(stored[g], 16)
                        act.dma_start(rows_of(k.XN, s), xn[g][:]).then_inc(stored[g], 16)
                        act.dma_start(rows_of(k.HT, s), tab[g][:]).then_inc(stored[g], 16)
                for g in range(2):
                    act.wait_ge(stored[g], 48 * PAIRS + 16)


def route_maxima(nc, k, T):
    e, ROW = GAT, GW + GH
    PAIRS = G // 2
    R = 4
    with Phase(nc, "maxima", R) as f:
        def ring(name, shape, dt=F32):
            return [f.sb(f"{name}{r}", shape, dt) for r in range(R)]

        stage = ring("stage", [P, G], I32)
        gb = ring("gb", [P, G, ROW])
        dst_rows, other = ring("dst_rows", [P, G * P], BF16), ring("other", [P, G, P], BF16)
        ident = f.sb("ident", [P, P], BF16)
        mt, mp = ring("mt", [P, PAIRS, 2, GH]), ring("mp", [P, PAIRS, GH])
        spread_ps = f.ps("spread_ps", [P, G, GH * P])
        staged, gathered, rows_in = ([f.dma_sem(f"{n}{r}") for r in range(R)] for n in ("staged", "gathered", "rows_in"))
        go = f.sem("go")
        compared, kept, ready = f.sem("compared"), f.sem("kept"), f.dma_sem("ready")
        spread, reduced = f.sem("spread", G), f.sem("reduced", G)
        f.start()
        with nc.Block() as block:
            @block.sync
            def _(sp):
                def body(st):
                    s, r = st.n(), st.slot()
                    sp.wait_ge(kept, f.at(kept, s, back=R))
                    sp.dma_start(stage[r][:], T.idx_v[:, ds(s * G, G)]).then_inc(staged[r], 16)
                    sp.wait_ge(compared, f.at(compared, s, back=R))
                    sp.dma_start(dst_rows[r][:], T.rows[ds(s * G, G), :].rearrange("(a t) e -> a (t e)", a=1)
                                 .to_broadcast([P, G * P])).then_inc(rows_in[r], 16)
                steps(sp, 2 * e.steps, R, 0, 0, body)

            @block.gpsimd
            def _(pool):
                def body(st):
                    s, r = st.n(), st.slot()
                    pool.wait_ge(staged[r], st.turn() * 16 + 16)
                    pool.sem_inc(go, 1)
                    pool.wait_ge(spread, f.at(spread, s, back=R))
                    pool.sem_inc(go, 1)
                    pool.wait_ge(kept, f.at(kept, s, back=R))
                    pool.sem_inc(go, 1)
                    for t in range(G):
                        pool.indirect_dma_start(out=gb[r][:, t, :], out_offset=None, in_=k.HT,
                                                in_offset=bass.IndirectOffsetOnAxis(ap=stage[r][:, t:t + 1], axis=0)
                                                ).then_inc(gathered[r], 16)
                steps(pool, 2 * e.steps, R, 0, 0, body)

            @block.vector
            def _(dve):
                V = nc.vector
                V.tensor_copy(k.gm_all[:].rearrange("p (n h) -> p n h", h=GH),
                              k.h_all[:].rearrange("p (n r) -> p n r", r=ROW)[:, :, GW:ROW])
                V.tensor_copy(ident[:], k.ident[:]).then_inc(ready, 1)
                dve.drain()
                regs = [[dve.alloc_register(f"max_owner{r}_{t}") for t in range(PAIRS)] for r in range(R)]

                def body(st):
                    if st.real():
                        n, r = st.n(), st.slot()
                        load_owners(dve, T.owner, n, regs[r])
                        for t in range(G):
                            dve.wait_ge(spread, f.at(spread, n, t))
                            V.tensor_reduce(mt[r][:, t // 2, t % 2, :], spread_ps[:, t, :].rearrange("p (h e) -> p h e", e=P),
                                            AX.X, ALU.max).then_inc(reduced, 1)
                    if st.real(2):
                        n, r = st.n(2), st.slot(2)
                        dve.wait_ge(rows_in[r], st.turn(2) * 16 + 16)
                        dve.wait_ge(spread, f.at(spread, n, back=R))
                        V.tensor_scalar(other[r][:].rearrange("p t e -> p (t e)"), dst_rows[r][:], k.iota_p[:], NEG,
                                        ALU.not_equal, ALU.mult).then_inc(compared, 1)
                    if st.real():
                        r = st.slot()
                        dve.drain()
                        V.tensor_tensor(mp[r][:], mt[r][:, :, 0, :], mt[r][:, :, 1, :], ALU.max)
                        for t in range(PAIRS):
                            owner = dve.snap(regs[r][t], min_val=0, max_val=BUCKETS - 1)
                            m = k.gm_all[:, ds(owner * GH, GH)]
                            dve.drain()
                            V.tensor_tensor(m, m, mp[r][:, t, :], ALU.max)
                steps(dve, 2 * e.steps, R, 2, 0, body)

            @block.scalar
            def _(act):
                def body(st):
                    n, r = st.n(), st.slot()
                    act.wait_ge(gathered[r], st.turn() * (16 * G) + 16 * G)
                    nc.scalar.copy(k.g_all[:, ds(n * G * ROW, G * ROW)], gb[r][:].rearrange("p t r -> p (t r)")).then_inc(kept, 1)
                steps(act, 2 * e.steps, R, 0, 0, body)

            @block.tensor
            def _(pe):
                pe.wait_ge(ready, 1)

                def body(st):
                    n, r = st.n(), st.slot()
                    pe.wait_ge(compared, f.at(compared, n))
                    pe.wait_ge(gathered[r], st.turn() * (16 * G) + 16 * G)
                    for t in range(G):
                        pe.wait_ge(reduced, f.at(reduced, n, t, back=1))
                        nc.tensor.matmul(spread_ps[:, t, :].rearrange("p (h e) -> p h e", e=P), ident[:],
                                         other[r][:, t, :].unsqueeze(1).to_broadcast([P, GH, P]), start=True, stop=False)
                        for h in range(GH):
                            op = nc.tensor.matmul(spread_ps[:, t, h * P:(h + 1) * P],
                                                  gb[r][:, t, GW + h:GW + h + 1].to_broadcast([P, P]), k.ident[:], start=False, stop=(h == GH - 1))
                        op.then_inc(spread, 1)
                steps(pe, 2 * e.steps, R, 0, 0, body)


def route_sums(nc, k, T):
    e, ROW, ALL = GAT, GW + GH, NODE_TILES
    PAIRS = G // 2
    R = 4
    with Phase(nc, "route", R) as f:
        def ring(name, shape, dt=F32):
            return [f.sb(f"{name}{r}", shape, dt) for r in range(R)]

        dst_rows = ring("dst_rows", [P, G * P], BF16)
        to_node, to_edge = ring("to_node", [P, G, P]), ring("to_edge", [P, G * P], BF16)
        parts = f.sb("parts", [P, ALL, 3, 2 * GH], BF16)
        left = f.sb("left", [P, ALL, 2 * GH])
        own = f.sb("own", [P, ALL, GH])
        tmp = f.sb("tmp", [P, ALL, GH])
        terms = ring("terms", [P, G, GH])
        wv = ring("wv", [P, G, ROW])
        back_ps, sum_ps = f.ps("back_ps", [P, 512]), f.ps("sum_ps", [P, 512])
        rows_in, split = [f.dma_sem(f"rows_in{r}") for r in range(R)], f.dma_sem("split")
        own_ready, own_exp, hot, fetched, formed, weighed, scaled, summed, added = (
            f.sem(x) for x in ("own_ready", "own_exp", "hot", "fetched", "formed", "weighed", "scaled", "summed", "added"))
        both = k.t2_all[:].rearrange("p (n x) -> p n x", x=2 * GH)
        h_rows = k.h_all[:].rearrange("p (n r) -> p n r", r=ROW)
        f.start()
        with nc.Block() as block:
            @block.sync
            def _(sp):
                def body(st):
                    s, r = st.n(), st.slot()
                    sp.wait_ge(hot, f.at(hot, s, back=R))
                    sp.dma_start(dst_rows[r][:], T.rows[ds(s * G, G), :].rearrange("(a t) e -> a (t e)", a=1)
                                 .to_broadcast([P, G * P])).then_inc(rows_in[r], 16)
                steps(sp, 2 * e.steps, R, 0, 0, body)

            @block.vector
            def _(dve):
                V = nc.vector

                def leaky(out, tmp_, x):
                    V.tensor_single_scalar(tmp_, x, 0.2, op=ALU.mult)
                    dve.drain()
                    V.tensor_tensor(out, x, tmp_, ALU.max)
                    dve.drain()

                dst = k.dst_term[:].rearrange("p (n h) -> p n h", h=GH)
                top = k.gm_all[:].rearrange("p (n h) -> p n h", h=GH)
                V.tensor_copy(both[:, :, 0:GH], dst)
                V.tensor_tensor(top, top, dst, ALU.add)
                dve.drain()
                leaky(both[:, :, GH:2 * GH], tmp[:], top)
                V.tensor_tensor(own[:], h_rows[:, :, GW:ROW], dst, ALU.add)
                dve.drain()
                leaky(own[:], tmp[:], own[:])
                V.tensor_tensor(own[:], own[:], both[:, :, GH:2 * GH], ALU.subtract)
                dve.drain().then_inc(own_ready, 1)
                V.tensor_copy(parts[:, :, 0, :], both)
                dve.drain()
                V.tensor_tensor(left[:], both, parts[:, :, 0, :], ALU.subtract)
                dve.drain()
                V.tensor_copy(parts[:, :, 1, :], left[:])
                dve.drain()
                V.tensor_tensor(left[:], left[:], parts[:, :, 1, :], ALU.subtract)
                dve.drain()
                V.tensor_copy(parts[:, :, 2, :], left[:])
                dve.drain().then_inc(split, 1)
                dve.wait_ge(own_exp, 1 + R)
                sums = k.gs_all[:].rearrange("p (n r) -> p n r", r=ROW)
                V.tensor_copy(sums[:, :, GW:ROW], own[:])
                V.tensor_tensor(sums[:, :, 0:GW].rearrange("p n (h x) -> p n h x", x=EXPERTS),
                                h_rows[:, :, 0:GW].rearrange("p n (h x) -> p n h x", x=EXPERTS),
                                own[:].unsqueeze(3).to_broadcast([P, ALL, GH, EXPERTS]), ALU.mult)
                dve.drain()
                regs = [[dve.alloc_register(f"route_owner{r}_{t}") for t in range(PAIRS)] for r in range(R)]

                def body(st):
                    if st.real():
                        n, r = st.n(), st.slot()
                        dve.wait_ge(fetched, f.at(fetched, n))
                        rows = k.g_all[:, ds(n * G * ROW, G * ROW)].rearrange("p (t r) -> p t r", r=ROW)
                        back = back_ps[:, 0:G * 2 * GH].rearrange("p (t x) -> p t x", x=2 * GH)
                        t_ = terms[r]
                        V.tensor_tensor(t_[:], rows[:, :, GW:ROW], back[:, :, 0:GH], ALU.add)
                        dve.drain()
                        V.scalar_tensor_tensor(out=t_[:], in0=t_[:], scalar=0.2, in1=t_[:], op0=ALU.mult, op1=ALU.max)
                        dve.drain()
                        V.tensor_tensor(t_[:], t_[:], back[:, :, GH:2 * GH], ALU.subtract).then_inc(formed, 1)
                    if st.real(1):
                        n, r = st.n(1), st.slot(1)
                        dve.wait_ge(rows_in[r], st.turn(1) * 16 + 16)
                        dve.wait_ge(summed, f.at(summed, n, back=R))
                        one_hots(nc, k, dve, T, n, r, dst_rows, to_node, to_edge)
                        load_owners(dve, T.owner, n, regs[r])
                        dve.drain().then_inc(hot, 1)
                    if st.real():
                        n, r = st.n(), st.slot()
                        dve.wait_ge(weighed, f.at(weighed, n))
                        V.tensor_tensor(wv[r][:, :, 0:GW].rearrange("p t (h x) -> p t h x", x=EXPERTS),
                                        rows[:, :, 0:GW].rearrange("p t (h x) -> p t h x", x=EXPERTS),
                                        wv[r][:, :, GW:ROW].unsqueeze(3).to_broadcast([P, G, GH, EXPERTS]), ALU.mult).then_inc(scaled, 1)
                    if st.real(-1):
                        n, r = st.n(-1), st.slot(-1)
                        dve.wait_ge(summed, f.at(summed, n))
                        for t in range(PAIRS):
                            owner = dve.snap(regs[r][t], min_val=0, max_val=BUCKETS - 1)
                            a = k.gs_all[:, ds(owner * ROW, ROW)]
                            V.tensor_tensor(a, a, sum_ps[:, t * ROW:(t + 1) * ROW], ALU.add)
                            if t == PAIRS - 1:
                                dve.drain().then_inc(added, 1)
                            else:
                                dve.drain()
                steps(dve, 2 * e.steps, R, 1, 1, body)

            @block.scalar
            def _(act):
                act.wait_ge(own_ready, 1 + R)
                nc.scalar.activation(own[:], own[:], ACT.Exp).then_inc(own_exp, 1)

                def body(st):
                    n, r = st.n(), st.slot()
                    act.wait_ge(formed, f.at(formed, n))
                    act.wait_ge(summed, f.at(summed, n, back=R))
                    nc.scalar.activation(wv[r][:, :, GW:ROW], terms[r][:], ACT.Exp).then_inc(weighed, 1)
                steps(act, 2 * e.steps, R, 0, 0, body)

            @block.tensor
            def _(pe):
                regs = [[pe.alloc_register(f"route_fetch_owner{r}_{t}") for t in range(PAIRS)] for r in range(2)]
                pe.wait_ge(split, 1)

                def body(st):
                    if st.real(1):
                        n, r = st.n(1), st.slot(1)
                        pe.wait_ge(hot, f.at(hot, n))
                        pe.wait_ge(formed, f.at(formed, n, back=1))
                        for t in range(G):
                            owner = pe.snap(regs[r % 2][t // 2], min_val=0, max_val=BUCKETS - 1)
                            for part in range(3):
                                op = nc.tensor.matmul(back_ps[:, t * 2 * GH:(t + 1) * 2 * GH], to_edge[r][:, t * P:(t + 1) * P],
                                                      parts[:, ds(owner, 1), part, :].rearrange("p a x -> p (a x)"),
                                                      start=(part == 0), stop=(part == 2))
                        op.then_inc(fetched, 1)
                    if st.real():
                        n, r = st.n(), st.slot()
                        pe.wait_ge(scaled, f.at(scaled, n))
                        pe.wait_ge(added, f.at(added, n, back=1))
                        for t in range(G):
                            op = nc.tensor.matmul(sum_ps[:, t // 2 * ROW:(t // 2 + 1) * ROW], to_node[r][:, t, :], wv[r][:, t, :],
                                                  start=(t % 2 == 0), stop=(t % 2 == 1))
                        op.then_inc(summed, 1)
                    if st.real(2):
                        load_owners(pe, T.owner, st.n(2), regs[st.slot(2) % 2])
                steps(pe, 2 * e.steps, R, 2, 0, body)


def route_gates(nc, k):
    ROW, ALL = GW + GH, NODE_TILES
    with Phase(nc, "gates") as f:
        bg, gam, bet = (f.sb(n, [P, GW]) for n in ("bg", "gam", "bet"))
        agg, dev, sq = (f.sb(n, [P, ALL, GW]) for n in ("agg", "dev", "sq"))
        den = f.sb("den", [P, ALL, GH])
        mean, var, rstd, top, tot = (f.sb(n, [P, ALL]) for n in ("mean", "var", "rstd", "top", "tot"))
        sc, rank, cmp = (f.sb(n, [P, ALL, EXPERTS]) for n in ("sc", "rank", "cmp"))
        eq = f.sb("eq", [P, ALL])
        weights, var_ready, rooted, shifted, exps = f.dma_sem("weights"), f.sem("var_ready"), f.sem("rooted"), f.sem("shifted"), f.sem("exps")
        gates = k.gates[:].rearrange("p (n x) -> p n x", x=EXPERTS)
        f.start()
        with nc.Block() as block:
            @block.sync
            def _(sp):
                for to, of in ((bg, k.b_gat), (gam, k.ln_gamma), (bet, k.ln_beta)):
                    sp.dma_start(to[:], of.rearrange("(a n) -> a n", a=1).to_broadcast([P, GW])).then_inc(weights, 16)

            @block.gpsimd
            def _(pool):
                pool.wait_ge(var_ready, 1 + CREDIT)
                nc.gpsimd.tensor_tensor(rstd[:], var[:], k.power[:].to_broadcast([P, ALL]), ALU.pow).then_inc(rooted, 1)

            @block.scalar
            def _(act):
                act.wait_ge(shifted, 1 + CREDIT)
                nc.scalar.activation(cmp[:], cmp[:], ACT.Exp).then_inc(exps, 1)

            @block.vector
            def _(dve):
                V = nc.vector
                sums = k.gs_all[:].rearrange("p (n r) -> p n r", r=ROW)

                def step(op):
                    dve.drain()

                def wide(row):
                    return row[:].unsqueeze(1).to_broadcast([P, ALL, GW])

                def along(x, n):
                    return x[:].unsqueeze(2).to_broadcast([P, ALL, n])

                dve.wait_ge(weights, 48)
                step(V.tensor_single_scalar(den[:], sums[:, :, GW:ROW], 1e-16, op=ALU.add))
                step(V.reciprocal(den[:], den[:]))
                step(V.tensor_tensor(agg[:].rearrange("p n (h x) -> p n h x", x=EXPERTS),
                                     sums[:, :, 0:GW].rearrange("p n (h x) -> p n h x", x=EXPERTS),
                                     den[:].unsqueeze(3).to_broadcast([P, ALL, GH, EXPERTS]), ALU.mult))
                step(V.tensor_tensor(agg[:], agg[:], wide(bg), ALU.add))
                step(V.tensor_reduce(mean[:], agg[:], AX.X, ALU.add))
                step(V.tensor_single_scalar(mean[:], mean[:], 1.0 / GW, op=ALU.mult))
                step(V.tensor_tensor(dev[:], agg[:], along(mean, GW), ALU.subtract))
                step(V.tensor_tensor(sq[:], dev[:], dev[:], ALU.mult))
                step(V.tensor_reduce(var[:], sq[:], AX.X, ALU.add))
                V.tensor_scalar(var[:], var[:], 1.0 / GW, 1e-5, ALU.mult, ALU.add).then_inc(var_ready, 1)
                dve.wait_ge(rooted, 1 + CREDIT)
                step(V.tensor_tensor(dev[:], dev[:], along(rstd, GW), ALU.mult))
                step(V.tensor_tensor(dev[:], dev[:], wide(gam), ALU.mult))
                step(V.tensor_tensor(dev[:], dev[:], wide(bet), ALU.add))
                step(V.tensor_reduce(sc[:], dev[:].rearrange("p n (h x) -> p n x h", x=EXPERTS), AX.X, ALU.add))
                step(V.tensor_single_scalar(sc[:], sc[:], 1.0 / GH, op=ALU.mult))
                V.memset(rank[:], 0.0)
                for j in range(EXPERTS):
                    step(V.tensor_tensor(cmp[:], sc[:, :, j:j + 1].to_broadcast([P, ALL, EXPERTS]), sc[:], ALU.is_gt))
                    step(V.tensor_tensor(rank[:], rank[:], cmp[:], ALU.add))
                for i_ in range(1, EXPERTS):
                    for j in range(i_):
                        step(V.tensor_tensor(eq[:], sc[:, :, j], sc[:, :, i_], ALU.is_equal))
                        step(V.tensor_tensor(rank[:, :, i_], rank[:, :, i_], eq[:], ALU.add))
                step(V.tensor_single_scalar(rank[:], rank[:], 1.5, op=ALU.is_lt))
                step(V.tensor_reduce(top[:], sc[:], AX.X, ALU.max))
                V.tensor_tensor(cmp[:], sc[:], along(top, EXPERTS), ALU.subtract).then_inc(shifted, 1)
                dve.wait_ge(exps, 1 + CREDIT)
                step(V.tensor_tensor(cmp[:], cmp[:], rank[:], ALU.mult))
                step(V.tensor_reduce(tot[:], cmp[:], AX.X, ALU.add))
                step(V.reciprocal(tot[:], tot[:]))
                step(V.tensor_tensor(gates, cmp[:], along(tot, EXPERTS), ALU.mult))


def experts(nc, k):
    PAIRS, MC = NODE_TILES // 2, MF // P
    with Phase(nc, "experts") as f:
        w1, w2 = f.sb("w1", [P, EXPERTS, 2, MF]), f.sb("w2", [P, EXPERTS, MC, D])
        b1, b2 = f.sb("b1", [P, EXPERTS * MC]), f.sb("b2", [P, EXPERTS, D])
        xn, o, y = f.pair("xn", [P, 2, D]), f.pair("o", [P, 2, D]), f.sb("y", [P, 2, D])
        xT = f.pair("xT", [P, 2, 2, P])
        hT = f.pair("hT", [P, MC, 2 * P])
        xT_ps = f.ps("xT_ps", [P, 2, 2, P])
        h_ps = [f.ps(f"h_ps{b}", [P, MC, 2 * P]) for b in range(2)]
        y_ps = [f.ps(f"y_ps{b}", [P, 2, D]) for b in range(2)]
        weights, loaded, o_loaded, stored = f.dma_sem("weights"), f.dma_pair("loaded"), f.dma_pair("o_loaded"), f.store_pair("stored")
        turned, copied = f.sem("turned"), f.sem("copied")
        BANKS = MC // 2
        hidden, activated = f.sem("hidden", EXPERTS * BANKS), f.sem("activated", EXPERTS * BANKS)
        contracted, added = f.sem("contracted", EXPERTS), f.sem("added", EXPERTS)
        f.start()
        with nc.Block() as block:
            @block.sync
            def _(sp):
                for x in range(EXPERTS):
                    sp.dma_start(w1[:, x, :, :], k.W1[x, :, :].rearrange("(c p) n -> p c n", p=P)).then_inc(weights, 16)
                    sp.dma_start(w2[:, x, :, :], k.W2[x, :, :].rearrange("(c p) n -> p c n", p=P)).then_inc(weights, 16)
                with nc.allow_non_contiguous_dma(reason="2048 words"):
                    sp.dma_start(b1[:], k.mb1.rearrange("x (c p) -> p (x c)", p=P)).then_inc(weights, 16)
                sp.dma_start(b2[:].rearrange("p x n -> p (x n)"), k.mb2.rearrange("(a x) n -> a (x n)", a=1).to_broadcast([P, EXPERTS * D])).then_inc(weights, 16)

                def body(st):
                    if st.real(2):
                        n, r = st.n(2), st.slot(2)
                        sp.wait_ge(turned, f.at(turned, n, back=2))
                        sp.dma_start(xn[r][:], pair_of(k.XN, n)).then_inc(loaded[r], 16)
                    if st.real(1):
                        n, r = st.n(1), st.slot(1)
                        sp.wait_ge(stored[r], st.turn(1) * 16 + 16)
                        sp.dma_start(o[r][:], pair_of(k.X2, n)).then_inc(o_loaded[r], 16)
                    if st.real():
                        n, r = st.n(), st.slot()
                        sp.wait_ge(added, f.at(added, n))
                        sp.dma_start(pair_of(k.XO, n), o[r][:]).then_inc(stored[r], 16)
                steps(sp, PAIRS, 2, 2, 0, body)
                for r in range(2):
                    sp.wait_ge(stored[r], 16 * (PAIRS // 2) + 16)

            @block.vector
            def _(dve):
                V = nc.vector
                dve.wait_ge(weights, 16 * 10)

                def body(st):
                    n, r = st.n(), st.slot()
                    dve.wait_ge(o_loaded[r], st.turn() * 16 + 16)
                    for x in range(EXPERTS):
                        dve.wait_ge(contracted, f.at(contracted, n, x))
                        V.tensor_tensor(y[:], y_ps[x % 2][:], b2[:, x, :].unsqueeze(1).to_broadcast([P, 2, D]), ALU.add)
                        dve.drain()
                        for g in range(2):
                            V.scalar_tensor_tensor(out=o[r][:, g, :], in0=y[:, g, :], scalar=k.gates[:, ds((n * 2 + g) * EXPERTS + x, 1)],
                                                   in1=o[r][:, g, :], op0=ALU.mult, op1=ALU.add)
                        dve.drain().then_inc(added, 1)
                steps(dve, PAIRS, 2, 0, 0, body)

            @block.tensor
            def _(pe):
                T = nc.tensor
                pe.wait_ge(weights, 16 * 10)

                def turn(n, r, turns):
                    pe.wait_ge(loaded[r], turns * 16 + 16)
                    pe.wait_ge(copied, f.at(copied, n, back=1))
                    for g in range(2):
                        for half in range(2):
                            op = T.transpose(xT_ps[:, half, g, :], xn[r][:, g, half * P:(half + 1) * P], k.ident[:])
                    op.then_inc(turned, 1)

                def up(n, r, x):
                    for c in range(MC):
                        b = x * BANKS + c // 2
                        if c % 2 == 0:
                            pe.wait_ge(activated, f.at(activated, n, b - 2 * BANKS) if x >= 2 else f.at(activated, n, b + 2 * BANKS, back=1))
                        for half in range(2):
                            op = T.matmul(h_ps[x % 2][:, c, :], w1[:, x, half, c * P:(c + 1) * P],
                                          xT[r][:, half, :, :].rearrange("p g n -> p (g n)"), start=(half == 0), stop=(half == 1))
                        if c % 2:
                            op.then_inc(hidden, 1)

                def down(n, x):
                    pe.wait_ge(added, f.at(added, n, x - 2) if x >= 2 else f.at(added, n, x + 2, back=1))
                    for g in range(2):
                        for c in range(MC):
                            if g == 0 and c % 2 == 0:
                                pe.wait_ge(activated, f.at(activated, n, x * BANKS + c // 2))
                            op = T.matmul(y_ps[x % 2][:, g, :], hT[x % 2][:, c, g * P:(g + 1) * P], w2[:, x, c, :],
                                          start=(c == 0), stop=(c == MC - 1))
                    op.then_inc(contracted, 1)

                def body(st):
                    n, r = st.n(), st.slot()
                    if st.real():
                        pe.wait_ge(copied, f.at(copied, n))
                        up(n, r, 0)
                        for x in range(1, EXPERTS):
                            up(n, r, x)
                            if x < EXPERTS - 1:
                                down(n, x - 1)
                    if st.real(1):
                        turn(st.n(1), st.slot(1), st.turn(1))
                    if st.real():
                        down(n, EXPERTS - 2)
                        down(n, EXPERTS - 1)
                steps(pe, PAIRS, 2, 1, 0, body)

            @block.scalar
            def _(act):
                A = nc.scalar
                act.wait_ge(weights, 16 * 10)

                def body(st):
                    if st.real():
                        n = st.n()
                        for x in range(EXPERTS):
                            act.wait_ge(contracted, f.at(contracted, n, x - 2) if x >= 2 else f.at(contracted, n, x + 2, back=1))
                            for c in range(MC):
                                b = x * MC + c
                                if c % 2 == 0:
                                    act.wait_ge(hidden, f.at(hidden, n, b // 2))
                                A.activation(hT[x % 2][:, c, :], h_ps[x % 2][:, c, :], ACT.Gelu, bias=b1[:, b:b + 1])
                                if c % 2:
                                    act.drain().then_inc(activated, 1)
                    if st.real(1):
                        n, r = st.n(1), st.slot(1)
                        act.wait_ge(turned, f.at(turned, n))
                        act.wait_ge(hidden, f.at(hidden, n, back=2))
                        A.copy(xT[r][:].rearrange("p a g n -> p (a g n)"), xT_ps[:].rearrange("p a g n -> p (a g n)")).then_inc(copied, 1)
                steps(act, PAIRS, 2, 1, 0, body)


def program(nc, A):
    k = Space()
    k.x, k.src, k.dst, k.edge_type, k.node_type = (A["x"], A["src"], A["dst"], A["edge_type"], A["node_type"])
    k.W_Q, k.W_K, k.W_V, k.W_E, k.mu = (A["W_Q"], A["W_K"], A["W_V"], A["W_E"], A["mu"])
    k.Wo, k.bo, k.ln1_g, k.ln1_b, k.ln2_g = (A["Wo"], A["bo"], A["ln1_g"], A["ln1_b"], A["ln2_g"])
    k.ln2_b, k.w1, k.b1, k.w2, k.b2 = (A["ln2_b"], A["w1"], A["b1"], A["w2"], A["b2"])
    k.out_g, k.out_b, k.W_gat, k.att_src, k.att_dst = (A["out_g"], A["out_b"], A["W_gat"], A["att_src"], A["att_dst"])
    k.b_gat, k.ln_gamma, k.ln_beta, k.W1, k.mb1 = (A["b_gat"], A["ln_gamma"], A["ln_beta"], A["W1"], A["mb1"])
    k.W2, k.mb2, k.edge_src, k.edge_dst, k.out = (A["W2"], A["mb2"], A["edge_src"], A["edge_dst"], A["out"])
    with ExitStack() as ctx:
        k.sb = lambda name, shape, dt=F32: ctx.enter_context(nc.sbuf_tensor(name, shape, dt))

        def dram(name, shape, dt=F32):
            return nc.dram_tensor(name, shape, dt).ap()

        k.XP, k.X, k.X2, k.XN, k.XO = (dram(n, [NPAD, D]) for n in ("x_padded", "x_layer", "x_residual", "x_routed", "x_out"))
        k.KT, k.HT = dram("kv_table", [NPAD * EDGE_TYPES, KV]), dram("h_table", [NPAD, GW + GH])
        constants(nc, k)

        def edge_tables(name, e):
            T = Space()
            T.edges, T.owner = dram(name + "_edges", [e.tiles * P, 4]), dram(name + "_owner", [1, e.chunks * P], I32)
            T.rows = dram(name + "_rows", [e.tiles, P], BF16)
            T.pos, T.load = dram(name + "_pos", [P, e.padded], I32), dram(name + "_load", [P, e.padded, 4])
            return T

        def on_chip(T, name, e, gnn, scope):
            def sb(n, shape, dt=F32):
                return scope.enter_context(nc.sbuf_tensor(f"{name}_{n}", shape, dt))
            T.idx_v, T.rel = sb("idx_v", [P, e.tiles + 2 * G], I32), sb("rel", [P, e.tiles])
            if gnn:
                T.resets = dram(name + "_resets", [e.tiles, HEADS, P])
                T.idx_k, T.last = sb("idx_k", [P, e.tiles + 2 * G], I32), sb("last", [P, e.tiles])

        T, TG = edge_tables("gnn", GNN), edge_tables("gat", GAT)
        rank_edges(nc, k, "gnn_rank", GNN, k.src, k.dst, k.edge_type, T)
        rank_edges(nc, k, "gat_rank", GAT, k.edge_src, k.edge_dst, None, TG, other=(GNN, T))
        with ExitStack() as scope:
            on_chip(T, "gnn", GNN, True, scope)
            spread_edges(nc, k, "gnn_spread", GNN, T, True)

            def sb(n, shape, dt=F32):
                return scope.enter_context(nc.sbuf_tensor(n, shape, dt))
            k.type_mask = sb("type_mask", [P, NODE_TILES * NODE_TYPES])
            k.q_all, k.a_all = sb("q_all", [P, NODE_TILES * D]), sb("a_all", [P, NODE_TILES * AW])
            k.m_all = sb("m_all", [P, NODE_TILES * HEADS])
            node_types(nc, k)
            first_norm(nc, k)
            with nc.Fori(0, LAYERS, 1) as l:
                project(nc, k, l, TG)
                attend(nc, k, T)
                finish_layer(nc, k, l, TG)
        with ExitStack() as scope:
            def sb(n, shape, dt=F32):
                return scope.enter_context(nc.sbuf_tensor(n, shape, dt))
            k.gates = sb("gates", [P, NODE_TILES * EXPERTS])
            with ExitStack() as inner:
                on_chip(TG, "gat", GAT, False, inner)
                spread_edges(nc, k, "gat_spread", GAT, TG, False)

                def sbi(n, shape, dt=F32):
                    return inner.enter_context(nc.sbuf_tensor(n, shape, dt))
                k.h_all, k.gs_all = (sbi(n, [P, NODE_TILES * (GW + GH)]) for n in ("h_all", "gs_all"))
                k.dst_term, k.gm_all = (sbi(n, [P, NODE_TILES * GH]) for n in ("dst_term", "gm_all"))
                k.t2_all = sbi("t2_all", [P, NODE_TILES * 2 * GH])
                k.g_all = sbi("g_all", [P, GAT.tiles * (GW + GH)])
                route_inputs(nc, k)
                route_maxima(nc, k, TG)
                route_sums(nc, k, TG)
                route_gates(nc, k)
            experts(nc, k)
            cut_output(nc, k)


def node_types(nc, k):
    with Phase(nc, "types") as f:
        types_i, types = f.sb("types_i", [P, NODE_TILES], I32), f.sb("types", [P, NODE_TILES])
        zeroed, loaded = f.dma_sem("zeroed"), f.dma_sem("loaded")
        f.start()
        with nc.Block() as block:
            @block.sync
            def _(sp):
                sp.wait_ge(zeroed, 1)
                with nc.allow_non_contiguous_dma(reason="6250 words"):
                    sp.dma_start(types_i[:, 0:BUCKETS - 1], k.node_type[0:(BUCKETS - 1) * P].rearrange("(i p) -> p i", p=P)).then_inc(loaded, 16)
                    sp.dma_start(types_i[0:LAST, BUCKETS - 1:BUCKETS], k.node_type[(BUCKETS - 1) * P:N].rearrange("(p i) -> p i", i=1)).then_inc(loaded, 16)

            @block.vector
            def _(dve):
                nc.vector.memset(types_i[:], 0)
                dve.drain().then_inc(zeroed, 1)
                dve.wait_ge(loaded, 32)
                nc.vector.tensor_copy(types[:], types_i[:])
                dve.drain()
                for t in range(NODE_TYPES):
                    nc.vector.tensor_single_scalar(k.type_mask[:].rearrange("p (i t) -> p i t", t=NODE_TYPES)[:, :, t], types[:], float(t), op=ALU.is_equal)


def cut_output(nc, k):
    with Phase(nc, "cut") as f:
        written = f.dma_sem("written")
        f.start()
        with nc.Block() as block:
            @block.sync
            def _(sp):
                sp.dma_start(k.out, k.XO[0:N, :]).then_inc(written, 16)
                sp.wait_ge(written, 16)


_INS = {"x": "x", "src": "src", "dst": "dst", "edge_type_3": "edge_type", "node_type_4": "node_type",
        "L0_gnn_W_Q": "W_Q", "L0_gnn_W_K": "W_K", "L0_gnn_W_V": "W_V", "L0_gnn_W_E": "W_E", "L0_gnn_mu": "mu",
        "L0_gnn_Wo": "Wo", "L0_gnn_bo": "bo", "L0_gnn_ln1_g": "ln1_g", "L0_gnn_ln1_b": "ln1_b",
        "L0_gnn_ln2_g": "ln2_g", "L0_gnn_ln2_b": "ln2_b", "L0_gnn_w1": "w1", "L0_gnn_b1": "b1",
        "L0_gnn_w2": "w2", "L0_gnn_b2": "b2", "L0_gnn_out_g": "out_g", "L0_gnn_out_b": "out_b",
        "L0_ffn_W_gat": "W_gat", "L0_ffn_att_src": "att_src", "L0_ffn_att_dst": "att_dst", "L0_ffn_b_gat": "b_gat",
        "L0_ffn_ln_gamma": "ln_gamma", "L0_ffn_ln_beta": "ln_beta", "L0_ffn_W1": "W1", "L0_ffn_b1": "mb1",
        "L0_ffn_W2": "W2", "L0_ffn_b2": "mb2"}


def kernel(**inputs):
    import numpy as _np
    import concourse.bacc as _bacc
    from concourse.bass_utils import run_bass_kernel_spmd as _run

    nc = _bacc.Bacc("TRN2", target_bir_lowering=False, num_devices=1)
    arrays, aps = {}, {}

    def put(name, a):
        arrays[f"in_{name}"] = _np.ascontiguousarray(a)
        aps[name] = nc.dram_tensor(f"in_{name}", list(a.shape), mybir.dt.from_np(a.dtype), kind="ExternalInput").ap()

    for name, short in _INS.items():
        put(short, _np.asarray(inputs[name]))
    edges = _np.asarray(inputs["L0_ffn_edge_index"])
    put("edge_src", edges[0])
    put("edge_dst", edges[1])
    aps["out"] = nc.dram_tensor("out_x", [N, D], F32, kind="ExternalOutput").ap()
    program(nc, aps)
    r = _run(nc, [arrays], core_ids=[0])
    return r.results[0]["out_x"]
```
